# Optimizing a Trainium2 kernel written in Bass

```python
import numpy as np
import jax
import jax.numpy as jnp

def _softmax(x, axis=-1):
    return jax.nn.softmax(x, axis=axis)

def _gelu(x):
    return jax.nn.gelu(x, approximate=True)

def _silu(x):
    return jax.nn.silu(x)

def _sigmoid(x):
    return jax.nn.sigmoid(x)

def _layernorm(x, axis=-1, eps=1e-05):
    m = jnp.mean(x, axis=axis, keepdims=True)
    v = jnp.var(x, axis=axis, keepdims=True)
    return (x - m) / jnp.sqrt(v + eps)

def _scatter_add(tgt, idx, src, axis=0):
    return tgt.at[idx].add(src)

def _segment_sum(src, seg, n):
    return jax.ops.segment_sum(src, seg, n)
kernel_name = 'mk_decoder_postln_d1_seqx_r4_8a495b'

def setup_inputs(seed: int=0):
    np.random.seed(seed)
    _w = jnp.asarray

    def _rec_inputs():
        import jax
        import jax.numpy as jnp
        _rk = jax.random.key(seed)
        x = 7.22e-05 + 1 * jax.random.normal(jax.random.fold_in(_rk, 1), (4, 512, 256), jnp.float32)
        _lenS = 512 - jax.random.randint(jax.random.fold_in(_rk, 7), (4,), 0, max(1, 512 // 4) + 1, jnp.int32)
        _lenS2 = 1601 - jax.random.randint(jax.random.fold_in(_rk, 8), (4,), 0, max(1, 1601 // 4) + 1, jnp.int32)
        _ctx_1024P = jax.random.normal(jax.random.fold_in(_rk, 11), (4, 16, 256), jnp.float32)
        _ctx_1024c = jax.random.dirichlet(jax.random.fold_in(_rk, 511), 0.3 * jnp.ones((16,), jnp.float32), (4, 1601))
        _ctx_1024t = jnp.einsum('bsk,bkd->bsd', _ctx_1024c, _ctx_1024P)
        _ctx_1024t = _ctx_1024t * jax.lax.rsqrt(jnp.mean(jnp.square(_ctx_1024t)) + 1e-12) * 0.953939
        ctx_1024 = 4.13588e-05 + 0.999923 * (_ctx_1024t + 0.3 * jax.random.normal(jax.random.fold_in(_rk, 611), (4, 1601, 256), jnp.float32))
        return (x, ctx_1024)
    x, ctx_1024 = _rec_inputs()

    def _L0_attn_setup():
        import jax, jax.numpy as jnp
        import numpy as np
        E = 256
        H = 16
        D = E // H
        K = 15
        PAD_L = K // 2
        T, B = (512, 4)

        def dynamic_conv_tbc(x, dyn_w, dyn_b):
            t, b, c = x.shape
            r = c // H
            w = jax.nn.softmax((x @ dyn_w.T + dyn_b).reshape(t, b, H, K), axis=-1)
            xpad = jnp.pad(x, ((PAD_L, K - 1 - PAD_L), (0, 0), (0, 0)))
            xh = xpad.reshape(t + K - 1, b, H, r)
            out = jnp.zeros((t, b, H, r), x.dtype)
            for k in range(K):
                out = out + w[..., k:k + 1] * xh[k:k + t]
            return out.reshape(t, b, c)
        key = jax.random.key(seed)
        ks = jax.random.split(key, 6)
        s = 0.02
        return {'x': jax.random.normal(ks[0], (T, B, E), dtype=jnp.float32), 'in_proj_w': jax.random.normal(ks[1], (3 * E, E), dtype=jnp.float32) * s, 'in_proj_b': jnp.zeros((3 * E,), jnp.float32), 'out_proj_w': jax.random.normal(ks[2], (E, 2 * E), dtype=jnp.float32) * s, 'out_proj_b': jnp.zeros((E,), jnp.float32), 'dyn_w': jax.random.normal(ks[3], (H * K, E), dtype=jnp.float32) * s, 'dyn_b': jnp.zeros((H * K,), jnp.float32)}
    _L0_attn_all = _L0_attn_setup()
    _L0_attn_in = {k: v for k, v in _L0_attn_all.items() if k in ('in_proj_w', 'in_proj_b', 'out_proj_w', 'out_proj_b', 'dyn_w', 'dyn_b')}
    del _L0_attn_all

    def _L0_xattn_setup():
        import jax, jax.numpy as jnp
        import numpy as np
        HEADS = 16
        DIM_HEAD = 64
        DIM = 256
        CTX_DIM = 256
        INNER = HEADS * DIM_HEAD
        key = jax.random.key(seed)
        ks = jax.random.split(key, 6)
        b, n, m = (4, 512, 512)
        x = jax.random.normal(ks[0], (b, n, DIM), dtype=jnp.float32)
        context = jax.random.normal(ks[1], (b, m, CTX_DIM), dtype=jnp.float32)
        s = 0.02
        w_q = jax.random.normal(ks[2], (DIM, INNER), dtype=jnp.float32) * s
        w_kv = jax.random.normal(ks[3], (CTX_DIM, 2 * INNER), dtype=jnp.float32) * s
        w_out = jax.random.normal(ks[4], (INNER, DIM), dtype=jnp.float32) * s
        b_out = jnp.zeros((DIM,), dtype=jnp.float32)
        return {'x': x, 'context': context, 'w_q': w_q, 'w_kv': w_kv, 'w_out': w_out, 'b_out': b_out}
    _L0_xattn_all = _L0_xattn_setup()
    _L0_xattn_in = {k: v for k, v in _L0_xattn_all.items() if k in ('w_q', 'w_kv', 'w_out', 'b_out')}
    del _L0_xattn_all

    def _L0_ffn_setup():
        import jax, jax.numpy as jnp
        import numpy as np
        E = 8
        D = 256
        H = 512
        TOP_K = 2
        key = jax.random.key(seed)
        k_x, k_g, k_w1, k_w2 = jax.random.split(key, 4)
        B, S = (4, 512)
        inp = {'input': jax.random.normal(k_x, (B, S, D), dtype=jnp.float32), 'Wg': jax.random.normal(k_g, (D, E), dtype=jnp.float32) * 0.02, 'W1': jax.random.normal(k_w1, (E, D, H), dtype=jnp.float32) * 0.02, 'b1': jnp.zeros((E, H), dtype=jnp.float32), 'W2': jax.random.normal(k_w2, (E, H, D), dtype=jnp.float32) * 0.02, 'b2': jnp.zeros((E, D), dtype=jnp.float32)}
        return inp
    _L0_ffn_all = _L0_ffn_setup()
    _L0_ffn_in = {k: v for k, v in _L0_ffn_all.items() if k in ('Wg', 'W1', 'b1', 'W2', 'b2')}
    del _L0_ffn_all
    return {'x': x, 'ctx_1024': ctx_1024, 'L0_attn_in_proj_w': _L0_attn_in['in_proj_w'], 'L0_attn_in_proj_b': _L0_attn_in['in_proj_b'], 'L0_attn_out_proj_w': _L0_attn_in['out_proj_w'], 'L0_attn_out_proj_b': _L0_attn_in['out_proj_b'], 'L0_attn_dyn_w': _L0_attn_in['dyn_w'], 'L0_attn_dyn_b': _L0_attn_in['dyn_b'], 'L0_xattn_w_q': _L0_xattn_in['w_q'], 'L0_xattn_w_kv': _L0_xattn_in['w_kv'], 'L0_xattn_w_out': _L0_xattn_in['w_out'], 'L0_xattn_b_out': _L0_xattn_in['b_out'], 'L0_ffn_Wg': _L0_ffn_in['Wg'], 'L0_ffn_W1': _L0_ffn_in['W1'], 'L0_ffn_b1': _L0_ffn_in['b1'], 'L0_ffn_W2': _L0_ffn_in['W2'], 'L0_ffn_b2': _L0_ffn_in['b2']}

def reference(x, ctx_1024, L0_attn_in_proj_w, L0_attn_in_proj_b, L0_attn_out_proj_w, L0_attn_out_proj_b, L0_attn_dyn_w, L0_attn_dyn_b, L0_xattn_w_q, L0_xattn_w_kv, L0_xattn_w_out, L0_xattn_b_out, L0_ffn_Wg, L0_ffn_W1, L0_ffn_b1, L0_ffn_W2, L0_ffn_b2):
    import jax
    import jax.numpy as jnp

    def _L0_attn_ref(x, in_proj_w, in_proj_b, out_proj_w, out_proj_b, dyn_w, dyn_b):
        import jax, jax.numpy as jnp
        import numpy as np
        E = 256
        H = 16
        D = E // H
        K = 15
        PAD_L = K // 2
        T, B = (512, 4)

        def dynamic_conv_tbc(x, dyn_w, dyn_b):
            t, b, c = x.shape
            r = c // H
            w = jax.nn.softmax((x @ dyn_w.T + dyn_b).reshape(t, b, H, K), axis=-1)
            xpad = jnp.pad(x, ((PAD_L, K - 1 - PAD_L), (0, 0), (0, 0)))
            xh = xpad.reshape(t + K - 1, b, H, r)
            out = jnp.zeros((t, b, H, r), x.dtype)
            for k in range(K):
                out = out + w[..., k:k + 1] * xh[k:k + t]
            return out.reshape(t, b, c)
        t, b, _ = x.shape
        qkv = x @ in_proj_w.T + in_proj_b
        q, k, v = jnp.split(qkv, 3, axis=-1)
        q = q * D ** (-0.5)

        def heads(z):
            return z.reshape(t, b * H, D).transpose(1, 0, 2)
        qh, kh, vh = (heads(q), heads(k), heads(v))
        scores = jnp.einsum('ntd,nsd->nts', qh, kh)
        attn = jax.nn.softmax(scores, axis=-1)
        o = jnp.einsum('nts,nsd->ntd', attn, vh)
        attn_out = o.transpose(1, 0, 2).reshape(t, b, E)
        conv_out = dynamic_conv_tbc(v, dyn_w, dyn_b)
        cat = jnp.concatenate([attn_out, conv_out], axis=-1)
        return cat @ out_proj_w.T + out_proj_b

    def _L0_xattn_ref(x, context, w_q, w_kv, w_out, b_out):
        import jax, jax.numpy as jnp
        import numpy as np
        HEADS = 16
        DIM_HEAD = 64
        DIM = 256
        CTX_DIM = 256
        INNER = HEADS * DIM_HEAD
        b, n, _ = x.shape
        m = context.shape[1]
        scale = DIM_HEAD ** (-0.5)
        q = (x @ w_q).reshape(b, n, HEADS, DIM_HEAD)
        kv = (context @ w_kv).reshape(b, m, 2, HEADS, DIM_HEAD)
        k, v = (kv[:, :, 0], kv[:, :, 1])
        attn = jnp.einsum('bnhd,bmhd->bhnm', q, k) * scale
        attn = jax.nn.softmax(attn, axis=-1)
        out = jnp.einsum('bhnm,bmhd->bnhd', attn, v).reshape(b, n, INNER)
        return out @ w_out + b_out

    def _L0_ffn_ref(input, Wg, W1, b1, W2, b2):
        import jax, jax.numpy as jnp
        import numpy as np
        E = 8
        D = 256
        H = 512
        TOP_K = 2
        logits = jnp.einsum('bsd,de->bse', input, Wg)
        probs = jax.nn.softmax(logits, axis=-1)
        top_vals, top_idx = jax.lax.top_k(probs, TOP_K)
        top_vals = top_vals / jnp.sum(top_vals, axis=-1, keepdims=True)
        onehot = jax.nn.one_hot(top_idx, E, dtype=input.dtype)
        mask = jnp.sum(onehot, axis=2)
        scores = jnp.sum(onehot * top_vals[..., None], axis=2)
        xm = input[None] * jnp.moveaxis(mask, -1, 0)[..., None]
        h = jnp.einsum('ebsd,edh->ebsh', xm, W1) + b1[:, None, None, :]
        h = jax.nn.relu(h)
        y = jnp.einsum('ebsh,ehd->ebsd', h, W2) + b2[:, None, None, :]
        out = jnp.sum(y * jnp.moveaxis(scores, -1, 0)[..., None], axis=0)
        return out
    x = _layernorm(x + _L0_attn_ref(x, L0_attn_in_proj_w, L0_attn_in_proj_b, L0_attn_out_proj_w, L0_attn_out_proj_b, L0_attn_dyn_w, L0_attn_dyn_b), axis=-1)
    x = _layernorm(x + _L0_xattn_ref(x, ctx_1024, L0_xattn_w_q, L0_xattn_w_kv, L0_xattn_w_out, L0_xattn_b_out), axis=-1)
    x = _layernorm(x + _L0_ffn_ref(x, L0_ffn_Wg, L0_ffn_W1, L0_ffn_b1, L0_ffn_W2, L0_ffn_b2), axis=-1)
    return x

_drawn_inputs = setup_inputs


def setup_inputs(seed=0):
    import zlib

    import numpy as np

    out = dict(_drawn_inputs(seed))
    spreads = {'L0_attn_in_proj_b': (0.0, 0.1),
     'L0_attn_out_proj_b': (0.0, 0.1),
     'L0_attn_dyn_b': (0.0, 2.0),
     'L0_xattn_b_out': (0.0, 0.1),
     'L0_ffn_b1': (0.0, 0.365),
     'L0_ffn_b2': (0.0, 0.1)}
    factors = {'L0_attn_dyn_w': 22.087, 'L0_xattn_w_q': 8.0}
    for name, (base, spread) in spreads.items():
        noise = np.random.default_rng([zlib.crc32(name.encode()), seed]).standard_normal(out[name].shape)
        drawn = base * np.exp(spread * noise) if base else spread * noise
        out[name] = jnp.asarray(drawn.astype(out[name].dtype))
    for name, factor in factors.items():
        out[name] = (out[name] * factor).astype(out[name].dtype)
    return out
```

```python
from contextlib import ExitStack

import concourse.bass as bass
from concourse import mybir

P = 128
F32 = mybir.dt.float32
F32R = mybir.dt.float32r
U32 = mybir.dt.uint32
ALU = mybir.AluOpType
ACT = mybir.ActivationFunctionType
AX = mybir.AxisListType

B, N, E = 4, 512, 256
EC = E // P
NC = N // P
M = 1601
SH_, SD = 16, 16
TAPS, PAD_L = 15, 7
XH, XD = 16, 64
PAIRS = XH // 2
QUADS = XH // 4
MT = (M + P - 1) // P
M_LAST = M - (MT - 1) * P
CW = 402
KC0 = [0, CW, 2 * CW, M - CW]
NE, HID, TOPK = 8, 512, 2
HC = HID // P
QKV = 3 * E
DYN = SH_ * TAPS
ALLW = QKV + DYN
HALF = ALLW // 2
EPS = 1e-5


def sems(ctx, nc, names):
    return {n: ctx.enter_context(nc.semaphore(n)) for n in names.split()}


def need(eng, sem, value):
    if not isinstance(value, int) or value > 0:
        eng.wait_ge(sem, value)


def self_attention(nc, a, X, consts, x1_hi, x1_lo):
    ident, ones, neghalf = consts["ident"], consts["ones"], consts["neghalf"]
    with ExitStack() as ctx:
        def sb(name, shape, dt=F32):
            return ctx.enter_context(nc.sbuf_tensor("sa_" + name, shape, dt))

        w_raw = sb("w_raw", [P, EC, ALLW])
        w_hi = sb("w_hi", [P, EC, ALLW], F32R)
        w_lo = sb("w_lo", [P, EC, ALLW], F32R)
        wv_nat = sb("wv_nat", [P, EC, E])
        dynT = sb("dynT", [P, EC, DYN])
        bv_col = sb("bv_col", [P, EC])
        bv_wide = sb("bv_wide", [P, EC, P])
        bias = sb("bias", [P, ALLW])
        wo_raw = sb("wo_raw", [P, 2 * EC, E])
        wo_hi = sb("wo_hi", [P, 2 * EC, E], F32R)
        wo_lo = sb("wo_lo", [P, 2 * EC, E], F32R)
        bo = sb("bo", [P, E])
        xb = sb("xb", [P, E])
        xT = sb("xT", [P, 2, EC, B, P])
        xT_hi = sb("xT_hi", [P, 2, EC, B, P], F32R)
        xT_lo = sb("xT_lo", [P, 2, EC, B, P], F32R)
        qkv = sb("qkv", [P, 2, B, ALLW])
        prod = sb("prod", [P, B, B * E])
        sc = sb("sc", [P, B, B, SH_])
        mx = sb("mx", [P, B, SH_])
        den = sb("den", [P, B, SH_])
        tap = sb("tap", [P, B, SH_, TAPS])
        tmx = sb("tmx", [P, B, SH_])
        tden = sb("tden", [P, B, SH_])
        cprod = sb("cprod", [P, B, E])
        csum = sb("csum", [P, 2, E])
        cat = sb("cat", [P, B, 2 * E])
        cat_hi = sb("cat_hi", [P, 2, 2 * E], F32R)
        cat_lo = sb("cat_lo", [P, 2, 2 * E], F32R)
        y = sb("y", [P, B, E])
        st = sb("st", [P, B, 6])
        mv = sb("mv", [P, B, 2])
        rstd = sb("rstd", [P, B])
        x1s_hi = sb("x1s_hi", [P, 2, EC, P], F32R)
        x1s_lo = sb("x1s_lo", [P, 2, EC, P], F32R)
        xbo = sb("xbo", [P, E])

        ps_qkv = ctx.enter_context(nc.psum_tensor("ps_qkv", [P, 2, 2, 512], F32))
        ps_cat = ctx.enter_context(nc.psum_tensor("ps_cat", [P, 2, 512], F32))
        ps_out = ctx.enter_context(nc.psum_tensor("ps_out", [P, 512], F32))
        ps_x1 = ctx.enter_context(nc.psum_tensor("ps_x1", [P, 512], F32))

        s = sems(ctx, nc, "w_in x_in0 x_in1 const_ready fold_mm fold_evac w_hi_done w_lo_done x_hi_done x_lo_done "
                          "qkv_mm qkv_ready score_sub score_exp tap_max tap_sub tap_exp tap_inv tap_w conv_step "
                          "conv_done attn_done cat_tr cat_hi_done cat_lo_done out_mm var_ready rstd_half rstd_done "
                          "x1_done y_ready x1_tr x1_hi_done x1_lo_done x1_out0 x1_out1 step pstep")
        x_in = [s["x_in0"], s["x_in1"]]
        x1_out = [s["x1_out0"], s["x1_out1"]]
        block = ctx.enter_context(nc.Block())
        NW = 11

        @block.sync
        def _(sp):
            sp.dma_start(w_raw[:, :, 0:QKV], a["w_inT"].rearrange("(k p) n -> p k n", p=P)).then_inc(s["w_in"], 16)
            sp.dma_start(wv_nat[:], a["w_v"].rearrange("(k p) n -> p k n", p=P)).then_inc(s["w_in"], 16)
            sp.dma_start(dynT[:], a["dynT"].rearrange("(k p) n -> p k n", p=P)).then_inc(s["w_in"], 16)
            sp.dma_start(bv_col[:], a["b_v"]).then_inc(s["w_in"], 16)
            sp.dma_start(bias[:, 0:QKV], a["b_in"].broadcast_to([P, QKV])).then_inc(s["w_in"], 16)
            sp.dma_start(bias[:, QKV:ALLW], a["b_dyn"].broadcast_to([P, DYN])).then_inc(s["w_in"], 16)
            sp.dma_start(wo_raw[:], a["w_oT"].rearrange("(k p) n -> p k n", p=P)).then_inc(s["w_in"], 16)
            sp.dma_start(bo[:], a["b_o"].broadcast_to([P, E])).then_inc(s["w_in"], 16)
            sp.dma_start(xbo[:], a["b_xo"].broadcast_to([P, E])).then_inc(s["w_in"], 16)
            for c in range(NC):
                for k in range(EC):
                    if c >= 2 and k == 0:
                        sp.wait_ge(s["x_lo_done"], c - 1)
                    src = a["xT"].rearrange("(k p) (t c n) -> p k t c n", p=P, t=B, c=NC)[:, k, :, c, :]
                    sp.dma_start(xT[:, c % 2, k], src).then_inc(x_in[c % 2], 16)
                if c == 0:
                    sp.dma_start(X[:], a["x"].rearrange("(t p) e -> p t e", p=P)).then_inc(s["w_in"], 16)
            for n in range(NC * B):
                c, t = n // B, n % B
                sp.wait_ge(s["x1_hi_done"], n + 1)
                sp.dma_start(x1_hi[t][:, :, c * P:(c + 1) * P], x1s_hi[:, n % 2].bitcast(F32)).then_inc(x1_out[n % 2], 16)
                sp.wait_ge(s["x1_lo_done"], n + 1)
                sp.dma_start(x1_lo[t][:, :, c * P:(c + 1) * P], x1s_lo[:, n % 2].bitcast(F32)).then_inc(x1_out[n % 2], 16)
            for q in x1_out:
                sp.wait_ge(q, 16 * NC * B)

        LOADS = 16 * 10

        @block.gpsimd
        def _(pool):
            pool.memset(ones[:], 1.0)
            pool.memset(neghalf[:], -0.5)
            pool.memset(ident[:], 0.0).then_inc(s["pstep"], 1)
            pool.wait_ge(s["pstep"], 1)
            nc.gpsimd.affine_select(out=ident[:], in_=ident[:], compare_op=ALU.not_equal, fill=1.0, base=0,
                                    pattern=[[-1, P]], channel_multiplier=1).then_inc(s["const_ready"], 1)
            nsteps = 1

            def split_x(c):
                pool.wait_ge(s["x_hi_done"], c + 1)
                nc.gpsimd.tensor_tensor(xT_lo[:, c % 2], xT[:, c % 2], xT_hi[:, c % 2].bitcast(F32),
                                        ALU.subtract).then_inc(s["x_lo_done"], 1)

            split_x(0)
            split_x(1)
            for c in range(NC):
                u = c % 2
                logits = qkv[:, u, :, QKV:ALLW].rearrange("p t (h k) -> p t h k", k=TAPS)
                for t in range(B):
                    if t == 0:
                        pool.wait_ge(s["tap_max"], c + 1)
                    nc.gpsimd.tensor_tensor(tap[:, t], logits[:, t],
                                            tmx[:, t].unsqueeze(2).broadcast_to([P, SH_, TAPS]),
                                            ALU.subtract).then_inc(s["tap_sub"], 1)
                for t in range(B):
                    if t == 0:
                        pool.wait_ge(s["tap_inv"], c + 1)
                    ins = nc.gpsimd.tensor_tensor(tap[:, t], tap[:, t],
                                                  tden[:, t].unsqueeze(2).broadcast_to([P, SH_, TAPS]), ALU.mult)
                    ins.then_inc(s["tap_w"], 1)
                pool.wait_ge(s["tap_w"], B * (c + 1))
                if c >= 1:
                    pool.wait_ge(s["cat_tr"], B * c)
                for t in range(B):
                    w = tap[:, t, :, PAD_L - t:PAD_L - t + B].rearrange("p h i -> p i h")
                    for i in range(B):
                        ins = nc.gpsimd.tensor_tensor(
                            cprod[:, i].rearrange("p (h d) -> p h d", d=SD),
                            qkv[:, u, i, 2 * E:3 * E].rearrange("p (h d) -> p h d", d=SD),
                            w[:, i].unsqueeze(2).broadcast_to([P, SH_, SD]), ALU.mult)
                    ins.then_inc(s["conv_step"], 1)
                    k = 3 * (B * c + t)
                    pool.wait_ge(s["conv_step"], k + 1)
                    nc.gpsimd.tensor_tensor(csum[:], cprod[:, 0:2], cprod[:, 2:4], ALU.add).then_inc(s["conv_step"], 1)
                    pool.wait_ge(s["conv_step"], k + 2)
                    nc.gpsimd.tensor_tensor(cat[:, t, E:2 * E], csum[:, 0], csum[:, 1],
                                            ALU.add).then_inc(s["conv_step"], 1)
                    pool.wait_ge(s["conv_step"], k + 3)
                if c + 2 < NC:
                    pool.wait_ge(s["qkv_mm"], 2 * B * (c + 1))
                    split_x(c + 2)
                pool.wait_ge(s["var_ready"], c + 1)
                nc.gpsimd.tensor_scalar(rstd[:], mv[:, :, 1], EPS, None, ALU.add).then_inc(s["rstd_half"], 1)
                pool.wait_ge(s["rstd_half"], c + 1)
                nc.gpsimd.tensor_tensor(rstd[:], rstd[:], neghalf[:, 0:B], ALU.pow).then_inc(s["rstd_done"], 1)

        @block.tensor
        def _(pe):
            pe.wait_ge(s["w_in"], LOADS)
            for kc in range(EC):
                for ec in range(EC):
                    ins = nc.tensor.matmul(ps_qkv[:, 0, kc, 0:DYN], wv_nat[:, ec, kc * P:(kc + 1) * P], dynT[:, ec],
                                           start=ec == 0, stop=ec == EC - 1)
            ins.then_inc(s["fold_mm"], 1)
            pe.wait_ge(s["step"], 1)
            for ec in range(EC):
                ins = nc.tensor.matmul(ps_qkv[:, 1, 0, 0:DYN], bv_wide[:, ec], dynT[:, ec],
                                       start=ec == 0, stop=ec == EC - 1)
            ins.then_inc(s["fold_mm"], 1)

            def project(c):
                pe.wait_ge(s["x_lo_done"], c + 1)
                for t in range(B):
                    n = B * c + t
                    for h in range(2):
                        if n < 2:
                            pe.wait_ge(s["fold_evac"], 2)
                            pe.wait_ge(s["w_lo_done"], 1)
                        else:
                            pe.wait_ge(s["qkv_ready"], 2 * (n - 2) + h + 1)
                        for q, (xx, ww) in enumerate(((xT_hi, w_hi), (xT_lo, w_hi), (xT_hi, w_lo))):
                            for k in range(EC):
                                ins = nc.tensor.matmul(ps_qkv[:, n % 2, h, 0:HALF], xx[:, c % 2, k, t],
                                                       ww[:, k, h * HALF:(h + 1) * HALF],
                                                       start=q == 0 and k == 0, stop=q == 2 and k == EC - 1)
                        ins.then_inc(s["qkv_mm"], 1)

            def finish(c):
                for t in range(B):
                    n = B * c + t
                    if t == 0:
                        pe.wait_ge(s["attn_done"], c + 1)
                        pe.wait_ge(s["conv_step"], 3 * B * (c + 1))
                        if c == 0:
                            pe.wait_ge(s["const_ready"], 1)
                    if n >= 2:
                        pe.wait_ge(s["cat_lo_done"], n - 1)
                    for j in range(2 * EC):
                        ins = nc.tensor.transpose(ps_cat[:, n % 2, j * P:(j + 1) * P], cat[:, t, j * P:(j + 1) * P],
                                                  ident[:])
                    ins.then_inc(s["cat_tr"], 1)
                for t in range(B):
                    n = B * c + t
                    pe.wait_ge(s["cat_lo_done"], n + 1)
                    need(pe, s["y_ready"], n)
                    for q, (cc, ww) in enumerate(((cat_hi, wo_hi), (cat_lo, wo_hi), (cat_hi, wo_lo))):
                        for j in range(2 * EC):
                            ins = nc.tensor.matmul(ps_out[:, 0:E], cc[:, n % 2, j * P:(j + 1) * P], ww[:, j],
                                                   start=q == 0 and j == 0, stop=q == 2 and j == 2 * EC - 1)
                    ins.then_inc(s["out_mm"], 1)
                for t in range(B):
                    n = B * c + t
                    pe.wait_ge(s["x1_done"], n + 1)
                    need(pe, s["x1_lo_done"], n)
                    for k in range(EC):
                        ins = nc.tensor.transpose(ps_x1[:, k * P:(k + 1) * P], X[:, t * NC + c, k * P:(k + 1) * P],
                                                  ident[:])
                    ins.then_inc(s["x1_tr"], 1)

            project(0)
            for c in range(NC):
                if c + 1 < NC:
                    project(c + 1)
                finish(c)

        @block.scalar
        def _(act):
            def split_x(c):
                act.wait_ge(x_in[c % 2], 16 * EC * (c // 2 + 1))
                if c >= 2:
                    act.wait_ge(s["qkv_mm"], 2 * B * (c - 1))
                nc.scalar.copy(xT_hi[:, c % 2], xT[:, c % 2]).then_inc(s["x_hi_done"], 1)

            split_x(0)
            act.wait_ge(s["fold_evac"], 1)
            nc.scalar.copy(w_hi[:], w_raw[:]).then_inc(s["w_hi_done"], 1)
            nc.scalar.copy(wo_hi[:], wo_raw[:]).then_inc(s["w_hi_done"], 1)
            split_x(1)
            for c in range(NC):
                act.wait_ge(s["tap_sub"], B * (c + 1))
                nc.scalar.activation(tap[:], tap[:], ACT.Exp).then_inc(s["tap_exp"], 1)
                act.wait_ge(s["score_sub"], c + 1)
                nc.scalar.activation(sc[:], sc[:], ACT.Exp, scale=SD ** -0.5).then_inc(s["score_exp"], 1)
                if c + 2 < NC:
                    split_x(c + 2)
                for t in range(B):
                    n = B * c + t
                    act.wait_ge(s["cat_tr"], n + 1)
                    need(act, s["out_mm"], n - 1)
                    nc.scalar.copy(cat_hi[:, n % 2], ps_cat[:, n % 2]).then_inc(s["cat_hi_done"], 1)
                for t in range(B):
                    n = B * c + t
                    act.wait_ge(s["x1_tr"], n + 1)
                    if n >= 2:
                        act.wait_ge(x1_out[n % 2], 32 * (n // 2))
                    nc.scalar.copy(x1s_hi[:, n % 2], ps_x1[:, 0:E].rearrange("p (k n) -> p k n", k=EC))\
                        .then_inc(s["x1_hi_done"], 1)

        @block.vector
        def _(dve):
            done = [0]

            def link(ins):
                done[0] += 1
                ins.then_inc(s["step"], 1)
                dve.wait_ge(s["step"], done[0])

            dve.wait_ge(s["w_in"], LOADS)
            dve.wait_ge(s["const_ready"], 1)
            for ec in range(EC):
                ins = nc.vector.tensor_scalar(bv_wide[:, ec], ones[:], bv_col[:, ec:ec + 1], None, ALU.mult)
            link(ins)
            dve.wait_ge(s["fold_mm"], 1)
            nc.vector.tensor_copy(w_raw[:, :, QKV:ALLW], ps_qkv[:, 0, :, 0:DYN]).then_inc(s["fold_evac"], 1)
            dve.wait_ge(s["fold_mm"], 2)
            nc.vector.tensor_tensor(bias[:, QKV:ALLW], bias[:, QKV:ALLW], ps_qkv[:, 1, 0, 0:DYN],
                                    ALU.add).then_inc(s["fold_evac"], 1)
            dve.wait_ge(s["w_hi_done"], 1)
            nc.vector.tensor_tensor(w_lo[:], w_raw[:], w_hi[:].bitcast(F32), ALU.subtract).then_inc(s["w_lo_done"], 1)
            dve.wait_ge(s["w_hi_done"], 2)
            nc.vector.tensor_tensor(wo_lo[:], wo_raw[:], wo_hi[:].bitcast(F32), ALU.subtract)\
                .then_inc(s["w_lo_done"], 1)
            dve.wait_ge(s["fold_evac"], 2)

            def take_projection(c):
                u = c % 2
                for t in range(B):
                    n = B * c + t
                    for h in range(2):
                        dve.wait_ge(s["qkv_mm"], 2 * n + h + 1)
                        nc.vector.tensor_tensor(qkv[:, u, t, h * HALF:(h + 1) * HALF], ps_qkv[:, n % 2, h, 0:HALF],
                                                bias[:, h * HALF:(h + 1) * HALF], ALU.add)\
                            .then_inc(s["qkv_ready"], 1)
                dve.wait_ge(s["qkv_ready"], 2 * B * (c + 1))
                logits = qkv[:, u, :, QKV:ALLW].rearrange("p t (h k) -> p t h k", k=TAPS)
                nc.vector.tensor_reduce(tmx[:], logits, AX.X, ALU.max).then_inc(s["tap_max"], 1)

            def attend(c):
                u = c % 2
                q = qkv[:, u, :, 0:E]
                k = qkv[:, u, :, E:2 * E]
                v = qkv[:, u, :, 2 * E:3 * E]
                for t in range(B):
                    ins = nc.vector.tensor_tensor(prod[:, t].rearrange("p (i e) -> p i e", e=E), k,
                                                  q[:, t].unsqueeze(1).broadcast_to([P, B, E]), ALU.mult)
                link(ins)
                link(nc.vector.tensor_reduce(sc[:].rearrange("p t i h -> p (t i h)"),
                                             prod[:].rearrange("p t (g d) -> p (t g) d", d=SD), AX.X, ALU.add))
                link(nc.vector.tensor_reduce(mx[:], sc[:].rearrange("p t i h -> p t h i"), AX.X, ALU.max))
                nc.vector.tensor_tensor(sc[:], sc[:], mx[:].unsqueeze(2).broadcast_to([P, B, B, SH_]),
                                        ALU.subtract).then_inc(s["score_sub"], 1)
                dve.wait_ge(s["tap_exp"], c + 1)
                link(nc.vector.tensor_reduce(tden[:], tap[:], AX.X, ALU.add))
                nc.vector.reciprocal(tden[:], tden[:]).then_inc(s["tap_inv"], 1)
                dve.wait_ge(s["score_exp"], c + 1)
                link(nc.vector.tensor_reduce(den[:], sc[:].rearrange("p t i h -> p t h i"), AX.X, ALU.add))
                link(nc.vector.reciprocal(den[:], den[:]))
                link(nc.vector.tensor_tensor(sc[:], sc[:], den[:].unsqueeze(2).broadcast_to([P, B, B, SH_]), ALU.mult))
                for t in range(B):
                    ins = nc.vector.tensor_tensor(
                        prod[:, t].rearrange("p (i h d) -> p i h d", h=SH_, d=SD),
                        v.rearrange("p i (h d) -> p i h d", d=SD),
                        sc[:, t].unsqueeze(3).broadcast_to([P, B, SH_, SD]), ALU.mult)
                link(ins)
                if c >= 1:
                    dve.wait_ge(s["cat_tr"], B * c)
                nc.vector.tensor_reduce(cat[:, :, 0:E], prod[:].rearrange("p t (i e) -> p t e i", e=E), AX.X,
                                        ALU.add).then_inc(s["attn_done"], 1)

            def finish(c):
                for t in range(B):
                    n = B * c + t
                    dve.wait_ge(s["cat_hi_done"], n + 1)
                    nc.vector.tensor_tensor(cat_lo[:, n % 2], ps_cat[:, n % 2], cat_hi[:, n % 2].bitcast(F32),
                                            ALU.subtract).then_inc(s["cat_lo_done"], 1)
                    if t >= 1:
                        residual(c, t - 1)
                residual(c, B - 1)
                link(nc.vector.bn_aggr(mv[:, 0], st[:, 0]))
                for t in range(1, B - 1):
                    nc.vector.bn_aggr(mv[:, t], st[:, t])
                nc.vector.bn_aggr(mv[:, B - 1], st[:, B - 1]).then_inc(s["var_ready"], 1)
                dve.wait_ge(s["rstd_done"], c + 1)
                for t in range(B):
                    nc.vector.tensor_scalar(X[:, t * NC + c], y[:, t], mv[:, t, 0:1], rstd[:, t:t + 1],
                                            ALU.subtract, ALU.mult).then_inc(s["x1_done"], 1)
                for t in range(B):
                    n = B * c + t
                    dve.wait_ge(s["x1_hi_done"], n + 1)
                    if n >= 2:
                        dve.wait_ge(x1_out[n % 2], 32 * (n // 2))
                    nc.vector.tensor_tensor(x1s_lo[:, n % 2], ps_x1[:, 0:E].rearrange("p (k n) -> p k n", k=EC),
                                            x1s_hi[:, n % 2].bitcast(F32), ALU.subtract).then_inc(s["x1_lo_done"], 1)
                for t in range(B):
                    ins = nc.vector.tensor_tensor(X[:, t * NC + c], X[:, t * NC + c], xbo[:], ALU.add)
                link(ins)

            def residual(c, t):
                n = B * c + t
                link(nc.vector.tensor_tensor(xb[:], X[:, t * NC + c], bo[:], ALU.add))
                dve.wait_ge(s["out_mm"], n + 1)
                nc.vector.tensor_tensor(y[:, t], ps_out[:, 0:E], xb[:], ALU.add).then_inc(s["y_ready"], 1)
                dve.wait_ge(s["y_ready"], n + 1)
                link(nc.vector.bn_stats(st[:, t], y[:, t]))

            take_projection(0)
            attend(0)
            for c in range(NC):
                if c + 1 < NC:
                    take_projection(c + 1)
                finish(c)
                if c + 1 < NC:
                    attend(c + 1)


RING = 3
RING_JOBS = ("K", "Q", "MX", "SH", "V", "RS", "OP")
NPB = 4


def prepare(p):
    keys = [("K", p, c) for c in range(4)]
    maxima = [("MX", p, c, h, n) for c in range(4) for h in range(2) for n in range(NC)]
    return keys, maxima


def first_round():
    keys, maxima = prepare(0)
    return ([("LDC",), ("LDA",), ("LDB",), ("X1",), ("CX", 0), ("CX", 1), ("WA",), ("WB",)] + keys[:1] + [("Q", 0)]
            + keys[1:] + [("K2", 0)] + maxima + [("SH", 0)] + [("V", t) for t in range(MT)])


def block(p, extra, maxima, tail):
    steps, maxima = [], list(maxima)

    def some(k):
        for _ in range(k):
            if maxima:
                steps.append(maxima.pop(0))

    for t in range(MT):
        steps.append(("S", p, t))
        if t >= MX_FROM:
            some(MX_AFTER_S)
        if t >= 2:
            steps.append(("PV", p, t - 2))
        steps.extend(extra.get(t, []))
        if t >= MX_FROM:
            some(MX_AFTER_PV)
    some(len(maxima))
    steps.append(("PV", p, MT - 2))
    steps += tail.get(0, [])
    steps.append(("PV", p, MT - 1))
    return steps + tail.get(1, [])


MX_FROM, MX_AFTER_S, MX_AFTER_PV = 2, 1, 2


def one_round(last):
    keys, maxima = prepare(1)
    extra = {0: [keys[0], ("Q", 1)], 1: [keys[1]], 2: [keys[2]], 3: [keys[3], ("K2", 1)], 5: [], 7: [],
             9: [("WA",)]}
    if not last:
        extra[4] = [("X1",), ("CX", 0)]
        extra[6] = [("CX", 1)]
    extra[0] = ([] if last else [("LDC",), ("LDB",)]) + [("LDA",)] + extra[0]
    a = block(0, extra, maxima, {0: [("SH", 1)]})
    extra = {2: [("RS", 0)], 7: [("OP", 0, 0)], 8: [("OP", 0, 1)]}
    tail = {1: [("RS", 1), ("OP", 1, 0), ("OP", 1, 1)]}
    maxima = []
    if not last:
        keys, maxima = prepare(0)
        extra = {0: [keys[0], ("Q", 0)], 1: [keys[1]], 2: [keys[2], ("RS", 0)], 3: [keys[3], ("K2", 0)],
                 5: [("WB",)], 7: [("OP", 0, 0)], 8: [("OP", 0, 1)]}
        vs = [("V", t) for t in range(MT)]
        tail = {0: [("SH", 0)], 1: vs[:4] + [("RS", 1)] + vs[4:] + [("OP", 1, 0), ("OP", 1, 1)]}
    return a + block(1, extra, maxima, tail)


class Count:

    def __init__(self, before, steps, prev):
        self.before, self.here, self.prev, self.jobs, self.njobs = before, {}, prev, {}, 0
        self.prologue = not prev
        self.total = {}
        for st in steps:
            for k in self.keys(st, None):
                self.total[k] = self.total.get(k, 0) + 1

    def keys(self, st, _):
        out = [st[0]]
        if st[0] == "PV" and st[2] >= 1:
            out.append("ADD")
        if st[0] == "PV" and st[2] == MT - 1:
            out.append("COPY")
        if st[0] in RING_JOBS:
            out.append("ring%d" % (self.njobs % RING))
            self.njobs += 1
        return out

    def start(self):
        self.njobs = 0

    def of(self, key):
        return self.before.get(key, 0) + self.here.get(key, 0)

    def slot(self):
        return self.njobs % RING

    def job(self, st):
        if st in self.jobs:
            slot, n = self.jobs[st]
            return slot, self.before.get("ring%d" % slot, 0) + n
        slot, n = self.prev[st]
        return slot, self.before.get("ring%d" % slot, 0) + n

    def take(self, st):
        for k in self.keys(st, None):
            self.here[k] = self.here.get(k, 0) + 1
            if k.startswith("ring"):
                self.jobs[st] = (int(k[4:]), self.here[k])

    def left(self):
        return {st: (slot, n - self.total["ring%d" % slot]) for st, (slot, n) in self.jobs.items()}


def walk(eng, handle):
    prologue, steady, final = first_round(), one_round(False), one_round(True)
    ROUNDS = B * QUADS

    def run(i, steps, before, prev):
        n = Count(before, steps, prev)
        n.start()
        for st in steps:
            handle(i, n, st)
            n.take(st)
        return n

    n0 = run(-1, prologue, {}, {})
    base = dict(n0.total)
    n1 = run(0, steady, base, n0.left())
    per = n1.total

    def before(i):
        return {k: base.get(k, 0) + i * per.get(k, 0) for k in set(base) | set(per)}

    left = n1.left()
    with eng.Fori(1, ROUNDS - 1) as i:
        run(i, steady, before(i), left)
    return run(ROUNDS - 1, final, before(ROUNDS - 1), left)


def cross_attention(nc, a, X, consts, x1_hi, x1_lo):
    ident, ones = consts["ident"], consts["ones"]
    with ExitStack() as ctx:
        def sb(name, shape, dt=F32):
            return ctx.enter_context(nc.sbuf_tensor("xa_" + name, shape, dt))

        WA_W = EC * (P + P + 2 * P) + 2 * E
        WB_W = EC * 2 * P
        ctx_raw = sb("ctx_raw", [P, EC, M])
        ctx_hi = sb("ctx_hi", [P, EC, M], F32R)
        ctx_lo = sb("ctx_lo", [P, EC, M], F32R)
        wa_raw, wa_hi, wa_lo = sb("wa_raw", [P, WA_W]), sb("wa_hi", [P, WA_W], F32R), sb("wa_lo", [P, WA_W], F32R)
        wb_raw, wb_hi, wb_lo = sb("wb_raw", [P, WB_W]), sb("wb_hi", [P, WB_W], F32R), sb("wb_lo", [P, WB_W], F32R)
        xh, xl = sb("xh", [P, EC, N], F32R), sb("xl", [P, EC, N], F32R)
        k_two = [sb(f"k_two{p}", [P, 2, M], F32R) for p in range(2)]
        k_one = [sb(f"k_one{p}", [P, 2, M], F32R) for p in range(2)]
        q_two = [sb(f"q_two{p}", [P, 2, N], F32R) for p in range(2)]
        q_low = [sb(f"q_low{p}", [P, 2, N], F32R) for p in range(2)]
        v = sb("v", [P, MT, 4 * XD])
        pexp = sb("pexp", [P, NPB, 2, N])
        total = [sb(f"total{p}", [P, 2, N]) for p in range(2)]
        parts = sb("parts", [P, 2, NC, 4])
        negmax = sb("negmax", [P, NC, P])
        pv_sb, sums, inv, att = (sb(x, [P, N]) for x in ("pv_sb", "sums", "inv", "att"))
        att_hi, att_lo = sb("att_hi", [P, N], F32R), sb("att_lo", [P, N], F32R)

        ps_s = ctx.enter_context(nc.psum_tensor("ps_s", [P, 2, 2, N], F32))
        ps_pv = ctx.enter_context(nc.psum_tensor("ps_pv", [P, N], F32))
        ps_ring = ctx.enter_context(nc.psum_tensor("ps_ring", [P, RING, 512], F32))

        s = sems(ctx, nc, "ones_set zero_set scores_ready exp_done pv_done add0_done add1_done pv_copied att_ready "
                          "k_hi_done q_hi_done k_one_in shift_ready ctx_in wa_in wb_in x1_in ctx_hi_done ctx_lo_done "
                          "wa_hi_done wa_lo_done wb_hi_done wb_lo_done dve_step filled0 filled1 filled2 "
                          "drained0 drained1 drained2")
        filled = [s[f"filled{r}"] for r in range(RING)]
        drained = [s[f"drained{r}"] for r in range(RING)]
        block = ctx.enter_context(nc.Block())

        def w_a(t, part, k):
            at = (k * P, EC * P + k * P, 2 * EC * P + k * 2 * P)[part]
            return t[:, at:at + (2 * P if part == 2 else P)]

        def w_b(t, part, k):
            return t[:, part * EC * P + k * P:part * EC * P + (k + 1) * P]

        def w_kq(hi, p, part, k):
            return w_a(wa_hi if hi else wa_lo, part, k) if p == 0 else w_b(wb_hi if hi else wb_lo, part, k)

        def w_out(t, p):
            at = EC * 4 * P + p * E
            return t[:, at:at + E]

        def rows(t):
            return M_LAST if t == MT - 1 else P

        def half(p64):
            return slice(0, XD) if p64 == 0 else slice(XD, P)

        def user_before(p, t):
            n = p * MT + t
            if n >= NPB:
                return n - NPB
            return max(m for m in range(2 * MT) if m % NPB == n % NPB) - 2 * MT

        def adds_through(m):
            return m // MT * (MT - 1) + max(m % MT, 1)

        def next_batch(i):
            return (i + 1) // QUADS

        def pack_at(i):
            return i % QUADS

        @block.sync
        def _(sp):
            def handle(i, n, st):
                kind = st[0]
                if kind == "LDC":
                    need(sp, s["ctx_lo_done"], n.of("CX"))
                    sp.dma_start(ctx_raw[:], a["ctxT"][bass.ds(next_batch(i), 1)]
                                 .rearrange("b (k p) m -> p (b k) m", p=P)).then_inc(s["ctx_in"], 16)
                elif kind == "LDA":
                    need(sp, s["wa_lo_done"], n.of("WA"))
                    sp.dma_start(wa_raw[:], a["pack_a"][bass.ds(pack_at(i), 1)].rearrange("b p w -> p (b w)"))\
                        .then_inc(s["wa_in"], 16)
                elif kind == "LDB":
                    need(sp, s["wb_lo_done"], n.of("WB"))
                    sp.dma_start(wb_raw[:], a["pack_b"][bass.ds(pack_at(i), 1)].rearrange("b p w -> p (b w)"))\
                        .then_inc(s["wb_in"], 16)
                elif kind == "X1":
                    if not n.prologue:
                        slot, c = n.job(("K", 1, 3))
                        sp.wait_ge(filled[slot], c)
                    for dst, src in ((xh, x1_hi), (xl, x1_lo)):
                        sp.dma_start(dst[:].bitcast(F32), src[bass.ds(next_batch(i), 1)]
                                     .rearrange("b p k n -> p (b k) n")).then_inc(s["x1_in"], 16)
                elif kind == "K2":
                    p = st[1]
                    if n.prologue:
                        sp.wait_ge(s["ones_set"], 4)
                    sp.wait_ge(s["k_hi_done"], 2 * n.of("K"))
                    for h in range(2):
                        sp.dma_start(k_one[p][half(h), h, :].bitcast(F32), k_two[p][half(h), h, :].bitcast(F32))\
                            .then_inc(s["k_one_in"], 16)

            walk(sp, handle)

        @block.tensor
        def _(pe):
            def take_bank(n):
                r = n.slot()
                need(pe, drained[r], n.of("ring%d" % r))
                return r

            def project(out, terms):
                for q, (w, x) in enumerate(terms):
                    ins = nc.tensor.matmul(out, w, x, start=q == 0, stop=q == len(terms) - 1)
                return ins

            def handle(i, n, st):
                kind = st[0]
                if kind == "S":
                    p, t = st[1:]
                    if t == 0:
                        r, c = n.job(("SH", p))
                        pe.wait_ge(drained[r], c)
                        pe.wait_ge(s["k_one_in"], 32 * n.of("K2"))
                    need(pe, s["exp_done"], n.of("S") - 1)
                    m, ms = rows(t), slice(t * P, t * P + rows(t))
                    for h in range(2):
                        nc.tensor.matmul(ps_s[0:m, t_of(n), h, :], k_two[p][:, h, ms], q_two[p][:, h, :],
                                         start=True, stop=False)
                        ins = nc.tensor.matmul(ps_s[0:m, t_of(n), h, :], k_one[p][:, h, ms], q_low[p][:, h, :],
                                               start=False, stop=True)
                    ins.then_inc(s["scores_ready"], 1)
                elif kind == "PV":
                    p, t = st[1:]
                    if t == 0:
                        need(pe, s["pv_copied"], n.of("COPY"))
                        if p == 0:
                            r, c = n.job(("V", MT - 1))
                            pe.wait_ge(drained[r], c)
                    pe.wait_ge(s["exp_done"], n.of("PV") + 1)
                    m, buf = rows(t), (p * MT + t) % NPB
                    for h in range(2):
                        at = (2 * p + h) * XD
                        ins = nc.tensor.matmul(ps_pv[half(h), :], v[0:m, t, at:at + XD], pexp[0:m, buf, h, :],
                                               start=t == 0, stop=t == MT - 1)
                    ins.then_inc(s["pv_done"], 1)
                elif kind == "K":
                    p, c = st[1:]
                    r = take_bank(n)
                    if c == 0:
                        if p == 0:
                            pe.wait_ge(s["ctx_lo_done"], n.of("CX"))
                            pe.wait_ge(s["wa_lo_done"], n.of("WA"))
                        else:
                            pe.wait_ge(s["wb_lo_done"], n.of("WB"))
                    cols = slice(KC0[c], KC0[c] + CW)
                    terms = [(w_kq(wh, p, 0, k), (ctx_hi if ch else ctx_lo)[:, k, cols])
                             for wh, ch in ((1, 1), (0, 1), (1, 0)) for k in range(EC)]
                    project(ps_ring[:, r, 0:CW], terms).then_inc(filled[r], 1)
                elif kind == "Q":
                    p = st[1]
                    r = take_bank(n)
                    pe.wait_ge(s["x1_in"], 32 * n.of("X1"))
                    terms = [(w_kq(wh, p, 1, k), (xh if ch else xl)[:, k, :])
                             for wh, ch in ((1, 1), (0, 1), (1, 0)) for k in range(EC)]
                    project(ps_ring[:, r, :], terms).then_inc(filled[r], 1)
                elif kind == "MX":
                    p, c, h, q = st[1:]
                    r = take_bank(n)
                    kr, kc = n.job(("K", p, c))
                    pe.wait_ge(drained[kr], kc)
                    if c == 0:
                        qr, qc = n.job(("Q", p))
                        pe.wait_ge(drained[qr], qc)
                    nc.tensor.matmul(ps_ring[:, r, 0:CW], q_two[p][:, h, q * P:(q + 1) * P],
                                     k_two[p][:, h, KC0[c]:KC0[c] + CW], start=True, stop=True)\
                        .then_inc(filled[r], 1)
                elif kind == "SH":
                    r = take_bank(n)
                    pe.wait_ge(s["shift_ready"], 2 * (n.of("SH") + 1))
                    for q in range(NC):
                        ins = nc.tensor.matmul(ps_ring[:, r, q * P:(q + 1) * P], negmax[:, q, :], ident[:],
                                               start=True, stop=True)
                    ins.then_inc(filled[r], 1)
                elif kind == "V":
                    t = st[1]
                    r = take_bank(n)
                    m, ms = rows(t), slice(t * P, t * P + rows(t))
                    terms = [((ctx_hi if ch else ctx_lo)[:, k, ms], w_a(wa_hi if wh else wa_lo, 2, k))
                             for wh, ch in ((1, 1), (0, 1), (1, 0)) for k in range(EC)]
                    project(ps_ring[0:m, r, 0:4 * XD], terms).then_inc(filled[r], 1)
                elif kind == "RS":
                    p = st[1]
                    r = take_bank(n)
                    pe.wait_ge(s["add0_done"], n.of("ADD"))
                    pe.wait_ge(s["add1_done"], n.of("ADD"))
                    for h in range(2):
                        ins = nc.tensor.matmul(ps_ring[half(h), r, :], ones[:, 0:XD], total[p][:, h, :],
                                               start=True, stop=True)
                    ins.then_inc(filled[r], 1)
                elif kind == "OP":
                    p, j = st[1:]
                    r = take_bank(n)
                    pe.wait_ge(s["att_ready"], n.of("RS"))
                    for q in range(2):
                        cs = slice((2 * j + q) * P, (2 * j + q + 1) * P)
                        terms = [(att_hi[:, cs], w_out(wa_hi, p)), (att_lo[:, cs], w_out(wa_hi, p)),
                                 (att_hi[:, cs], w_out(wa_lo, p))]
                        ins = project(ps_ring[:, r, q * E:(q + 1) * E], terms)
                    ins.then_inc(filled[r], 1)

            def t_of(n):
                return n.here.get("S", 0) % 2

            walk(pe, handle)

        @block.scalar
        def _(act):
            def handle(i, n, st):
                kind = st[0]
                if kind == "S":
                    p, t = st[1:]
                    act.wait_ge(s["scores_ready"], n.of("S") + 1)
                    m, buf, prev = rows(t), (p * MT + t) % NPB, user_before(p, t)
                    first = n.before.get("S", 0)
                    need(act, s["pv_done"], first + prev + 1)
                    need(act, s["add0_done"], n.before.get("ADD", 0) + adds_through(prev))
                    need(act, s["add1_done"], n.before.get("ADD", 0) + adds_through(prev))
                    nc.scalar.activation(pexp[0:m, buf], ps_s[0:m, (p * MT + t) % 2], ACT.Exp, scale=XD ** -0.5)\
                        .then_inc(s["exp_done"], 1)
                elif kind == "PV" and st[2] == MT - 1:
                    act.wait_ge(s["pv_done"], n.of("PV") + 1)
                    need(act, s["att_ready"], n.of("RS"))
                    nc.scalar.copy(pv_sb[:], ps_pv[:]).then_inc(s["pv_copied"], 1)
                elif kind == "K":
                    p, c = st[1:]
                    r = n.slot()
                    act.wait_ge(filled[r], n.of("ring%d" % r) + 1)
                    skip = 3 * CW - KC0[3] if c == 3 else 0
                    for h in range(2):
                        nc.scalar.copy(k_two[p][half(h), h, KC0[c] + skip:KC0[c] + CW],
                                       ps_ring[half(h), r, skip:CW]).then_inc(s["k_hi_done"], 1)
                elif kind == "Q":
                    p = st[1]
                    r = n.slot()
                    act.wait_ge(filled[r], n.of("ring%d" % r) + 1)
                    for h in range(2):
                        for to in range(2):
                            nc.scalar.copy(q_two[p][half(to), h, :], ps_ring[half(h), r, :])\
                                .then_inc(s["q_hi_done"], 1)
                elif kind == "RS":
                    r = n.slot()
                    act.wait_ge(filled[r], n.of("ring%d" % r) + 1)
                    need(act, s["att_ready"], n.of("RS"))
                    nc.scalar.copy(sums[:], ps_ring[:, r, :]).then_inc(drained[r], 1)
                elif kind == "SH":
                    p = st[1]
                    r = n.slot()
                    act.wait_ge(filled[r], n.of("ring%d" % r) + 1)
                    nc.scalar.copy(q_low[p][half(1), 0, :], ps_ring[half(1), r, :])
                    nc.scalar.copy(q_low[p][half(0), 1, :], ps_ring[half(0), r, :]).then_inc(drained[r], 1)
                elif kind == "V":
                    t = st[1]
                    r = n.slot()
                    act.wait_ge(filled[r], n.of("ring%d" % r) + 1)
                    nc.scalar.copy(v[0:rows(t), t, :], ps_ring[0:rows(t), r, 0:4 * XD]).then_inc(drained[r], 1)
                elif kind == "CX":
                    k = st[1]
                    act.wait_ge(s["ctx_in"], 16 * n.of("LDC"))
                    if k == 0 and not n.prologue:
                        r, c = n.job(("K", 1, 3))
                        act.wait_ge(filled[r], c)
                    nc.scalar.copy(ctx_hi[:, k], ctx_raw[:, k]).then_inc(s["ctx_hi_done"], 1)
                elif kind == "WA":
                    act.wait_ge(s["wa_in"], 16 * n.of("LDA"))
                    nc.scalar.copy(wa_hi[:], wa_raw[:]).then_inc(s["wa_hi_done"], 1)
                elif kind == "WB":
                    act.wait_ge(s["wb_in"], 16 * n.of("LDB"))
                    nc.scalar.copy(wb_hi[:], wb_raw[:]).then_inc(s["wb_hi_done"], 1)

            walk(act, handle)

        def add(eng, n, st, h, sem):
            p, t = st[1:]
            m, buf, b0 = rows(t), (p * MT + t) % NPB, (p * MT) % NPB
            eng.wait_ge(s["exp_done"], n.of("PV") + 1)
            need(eng, sem, n.of("ADD"))
            first = pexp[0:m, b0, h, :] if t == 1 else total[p][0:m, h, :]
            e = nc.vector if h == 0 else nc.gpsimd
            e.tensor_tensor(total[p][0:m, h, :], first, pexp[0:m, buf, h, :], ALU.add).then_inc(sem, 1)

        @block.gpsimd
        def _(pool):
            def handle(i, n, st):
                kind = st[0]
                if kind == "PV" and st[2] >= 1:
                    add(pool, n, st, 1, s["add1_done"])
                elif kind == "CX":
                    k = st[1]
                    pool.wait_ge(s["ctx_hi_done"], n.of("CX") + 1)
                    nc.gpsimd.tensor_tensor(ctx_lo[:, k], ctx_raw[:, k], ctx_hi[:, k].bitcast(F32), ALU.subtract)\
                        .then_inc(s["ctx_lo_done"], 1)
                elif kind == "WA":
                    pool.wait_ge(s["wa_hi_done"], n.of("WA") + 1)
                    nc.gpsimd.tensor_tensor(wa_lo[:], wa_raw[:], wa_hi[:].bitcast(F32), ALU.subtract)\
                        .then_inc(s["wa_lo_done"], 1)
                elif kind == "WB":
                    pool.wait_ge(s["wb_hi_done"], n.of("WB") + 1)
                    nc.gpsimd.tensor_tensor(wb_lo[:], wb_raw[:], wb_hi[:].bitcast(F32), ALU.subtract)\
                        .then_inc(s["wb_lo_done"], 1)

            walk(pool, handle)

        @block.vector
        def _(dve):
            nc.vector.memset(negmax[:], 0.0)
            nc.vector.memset(att[:], 1.0).then_inc(s["zero_set"], 1)
            dve.wait_ge(s["zero_set"], 1)
            for p in range(2):
                for h in range(2):
                    nc.vector.tensor_copy(k_one[p][half(1 - h), h, :],
                                          att[half(1 - h), 0:1].broadcast_to([XD, M])).then_inc(s["ones_set"], 1)

            def handle(i, n, st):
                kind = st[0]
                if kind == "PV" and st[2] >= 1:
                    add(dve, n, st, 0, s["add0_done"])
                elif kind == "K":
                    p, c = st[1:]
                    r = n.slot()
                    dve.wait_ge(s["k_hi_done"], 2 * (n.of("K") + 1))
                    skip = 3 * CW - KC0[3] if c == 3 else 0
                    cols = slice(KC0[c] + skip, KC0[c] + CW)
                    for h in range(2):
                        ins = nc.vector.tensor_tensor(k_two[p][half(1 - h), h, cols], ps_ring[half(h), r, skip:CW],
                                                      k_two[p][half(h), h, cols].bitcast(F32), ALU.subtract)
                    ins.then_inc(drained[r], 1)
                elif kind == "Q":
                    p = st[1]
                    r = n.slot()
                    dve.wait_ge(s["q_hi_done"], 4 * (n.of("Q") + 1))
                    for h in range(2):
                        ins = nc.vector.tensor_tensor(q_low[p][half(h), h, :], ps_ring[half(h), r, :],
                                                      q_two[p][half(h), h, :].bitcast(F32), ALU.subtract)
                    ins.then_inc(drained[r], 1)
                elif kind == "MX":
                    p, c, h, q = st[1:]
                    r = n.slot()
                    dve.wait_ge(filled[r], n.of("ring%d" % r) + 1)
                    nc.vector.tensor_reduce(parts[:, h, q, c:c + 1], ps_ring[:, r, 0:CW], AX.X, ALU.max)\
                        .then_inc(drained[r], 1)
                elif kind == "SH":
                    p = st[1]
                    r, c = n.job(("MX", p, 3, 1, NC - 1))
                    dve.wait_ge(drained[r], c)
                    for h, col in ((0, XD), (1, 0)):
                        nc.vector.tensor_reduce(negmax[:, :, col:col + 1], parts[:, h], AX.X, ALU.max, negate=True)\
                            .then_inc(s["shift_ready"], 1)
                elif kind == "RS":
                    r = n.slot()
                    dve.wait_ge(drained[r], n.of("ring%d" % r) + 1)
                    k = 3 * n.of("RS")
                    nc.vector.reciprocal(inv[:], sums[:]).then_inc(s["dve_step"], 1)
                    dve.wait_ge(s["dve_step"], k + 1)
                    dve.wait_ge(s["pv_copied"], n.of("RS") + 1)
                    nc.vector.tensor_tensor(att[:], pv_sb[:], inv[:], ALU.mult).then_inc(s["dve_step"], 1)
                    dve.wait_ge(s["dve_step"], k + 2)
                    nc.vector.tensor_copy(att_hi[:], att[:]).then_inc(s["dve_step"], 1)
                    dve.wait_ge(s["dve_step"], k + 3)
                    nc.vector.tensor_tensor(att_lo[:], att[:], att_hi[:].bitcast(F32), ALU.subtract)\
                        .then_inc(s["att_ready"], 1)
                elif kind == "OP":
                    p, j = st[1:]
                    r = n.slot()
                    dve.wait_ge(filled[r], n.of("ring%d" % r) + 1)
                    xs = X[:, bass.ds(i // QUADS * NC + 2 * j, 2), :].rearrange("p t e -> p (t e)")
                    nc.vector.tensor_tensor(xs, ps_ring[:, r, :], xs, ALU.add).then_inc(drained[r], 1)

            walk(dve, handle)


def expert_round(last):
    steps = [] if last else [("L", 0)]
    after = {1: [("W", 1)] + ([] if last else [("L", 1)]), 5: [] if last else [("W", 0)]}
    for u in range(2 * B):
        steps.append(("H", u))
        if u >= 1:
            steps.append(("Y", u - 1))
            if last and u > B:
                steps.append(("F1", u - 1 - B))
            if last and u > B + 1:
                steps.append(("F2", u - 2 - B))
        steps += after.get(u, [])
    steps.append(("Y", 2 * B - 1))
    if last:
        steps += [("F2", B - 2), ("F1", B - 1), ("F2", B - 1)]
    return steps


def expert_walk(eng, handle):
    ROUNDS = NE // 2

    def run(i, steps, before):
        n = {}
        for st in steps:
            handle(i, lambda k: before.get(k, 0) + n.get(k, 0), st)
            n[st[0]] = n.get(st[0], 0) + 1
        return n

    base = {"W": 1}
    n0 = run(0, expert_round(False), base)

    def before(i):
        return {k: base.get(k, 0) + i * n0.get(k, 0) for k in set(base) | set(n0)}

    with eng.Fori(1, ROUNDS - 1) as i:
        run(i, expert_round(False), before(i))
    run(ROUNDS - 1, expert_round(True), before(ROUNDS - 1))


def experts(nc, a, X, consts, out):
    ident, neghalf = consts["ident"], consts["neghalf"]
    T = B * NC
    with ExitStack() as ctx:
        def sb(name, shape, dt=F32):
            return ctx.enter_context(nc.sbuf_tensor("ex_" + name, shape, dt))

        WW = EC * HID + HC * E
        w_raw = [sb(f"w_raw{p}", [P, WW + HC]) for p in range(2)]
        b1 = [sb(f"b1{p}", [P, HC]) for p in range(2)]
        w_hi = [sb(f"w_hi{p}", [P, WW], F32R) for p in range(2)]
        w_lo = [sb(f"w_lo{p}", [P, WW], F32R) for p in range(2)]
        wg = sb("wg", [P, EC, NE])
        b2 = sb("b2", [NE, E])
        st_ = sb("st", [P, T, 6])
        mv = sb("mv", [P, T, 2])
        rstd = sb("rstd", [P, T])
        xT_hi = sb("xT_hi", [P, EC, B * N], F32R)
        xT_lo = sb("xT_lo", [P, EC, B * N], F32R)
        xT_f = sb("xT_f", [P, 2, EC, P])
        probs = sb("probs", [P, T, NE])
        gred = sb("gred", [P, T])
        top = sb("top", [P, T, 8])
        idx = sb("idx", [P, T, 8], U32)
        idxf = sb("idxf", [P, T, 8])
        norm = sb("norm", [P, T, TOPK])
        iota = sb("iota", [P, NE])
        hot = sb("hot", [P, T, NE])
        score = sb("score", [P, T, NE])
        scoreT = sb("scoreT", [NE, T, P])
        h_f = sb("h_f", [P, 2, N])
        h_hi = sb("h_hi", [P, 2, HC, N], F32R)
        h_lo = sb("h_lo", [P, 2, HC, N], F32R)

        ps_h = ctx.enter_context(nc.psum_tensor("ps_h", [P, 4, 512], F32))
        ps_y = ctx.enter_context(nc.psum_tensor("ps_y", [P, 2, 512], F32))
        ps_t = ctx.enter_context(nc.psum_tensor("ps_t", [P, 512], F32))
        ps_g = ctx.enter_context(nc.psum_tensor("ps_g", [P, 512], F32))

        s = sems(ctx, nc, "const_in w_in0 w_in1 w_hi_done w_lo_done var_ready rstd_half rstd_ready x_done xT_tr "
                          "xT_hi_done xT_lo_done gate_mm gate_sub gate_exp score_done score_tr scoreT_done b2_mm b2_added "
                          "h_mm h_act h_lo_done y_mm y_added step fstep fvar frstd_half frstd fdone stored")
        w_in = [s["w_in0"], s["w_in1"]]
        block = ctx.enter_context(nc.Block())
        pack = a["pack_e"]

        def w1(w, k, c):
            return w[:, k * HID + c * P:k * HID + (c + 1) * P]

        def w2(w, c):
            return w[:, EC * HID + c * E:EC * HID + (c + 1) * E]

        @block.sync
        def _(sp):
            for dst, src in ((wg[:], a["Wg"].rearrange("(k p) e -> p k e", p=P)), (b2[:], a["b2"])):
                sp.dma_start(dst, src).then_inc(s["const_in"], 16)
            for p in range(2):
                sp.dma_start(w_raw[p][:], pack[p]).then_inc(w_in[p], 16)

            def handle(i, n, st):
                if st[0] == "L":
                    p = st[1]
                    sp.wait_ge(s["w_lo_done"], n("W"))
                    sp.dma_start(w_raw[p][:], pack[bass.ds(2 * i + 2 + p, 1)].rearrange("e p w -> p (e w)"))\
                        .then_inc(w_in[p], 16)
                elif st[0] == "F2":
                    b = st[1]
                    sp.wait_ge(s["fdone"], NC * (b + 1))
                    sp.dma_start(out[b].rearrange("(t p) e -> p t e", p=P), X[:, NC * b:NC * (b + 1), :])\
                        .then_inc(s["stored"], 16)

            expert_walk(sp, handle)
            sp.wait_ge(s["stored"], 16 * B)

        @block.gpsimd
        def _(pool):
            for b in range(B):
                pool.wait_ge(s["var_ready"], b + 1)
                r = slice(NC * b, NC * (b + 1))
                nc.gpsimd.tensor_scalar(rstd[:, r], mv[:, r, 1], EPS, None, ALU.add).then_inc(s["rstd_half"], 1)
                pool.wait_ge(s["rstd_half"], b + 1)
                nc.gpsimd.tensor_tensor(rstd[:, r], rstd[:, r], neghalf[:, 0:NC], ALU.pow)\
                    .then_inc(s["rstd_ready"], 1)

            def split(p, k):
                pool.wait_ge(s["w_hi_done"], k)
                nc.gpsimd.tensor_tensor(w_lo[p][:], w_raw[p][:, 0:WW], w_hi[p][:].bitcast(F32), ALU.subtract)\
                    .then_inc(s["w_lo_done"], 1)

            split(0, 1)

            def handle(i, n, st):
                if st[0] == "W":
                    split(st[1], n("W") + 1)
                elif st[0] == "F1":
                    b = st[1]
                    pool.wait_ge(s["fvar"], b + 1)
                    r = slice(NC * b, NC * (b + 1))
                    nc.gpsimd.tensor_scalar(rstd[:, r], mv[:, r, 1], EPS, None, ALU.add).then_inc(s["frstd_half"], 1)
                    pool.wait_ge(s["frstd_half"], b + 1)
                    nc.gpsimd.tensor_tensor(rstd[:, r], rstd[:, r], neghalf[:, 0:NC], ALU.pow)\
                        .then_inc(s["frstd"], 1)

            expert_walk(pool, handle)

        @block.tensor
        def _(pe):
            pe.wait_ge(s["const_in"], 32)

            def gate(t):
                pe.wait_ge(s["xT_hi_done"], t + 1)
                for k in range(EC):
                    ins = nc.tensor.matmul(ps_g[:, t * NE:(t + 1) * NE], xT_f[:, t % 2, k], wg[:, k],
                                           start=k == 0, stop=k == EC - 1)
                ins.then_inc(s["gate_mm"], 1)

            for t in range(T):
                pe.wait_ge(s["x_done"], t + 1)
                need(pe, s["xT_lo_done"], t)
                for k in range(EC):
                    ins = nc.tensor.transpose(ps_t[:, k * P:(k + 1) * P], X[:, t, k * P:(k + 1) * P], ident[:])
                ins.then_inc(s["xT_tr"], 1)
                if t >= 1:
                    gate(t - 1)
            gate(T - 1)
            pe.wait_ge(s["score_done"], 1)
            for q in range(T // 4):
                for t in range(4):
                    ins = nc.tensor.transpose(ps_h[0:NE, q, t * P:(t + 1) * P], score[:, 4 * q + t, :], ident[:])
                ins.then_inc(s["score_tr"], 1)
            for j in range(T // 2):
                pe.wait_ge(s["scoreT_done"], j // 2 + 1)
                need(pe, s["b2_added"], j - 1)
                for q in range(2):
                    ins = nc.tensor.matmul(ps_y[:, j % 2, q * E:(q + 1) * E], scoreT[:, 2 * j + q, :], b2[:],
                                           start=True, stop=True)
                ins.then_inc(s["b2_mm"], 1)

            def handle(i, n, st):
                kind = st[0]
                if kind == "H":
                    u = st[1]
                    p, rows = u // B, slice(u % B * N, (u % B + 1) * N)
                    if u % B == 0:
                        pe.wait_ge(s["w_lo_done"], n("W"))
                    for c in range(HC):
                        need(pe, s["h_act"], HC * (n("H") - 1) + c + 1)
                        terms = [(w1(w_hi[p], k, c), xT_hi[:, k, rows]) for k in range(EC)] \
                            + [(w1(w_hi[p], k, c), xT_lo[:, k, rows]) for k in range(EC)] \
                            + [(w1(w_lo[p], k, c), xT_hi[:, k, rows]) for k in range(EC)]
                        for q, (w, x) in enumerate(terms):
                            ins = nc.tensor.matmul(ps_h[:, c, :], w, x, start=q == 0, stop=q == len(terms) - 1)
                        ins.then_inc(s["h_mm"], 1)
                elif kind == "Y":
                    u = st[1]
                    p = u // B
                    pe.wait_ge(s["h_lo_done"], HC * (n("Y") + 1))
                    for j in range(2):
                        need(pe, s["y_added"], 2 * n("Y") + j - 1)
                        for q in range(2):
                            cs = slice((2 * j + q) * P, (2 * j + q + 1) * P)
                            terms = [(h_hi[:, u % 2, c, cs], w2(w_hi[p], c)) for c in range(HC)] \
                                + [(h_lo[:, u % 2, c, cs], w2(w_hi[p], c)) for c in range(HC)] \
                                + [(h_hi[:, u % 2, c, cs], w2(w_lo[p], c)) for c in range(HC)]
                            for m, (h, w) in enumerate(terms):
                                ins = nc.tensor.matmul(ps_y[:, j, q * E:(q + 1) * E], h, w,
                                                       start=m == 0, stop=m == len(terms) - 1)
                        ins.then_inc(s["y_mm"], 1)

            pe.wait_ge(s["b2_added"], T // 2)
            expert_walk(pe, handle)

        @block.scalar
        def _(act):
            act.wait_ge(w_in[0], 16)
            nc.scalar.copy(b1[0][:], w_raw[0][:, WW:WW + HC])
            nc.scalar.copy(w_hi[0][:], w_raw[0][:, 0:WW]).then_inc(s["w_hi_done"], 1)
            for t in range(T):
                act.wait_ge(s["xT_tr"], t + 1)
                need(act, s["gate_mm"], t - 1)
                src = ps_t[:, 0:E].rearrange("p (k n) -> p k n", k=EC)
                nc.scalar.copy(xT_f[:, t % 2], src)
                nc.scalar.copy(xT_hi[:, :, t * P:(t + 1) * P], src).then_inc(s["xT_hi_done"], 1)
            act.wait_ge(s["gate_sub"], 1)
            nc.scalar.activation(probs[:], probs[:], ACT.Exp).then_inc(s["gate_exp"], 1)
            for q in range(T // 4):
                act.wait_ge(s["score_tr"], q + 1)
                nc.scalar.copy(scoreT[:, 4 * q:4 * q + 4, :], ps_h[0:NE, q, :].rearrange("e (t p) -> e t p", t=4))\
                    .then_inc(s["scoreT_done"], 1)

            def handle(i, n, st):
                kind = st[0]
                if kind == "H":
                    u = st[1]
                    if u % B == 0:
                        act.wait_ge(s["w_hi_done"], n("W"))
                    for c in range(HC):
                        act.wait_ge(s["h_mm"], HC * n("H") + c + 1)
                        need(act, s["h_lo_done"], HC * n("H") + c - 1)
                        if c == 0:
                            need(act, s["y_mm"], 2 * (n("H") - 1))
                        bias = b1[u // B][:, c:c + 1]
                        nc.scalar.activation(h_f[:, c % 2], ps_h[:, c, :], ACT.Relu, bias=bias)
                        nc.scalar.activation(h_hi[:, u % 2, c], ps_h[:, c, :], ACT.Relu, bias=bias)\
                            .then_inc(s["h_act"], 1)
                elif kind == "W":
                    p = st[1]
                    act.wait_ge(w_in[p], 16 * (i + (2 if p == 0 else 1)))
                    need(act, s["y_mm"], 2 * (n("Y") - 1))
                    nc.scalar.copy(b1[p][:], w_raw[p][:, WW:WW + HC])
                    nc.scalar.copy(w_hi[p][:], w_raw[p][:, 0:WW]).then_inc(s["w_hi_done"], 1)

            expert_walk(act, handle)

        @block.vector
        def _(dve):
            done = [0]

            def link(ins):
                done[0] += 1
                ins.then_inc(s["step"], 1)
                dve.wait_ge(s["step"], done[0])

            for e in range(NE):
                nc.vector.memset(iota[:, e:e + 1], float(e))

            def statistics(t0, sem):
                for t in range(t0, t0 + NC):
                    ins = nc.vector.bn_stats(st_[:, t], X[:, t])
                link(ins)
                for t in range(t0, t0 + NC):
                    ins = nc.vector.bn_aggr(mv[:, t], st_[:, t])
                ins.then_inc(sem, 1)

            def normalise(t0, sem):
                for t in range(t0, t0 + NC):
                    nc.vector.tensor_scalar(X[:, t], X[:, t], mv[:, t, 0:1], rstd[:, t:t + 1],
                                            ALU.subtract, ALU.mult).then_inc(sem, 1)

            def take_rows(b):
                for t in range(NC * b, NC * (b + 1)):
                    dve.wait_ge(s["xT_hi_done"], t + 1)
                    nc.vector.tensor_tensor(xT_lo[:, :, t * P:(t + 1) * P],
                                            ps_t[:, 0:E].rearrange("p (k n) -> p k n", k=EC),
                                            xT_hi[:, :, t * P:(t + 1) * P].bitcast(F32), ALU.subtract)\
                        .then_inc(s["xT_lo_done"], 1)

            statistics(0, s["var_ready"])
            for b in range(B):
                if b + 1 < B:
                    statistics(NC * (b + 1), s["var_ready"])
                dve.wait_ge(s["rstd_ready"], b + 1)
                normalise(NC * b, s["x_done"])
                take_rows(b)

            def over_experts(x):
                return x.unsqueeze(2).broadcast_to([P, T, NE])

            dve.wait_ge(s["gate_mm"], T)
            logits = ps_g[:, 0:T * NE].rearrange("p (t e) -> p t e", e=NE)
            link(nc.vector.tensor_reduce(gred[:], logits, AX.X, ALU.max))
            nc.vector.tensor_tensor(probs[:], logits, over_experts(gred[:]), ALU.subtract).then_inc(s["gate_sub"], 1)
            dve.wait_ge(s["gate_exp"], 1)
            link(nc.vector.tensor_reduce(gred[:], probs[:], AX.X, ALU.add))
            link(nc.vector.reciprocal(gred[:], gred[:]))
            link(nc.vector.tensor_tensor(probs[:], probs[:], over_experts(gred[:]), ALU.mult))
            for t in range(T):
                ins = nc.vector.max(top[:, t], probs[:, t])
            link(ins)
            for t in range(T):
                ins = nc.vector.max_index(idx[:, t], top[:, t], probs[:, t])
            link(ins)
            nc.vector.tensor_copy(idxf[:], idx[:])
            link(nc.vector.tensor_tensor(gred[:], top[:, :, 0], top[:, :, 1], ALU.add))
            link(nc.vector.reciprocal(gred[:], gred[:]))
            link(nc.vector.tensor_tensor(norm[:], top[:, :, 0:TOPK], gred[:].unsqueeze(2).broadcast_to([P, T, TOPK]),
                                         ALU.mult))
            for j in range(TOPK):
                dst = score if j == 0 else hot
                link(nc.vector.tensor_tensor(dst[:], iota[:].unsqueeze(1).broadcast_to([P, T, NE]),
                                             over_experts(idxf[:, :, j]), ALU.is_equal))
                link(nc.vector.tensor_tensor(dst[:], dst[:], over_experts(norm[:, :, j]), ALU.mult))
            nc.vector.tensor_tensor(score[:], score[:], hot[:], ALU.add).then_inc(s["score_done"], 1)
            for j in range(T // 2):
                dve.wait_ge(s["b2_mm"], j + 1)
                xs = X[:, 2 * j:2 * j + 2, :].rearrange("p t e -> p (t e)")
                nc.vector.tensor_tensor(xs, ps_y[:, j % 2, :], xs, ALU.add).then_inc(s["b2_added"], 1)

            def handle(i, n, st):
                kind = st[0]
                if kind == "H":
                    u = st[1]
                    for c in range(HC):
                        dve.wait_ge(s["h_act"], HC * n("H") + c + 1)
                        nc.vector.tensor_tensor(h_lo[:, u % 2, c], h_f[:, c % 2], h_hi[:, u % 2, c].bitcast(F32),
                                                ALU.subtract).then_inc(s["h_lo_done"], 1)
                elif kind == "Y":
                    u = st[1]
                    for j in range(2):
                        dve.wait_ge(s["y_mm"], 2 * n("Y") + j + 1)
                        for q in range(2):
                            t = u % B * NC + 2 * j + q
                            ins = nc.vector.scalar_tensor_tensor(
                                out=X[:, t], in0=ps_y[:, j, q * E:(q + 1) * E],
                                scalar=score[:, t, bass.ds(2 * i + u // B, 1)], in1=X[:, t],
                                op0=ALU.mult, op1=ALU.add)
                        ins.then_inc(s["y_added"], 1)
                elif kind == "F1":
                    dve.wait_ge(s["y_added"], 2 * n("Y"))
                    statistics(NC * st[1], s["fvar"])
                elif kind == "F2":
                    dve.wait_ge(s["frstd"], st[1] + 1)
                    normalise(NC * st[1], s["fdone"])

            expert_walk(dve, handle)


def build(nc, a, out):
    with ExitStack() as ctx:
        X = ctx.enter_context(nc.sbuf_tensor("X", [P, B * NC, E], F32))
        consts = {n: ctx.enter_context(nc.sbuf_tensor(n, [P, P], F32)) for n in ("ident", "ones", "neghalf")}
        x1_hi = nc.dram_tensor("x1_hi", [B, P, EC, N], F32, kind="Internal").ap()
        x1_lo = nc.dram_tensor("x1_lo", [B, P, EC, N], F32, kind="Internal").ap()
        self_attention(nc, a, X, consts, x1_hi, x1_lo)
        cross_attention(nc, a, X, consts, x1_hi, x1_lo)
        experts(nc, a, X, consts, out)

def layout(i):
    import numpy as np

    f = {k: np.asarray(v) for k, v in i.items()}
    q, k = f["L0_xattn_w_q"], f["L0_xattn_w_kv"][:, :XH * XD]
    v, o = f["L0_xattn_w_kv"][:, XH * XD:], f["L0_xattn_w_out"]

    def cols(w, quad, pair=None):
        lo = quad * 4 * XD if pair is None else (quad * 2 + pair) * 2 * XD
        w = w[:, lo:lo + (4 if pair is None else 2) * XD]
        return w.reshape(EC, P, -1).transpose(1, 0, 2).reshape(P, -1)

    def rows(quad, pair):
        return o[(quad * 2 + pair) * P:(quad * 2 + pair + 1) * P]

    nxt = [(j + 1) % QUADS for j in range(QUADS)]
    pack_a = np.stack([np.concatenate([cols(k, n, 0), cols(q, n, 0), cols(v, n), rows(j, 0), rows(j, 1)], 1)
                       for j, n in enumerate(nxt)])
    pack_b = np.stack([np.concatenate([cols(k, n, 1), cols(q, n, 1)], 1) for n in nxt])
    w1, w2 = f["L0_ffn_W1"], f["L0_ffn_W2"]
    pack_e = np.concatenate([w1.reshape(NE, EC, P, HID).transpose(0, 2, 1, 3).reshape(NE, P, -1),
                             w2.reshape(NE, HC, P, E).transpose(0, 2, 1, 3).reshape(NE, P, -1),
                             f["L0_ffn_b1"].reshape(NE, HC, P).transpose(0, 2, 1)], 2)
    x = f["x"].reshape(B * N, E)
    return {
        "x": x, "xT": x.T, "ctxT": f["ctx_1024"].transpose(0, 2, 1),
        "w_inT": f["L0_attn_in_proj_w"].T, "w_v": f["L0_attn_in_proj_w"][2 * E:], "dynT": f["L0_attn_dyn_w"].T,
        "b_in": f["L0_attn_in_proj_b"][None], "b_v": f["L0_attn_in_proj_b"][2 * E:].reshape(EC, P).T,
        "b_dyn": f["L0_attn_dyn_b"][None], "w_oT": f["L0_attn_out_proj_w"].T, "b_o": f["L0_attn_out_proj_b"][None],
        "b_xo": f["L0_xattn_b_out"][None], "pack_a": pack_a, "pack_b": pack_b,
        "Wg": f["L0_ffn_Wg"], "pack_e": pack_e,
        "b2": f["L0_ffn_b2"],
    }


def kernel(**inputs):
    import concourse.bacc as bacc
    import numpy as np
    from concourse.bass_utils import run_bass_kernel_spmd

    nc = bacc.Bacc("TRN2", target_bir_lowering=False, num_devices=1)
    arrays, a = {}, {}
    for name, v in layout(inputs).items():
        v = np.ascontiguousarray(v)
        arrays["in_" + name] = v
        a[name] = nc.dram_tensor("in_" + name, v.shape, mybir.dt.from_np(v.dtype), kind="ExternalInput").ap()
    out = nc.dram_tensor("out", (B, N, E), F32, kind="ExternalOutput").ap()
    build(nc, a, out)
    r = run_bass_kernel_spmd(nc, [arrays], core_ids=[0])
    return r.results[0]["out"]
```

```python
from contextlib import ExitStack

import concourse.bass as bass
from concourse import mybir

P = 128
F32 = mybir.dt.float32
F32R = mybir.dt.float32r
U32 = mybir.dt.uint32
ALU = mybir.AluOpType
ACT = mybir.ActivationFunctionType
AX = mybir.AxisListType

B, N, E = 4, 512, 256
EC = E // P
NC = N // P
M = 1601
SH_, SD = 16, 16
TAPS, PAD_L = 15, 7
XH, XD = 16, 64
PAIRS = XH // 2
QUADS = XH // 4
MT = (M + P - 1) // P
M_LAST = M - (MT - 1) * P
CW = 402
KC0 = [0, CW, 2 * CW, M - CW]
NE, HID, TOPK = 8, 512, 2
HC = HID // P
QKV = 3 * E
DYN = SH_ * TAPS
ALLW = QKV + DYN
HALF = ALLW // 2
EPS = 1e-5


def sems(ctx, nc, names):
    return {n: ctx.enter_context(nc.semaphore(n)) for n in names.split()}


def need(eng, sem, value):
    if not isinstance(value, int) or value > 0:
        eng.wait_ge(sem, value)


def self_attention(nc, a, X, consts, x1_hi, x1_lo):
    ident, ones, neghalf = consts["ident"], consts["ones"], consts["neghalf"]
    with ExitStack() as ctx:
        def sb(name, shape, dt=F32):
            return ctx.enter_context(nc.sbuf_tensor("sa_" + name, shape, dt))

        w_raw = sb("w_raw", [P, EC, ALLW])
        w_hi = sb("w_hi", [P, EC, ALLW], F32R)
        w_lo = sb("w_lo", [P, EC, ALLW], F32R)
        wv_nat = sb("wv_nat", [P, EC, E])
        dynT = sb("dynT", [P, EC, DYN])
        bv_col = sb("bv_col", [P, EC])
        bv_wide = sb("bv_wide", [P, EC, P])
        bias = sb("bias", [P, ALLW])
        wo_raw = sb("wo_raw", [P, 2 * EC, E])
        wo_hi = sb("wo_hi", [P, 2 * EC, E], F32R)
        wo_lo = sb("wo_lo", [P, 2 * EC, E], F32R)
        bo = sb("bo", [P, E])
        sel_raw, sel = sb("sel_raw", [P, P]), sb("sel", [P, P], F32R)
        bias2, bo2 = sb("bias2", [P, ALLW], F32R), sb("bo2", [P, E], F32R)
        xT = sb("xT", [P, 2, EC, B, P])
        xT_hi = sb("xT_hi", [P, 2, EC, B, P], F32R)
        xT_lo = sb("xT_lo", [P, 2, EC, B, P], F32R)
        qkv = sb("qkv", [P, 2, B, ALLW])
        prod = sb("prod", [P, B, B * E])
        sc = sb("sc", [P, B, B, SH_])
        mx = sb("mx", [P, B, SH_])
        den = sb("den", [P, B, SH_])
        tap = sb("tap", [P, B, SH_, TAPS])
        tmx = sb("tmx", [P, B, SH_])
        tden = sb("tden", [P, B, SH_])
        cprod = sb("cprod", [P, B, E])
        csum = sb("csum", [P, 2, E])
        cat = sb("cat", [P, B, 2 * E])
        cat_hi = sb("cat_hi", [P, 2, 2 * E], F32R)
        cat_lo = sb("cat_lo", [P, 2, 2 * E], F32R)
        y = sb("y", [P, B, E])
        st = sb("st", [P, B, 6])
        mv = sb("mv", [P, B, 2])
        rstd = sb("rstd", [P, B])
        x1s_hi = sb("x1s_hi", [P, 2, EC, P], F32R)
        x1s_lo = sb("x1s_lo", [P, 2, EC, P], F32R)
        xbo = sb("xbo", [P, E])

        ps_qkv = ctx.enter_context(nc.psum_tensor("ps_qkv", [P, 2, 2, 512], F32))
        ps_cat = ctx.enter_context(nc.psum_tensor("ps_cat", [P, 2, 512], F32))
        ps_out = ctx.enter_context(nc.psum_tensor("ps_out", [P, 512], F32))
        ps_x1 = ctx.enter_context(nc.psum_tensor("ps_x1", [P, 512], F32))

        s = sems(ctx, nc, "fold_in w_in b_in wo_in res_in x_in0 x_in1 const_ready fold_mm fold_evac w_hi_done w_lo_done x_hi_done x_lo_done "
                          "qkv_mm qkv_ready score_sub score_exp tap_max tap_sub tap_exp tap_inv tap_w conv_step "
                          "conv_done attn_done cat_tr cat_hi_done cat_lo_done out_mm var_ready rstd_half rstd_done bias_hi bias_ready bo_ready "
                          "x1_done y_ready x1_tr x1_hi_done x1_lo_done x1_out0 x1_out1 step pstep")
        x_in = [s["x_in0"], s["x_in1"]]
        x1_out = [s["x1_out0"], s["x1_out1"]]
        block = ctx.enter_context(nc.Block())

        RSTD_AT = 2

        def run(steps, order):
            for c in range(NC + 2):
                for name in order.split():
                    step, d = steps[name[0]]
                    if (0 if d < 1 else 1) <= c + d < NC:
                        if len(name) > 1:
                            step(c + d, int(name[1:]))
                        else:
                            step(c + d)

        @block.sync
        def _(sp):
            sp.dma_start(wv_nat[:], a["w_v"].rearrange("(k p) n -> p k n", p=P)).then_inc(s["fold_in"], 16)
            sp.dma_start(dynT[:], a["dynT"].rearrange("(k p) n -> p k n", p=P)).then_inc(s["fold_in"], 16)
            sp.dma_start(bv_col[:], a["b_v"]).then_inc(s["fold_in"], 16)
            sp.dma_start(w_raw[:, :, 0:QKV], a["w_inT"].rearrange("(k p) n -> p k n", p=P)).then_inc(s["w_in"], 16)
            sp.dma_start(bias[:, 0:QKV], a["b_in"].broadcast_to([P, QKV])).then_inc(s["b_in"], 16)
            sp.dma_start(bias[:, QKV:ALLW], a["b_dyn"].broadcast_to([P, DYN])).then_inc(s["b_in"], 16)
            for c in range(NC):
                for k in range(EC):
                    if c >= 2 and k == 0:
                        sp.wait_ge(s["x_lo_done"], c - 1)
                    src = a["xT"].rearrange("(k p) (t c n) -> p k t c n", p=P, t=B, c=NC)[:, k, :, c, :]
                    sp.dma_start(xT[:, c % 2, k], src).then_inc(x_in[c % 2], 16)
                if c == 0:
                    sp.dma_start(X[:], a["x"].rearrange("(t p) e -> p t e", p=P)).then_inc(s["res_in"], 16)
                    sp.dma_start(bo[:], a["b_o"].broadcast_to([P, E])).then_inc(s["res_in"], 16)
                    sp.dma_start(xbo[:], a["b_xo"].broadcast_to([P, E])).then_inc(s["res_in"], 16)
                    sp.dma_start(wo_raw[:], a["w_oT"].rearrange("(k p) n -> p k n", p=P)).then_inc(s["wo_in"], 16)
            for n in range(NC * B):
                c, t = n // B, n % B
                sp.wait_ge(s["x1_hi_done"], n + 1)
                sp.dma_start(x1_hi[t][:, :, c * P:(c + 1) * P], x1s_hi[:, n % 2].bitcast(F32)).then_inc(x1_out[n % 2], 16)
                sp.wait_ge(s["x1_lo_done"], n + 1)
                sp.dma_start(x1_lo[t][:, :, c * P:(c + 1) * P], x1s_lo[:, n % 2].bitcast(F32)).then_inc(x1_out[n % 2], 16)
            for q in x1_out:
                sp.wait_ge(q, 16 * NC * B)


        @block.gpsimd
        def _(pool):
            pool.memset(ones[:], 1.0)
            pool.memset(neghalf[:], -0.5)
            pool.memset(ident[:], 0.0).then_inc(s["pstep"], 1)
            pool.wait_ge(s["pstep"], 1)
            nc.gpsimd.affine_select(out=ident[:], in_=ident[:], compare_op=ALU.not_equal, fill=1.0, base=0,
                                    pattern=[[-1, P]], channel_multiplier=1).then_inc(s["const_ready"], 1)

            def split_x(c):
                pool.wait_ge(s["x_hi_done"], c + 1)
                nc.gpsimd.tensor_tensor(xT_lo[:, c % 2], xT[:, c % 2], xT_hi[:, c % 2].bitcast(F32),
                                        ALU.subtract).then_inc(s["x_lo_done"], 1)

            def conv(c, t):
                w = tap[:, t, :, PAD_L - t:PAD_L - t + B].rearrange("p h i -> p i h")
                for i in range(B):
                    ins = nc.gpsimd.tensor_tensor(
                        cprod[:, i].rearrange("p (h d) -> p h d", d=SD),
                        qkv[:, c % 2, i, 2 * E:3 * E].rearrange("p (h d) -> p h d", d=SD),
                        w[:, i].unsqueeze(2).broadcast_to([P, SH_, SD]), ALU.mult)
                ins.then_inc(s["conv_step"], 1)
                k = 3 * (B * c + t)
                pool.wait_ge(s["conv_step"], k + 1)
                nc.gpsimd.tensor_tensor(csum[:], cprod[:, 0:2], cprod[:, 2:4], ALU.add).then_inc(s["conv_step"], 1)
                pool.wait_ge(s["conv_step"], k + 2)
                need(pool, s["cat_tr"], B * (c - 1) + t + 1)
                nc.gpsimd.tensor_tensor(cat[:, t, E:2 * E], csum[:, 0], csum[:, 1],
                                        ALU.add).then_inc(s["conv_step"], 1)
                pool.wait_ge(s["conv_step"], k + 3)

            def deviation(c):
                pool.wait_ge(s["var_ready"], c + 1)
                nc.gpsimd.tensor_scalar(rstd[:], mv[:, :, 1], EPS, None, ALU.add).then_inc(s["rstd_half"], 1)
                pool.wait_ge(s["rstd_half"], c + 1)
                nc.gpsimd.tensor_tensor(rstd[:], rstd[:], neghalf[:, 0:B], ALU.pow).then_inc(s["rstd_done"], 1)

            split_x(0)
            split_x(1)
            for c in range(NC):
                logits = qkv[:, c % 2, :, QKV:ALLW].rearrange("p t (h k) -> p t h k", k=TAPS)
                pool.wait_ge(s["tap_max"], c + 1)
                for t in range(B):
                    ins = nc.gpsimd.tensor_tensor(tap[:, t], logits[:, t],
                                                  tmx[:, t].unsqueeze(2).broadcast_to([P, SH_, TAPS]), ALU.subtract)
                ins.then_inc(s["tap_sub"], 1)
                pool.wait_ge(s["tap_inv"], c + 1)
                for t in range(B):
                    ins = nc.gpsimd.tensor_tensor(tap[:, t], tap[:, t],
                                                  tden[:, t].unsqueeze(2).broadcast_to([P, SH_, TAPS]), ALU.mult)
                ins.then_inc(s["tap_w"], 1)
                pool.wait_ge(s["tap_w"], c + 1)
                for t in range(B):
                    conv(c, t)
                    if t == 1 and c + 2 < NC:
                        split_x(c + 2)
                    if t == RSTD_AT and c >= 1:
                        deviation(c - 1)
            deviation(NC - 1)

        @block.tensor
        def _(pe):
            pe.wait_ge(s["fold_in"], 48)
            for kc in range(EC):
                for ec in range(EC):
                    ins = nc.tensor.matmul(ps_qkv[:, 0, kc, 0:DYN], wv_nat[:, ec, kc * P:(kc + 1) * P], dynT[:, ec],
                                           start=ec == 0, stop=ec == EC - 1)
            ins.then_inc(s["fold_mm"], 1)
            pe.wait_ge(s["step"], 3)
            for ec in range(EC):
                ins = nc.tensor.matmul(ps_qkv[:, 1, 0, 0:DYN], bv_wide[:, ec], dynT[:, ec],
                                       start=ec == 0, stop=ec == EC - 1)
            ins.then_inc(s["fold_mm"], 1)

            def project(c, t):
                if t == 0:
                    pe.wait_ge(s["x_lo_done"], c + 1)
                n = B * c + t
                for h in range(2):
                    if n < 2:
                        pe.wait_ge(s["fold_evac"], 2)
                        pe.wait_ge(s["w_lo_done"], 1)
                        pe.wait_ge(s["bias_ready"], 1)
                    else:
                        pe.wait_ge(s["qkv_ready"], 2 * (n - 2) + h + 1)
                    for q, (xx, ww) in enumerate(((xT_hi, w_hi), (xT_lo, w_hi), (xT_hi, w_lo))):
                        for k in range(EC):
                            ins = nc.tensor.matmul(ps_qkv[:, n % 2, h, 0:HALF], xx[:, c % 2, k, t],
                                                   ww[:, k, h * HALF:(h + 1) * HALF],
                                                   start=q == 0 and k == 0, stop=False)
                    nc.tensor.matmul(ps_qkv[:, n % 2, h, 0:HALF], sel[:], bias2[:, h * HALF:(h + 1) * HALF],
                                     start=False, stop=True).then_inc(s["qkv_mm"], 1)

            def turn_cat(c, t):
                n = B * c + t
                if t == 0:
                    pe.wait_ge(s["attn_done"], c + 1)
                    if c == 0:
                        pe.wait_ge(s["const_ready"], 1)
                pe.wait_ge(s["conv_step"], 3 * (n + 1))
                if n >= 2:
                    pe.wait_ge(s["cat_lo_done"], n - 1)
                for j in range(2 * EC):
                    ins = nc.tensor.transpose(ps_cat[:, n % 2, j * P:(j + 1) * P], cat[:, t, j * P:(j + 1) * P],
                                              ident[:])
                ins.then_inc(s["cat_tr"], 1)

            def project_out(c, t):
                n = B * c + t
                if n == 0:
                    pe.wait_ge(s["w_lo_done"], 2)
                    pe.wait_ge(s["bo_ready"], 1)
                pe.wait_ge(s["cat_lo_done"], n + 1)
                need(pe, s["y_ready"], n)
                for q, (cc, ww) in enumerate(((cat_hi, wo_hi), (cat_lo, wo_hi), (cat_hi, wo_lo))):
                    for j in range(2 * EC):
                        ins = nc.tensor.matmul(ps_out[:, 0:E], cc[:, n % 2, j * P:(j + 1) * P], ww[:, j],
                                               start=q == 0 and j == 0, stop=False)
                nc.tensor.matmul(ps_out[:, 0:E], sel[:], bo2[:], start=False, stop=True).then_inc(s["out_mm"], 1)

            def turn_x1(c, t):
                n = B * c + t
                pe.wait_ge(s["x1_done"], n + 1)
                need(pe, s["x1_lo_done"], n)
                for k in range(EC):
                    ins = nc.tensor.transpose(ps_x1[:, k * P:(k + 1) * P], X[:, t * NC + c, k * P:(k + 1) * P],
                                              ident[:])
                ins.then_inc(s["x1_tr"], 1)

            steps = dict(P=(project, 1), C=(turn_cat, -1), O=(project_out, -1), X=(turn_x1, -2))
            for t in range(B):
                project(0, t)
            run(steps, "C0 C1 P0 X0 P1 X1 C2 O0 X2 C3 O1 P2 X3 O2 O3 P3")

        @block.scalar
        def _(act):
            def split_x(c):
                act.wait_ge(x_in[c % 2], 16 * EC * (c // 2 + 1))
                if c >= 2:
                    act.wait_ge(s["qkv_mm"], 2 * B * (c - 1))
                nc.scalar.copy(xT_hi[:, c % 2], xT[:, c % 2]).then_inc(s["x_hi_done"], 1)

            def exp_taps(c):
                act.wait_ge(s["tap_sub"], c + 1)
                nc.scalar.activation(tap[:], tap[:], ACT.Exp).then_inc(s["tap_exp"], 1)

            def exp_scores(c):
                act.wait_ge(s["score_sub"], c + 1)
                nc.scalar.activation(sc[:], sc[:], ACT.Exp, scale=SD ** -0.5).then_inc(s["score_exp"], 1)

            def high_cat(c, t):
                n = B * c + t
                act.wait_ge(s["cat_tr"], n + 1)
                need(act, s["out_mm"], n - 1)
                nc.scalar.copy(cat_hi[:, n % 2], ps_cat[:, n % 2]).then_inc(s["cat_hi_done"], 1)

            def high_x1(c, t):
                n = B * c + t
                act.wait_ge(s["x1_tr"], n + 1)
                if n >= 2:
                    act.wait_ge(x1_out[n % 2], 32 * (n // 2))
                nc.scalar.copy(x1s_hi[:, n % 2], ps_x1[:, 0:E].rearrange("p (k n) -> p k n", k=EC))\
                    .then_inc(s["x1_hi_done"], 1)

            def take(c, t):
                n = B * c + t
                if t == 0 and c >= 2:
                    act.wait_ge(s["attn_done"], c - 1)
                    act.wait_ge(s["conv_step"], 3 * B * (c - 1))
                for h in range(2):
                    act.wait_ge(s["qkv_mm"], 2 * n + h + 1)
                    nc.scalar.copy(qkv[:, c % 2, t, h * HALF:(h + 1) * HALF], ps_qkv[:, n % 2, h, 0:HALF])\
                        .then_inc(s["qkv_ready"], 1)

            split_x(0)
            act.wait_ge(s["w_in"], 16)
            act.wait_ge(s["fold_evac"], 1)
            nc.scalar.copy(w_hi[:], w_raw[:]).then_inc(s["w_hi_done"], 1)
            act.wait_ge(s["step"], 2)
            nc.scalar.copy(sel[:], sel_raw[:])
            act.wait_ge(s["fold_evac"], 2)
            nc.scalar.copy(bias2[:], bias[:]).then_inc(s["bias_hi"], 1)
            split_x(1)
            act.wait_ge(s["wo_in"], 16)
            nc.scalar.copy(wo_hi[:], wo_raw[:]).then_inc(s["w_hi_done"], 1)
            act.wait_ge(s["res_in"], 48)
            nc.scalar.copy(bo2[:], bo[:]).then_inc(s["bias_hi"], 1)
            for t in range(B):
                take(0, t)
            steps = dict(P=(take, 1), C=(high_cat, -1), X=(high_x1, -2), T=(exp_taps, 0), E=(exp_scores, 0), S=(split_x, 2))
            run(steps, "X0 C0 C1 T X1 C2 P0 E P1 X2 P2 C3 X3 S P3")

        @block.vector
        def _(dve):
            done = [0]

            def link(ins):
                done[0] += 1
                ins.then_inc(s["step"], 1)
                dve.wait_ge(s["step"], done[0])

            link(nc.vector.memset(sel_raw[:], 0.0))
            nc.vector.memset(sel_raw[0:1], 1.0)
            link(nc.vector.memset(sel_raw[32:33], 1.0))
            dve.wait_ge(s["const_ready"], 1)
            dve.wait_ge(s["fold_in"], 48)
            for ec in range(EC):
                ins = nc.vector.tensor_scalar(bv_wide[:, ec], ones[:], bv_col[:, ec:ec + 1], None, ALU.mult)
            link(ins)
            dve.wait_ge(s["fold_mm"], 1)
            nc.vector.tensor_copy(w_raw[:, :, QKV:ALLW], ps_qkv[:, 0, :, 0:DYN]).then_inc(s["fold_evac"], 1)
            dve.wait_ge(s["fold_mm"], 2)
            dve.wait_ge(s["b_in"], 32)
            nc.vector.tensor_tensor(bias[:, QKV:ALLW], bias[:, QKV:ALLW], ps_qkv[:, 1, 0, 0:DYN],
                                    ALU.add).then_inc(s["fold_evac"], 1)
            dve.wait_ge(s["w_hi_done"], 1)
            nc.vector.tensor_tensor(w_lo[:], w_raw[:], w_hi[:].bitcast(F32), ALU.subtract).then_inc(s["w_lo_done"], 1)
            low = slice(32, 64)
            dve.wait_ge(s["bias_hi"], 1)
            nc.vector.tensor_tensor(bias2[low], bias[low], bias2[low].bitcast(F32), ALU.subtract)\
                .then_inc(s["bias_ready"], 1)

            def split_out():
                dve.wait_ge(s["w_hi_done"], 2)
                nc.vector.tensor_tensor(wo_lo[:], wo_raw[:], wo_hi[:].bitcast(F32), ALU.subtract)\
                    .then_inc(s["w_lo_done"], 1)
                dve.wait_ge(s["bias_hi"], 2)
                nc.vector.tensor_tensor(bo2[low], bo[low], bo2[low].bitcast(F32), ALU.subtract)\
                    .then_inc(s["bo_ready"], 1)

            def tap_maxima(c):
                dve.wait_ge(s["qkv_ready"], 2 * B * (c + 1))
                logits = qkv[:, c % 2, :, QKV:ALLW].rearrange("p t (h k) -> p t h k", k=TAPS)
                nc.vector.tensor_reduce(tmx[:], logits, AX.X, ALU.max).then_inc(s["tap_max"], 1)

            def attend(c, part):
                q, k, v = (qkv[:, c % 2, :, j * E:(j + 1) * E] for j in range(3))
                if part == 0:
                    need(dve, s["attn_done"], c)
                    for t in range(B):
                        ins = nc.vector.tensor_tensor(prod[:, t].rearrange("p (i e) -> p i e", e=E), k,
                                                      q[:, t].unsqueeze(1).broadcast_to([P, B, E]), ALU.mult)
                    link(ins)
                elif part == 1:
                    link(nc.vector.tensor_reduce(sc[:].rearrange("p t i h -> p (t i h)"),
                                                 prod[:].rearrange("p t (g d) -> p (t g) d", d=SD), AX.X, ALU.add))
                    link(nc.vector.tensor_reduce(mx[:], sc[:].rearrange("p t i h -> p t h i"), AX.X, ALU.max))
                    nc.vector.tensor_tensor(sc[:], sc[:], mx[:].unsqueeze(2).broadcast_to([P, B, B, SH_]),
                                            ALU.subtract).then_inc(s["score_sub"], 1)
                elif part == 2:
                    dve.wait_ge(s["tap_exp"], c + 1)
                    link(nc.vector.tensor_reduce(tden[:], tap[:], AX.X, ALU.add))
                    nc.vector.reciprocal(tden[:], tden[:]).then_inc(s["tap_inv"], 1)
                elif part == 3:
                    dve.wait_ge(s["score_exp"], c + 1)
                    link(nc.vector.tensor_reduce(den[:], sc[:].rearrange("p t i h -> p t h i"), AX.X, ALU.add))
                    link(nc.vector.reciprocal(den[:], den[:]))
                    link(nc.vector.tensor_tensor(sc[:], sc[:], den[:].unsqueeze(2).broadcast_to([P, B, B, SH_]),
                                                 ALU.mult))
                elif part == 4:
                    for t in range(B):
                        ins = nc.vector.tensor_tensor(
                            prod[:, t].rearrange("p (i h d) -> p i h d", h=SH_, d=SD),
                            v.rearrange("p i (h d) -> p i h d", d=SD),
                            sc[:, t].unsqueeze(3).broadcast_to([P, B, SH_, SD]), ALU.mult)
                    link(ins)
                else:
                    need(dve, s["cat_tr"], B * c)
                    nc.vector.tensor_reduce(cat[:, :, 0:E], prod[:].rearrange("p t (i e) -> p t e i", e=E), AX.X,
                                            ALU.add).then_inc(s["attn_done"], 1)

            def low_cat(c, t):
                n = B * c + t
                dve.wait_ge(s["cat_hi_done"], n + 1)
                nc.vector.tensor_tensor(cat_lo[:, n % 2], ps_cat[:, n % 2], cat_hi[:, n % 2].bitcast(F32),
                                        ALU.subtract).then_inc(s["cat_lo_done"], 1)

            def residual(c, t):
                n = B * c + t
                if n == 0:
                    dve.wait_ge(s["res_in"], 48)
                elif t == 0:
                    dve.wait_ge(s["x1_done"], n)
                dve.wait_ge(s["out_mm"], n + 1)
                nc.vector.tensor_tensor(y[:, t], ps_out[:, 0:E], X[:, t * NC + c], ALU.add).then_inc(s["y_ready"], 1)
                dve.wait_ge(s["y_ready"], n + 1)
                ins = nc.vector.bn_stats(st[:, t], y[:, t])
                if t == B - 1:
                    link(ins)

            def statistics(c):
                for t in range(B):
                    ins = nc.vector.bn_aggr(mv[:, t], st[:, t])
                ins.then_inc(s["var_ready"], 1)

            def normalise(c):
                dve.wait_ge(s["rstd_done"], c + 1)
                for t in range(B):
                    nc.vector.tensor_scalar(X[:, t * NC + c], y[:, t], mv[:, t, 0:1], rstd[:, t:t + 1],
                                            ALU.subtract, ALU.mult).then_inc(s["x1_done"], 1)

            def low_x1(c, t):
                n = B * c + t
                dve.wait_ge(s["x1_hi_done"], n + 1)
                if n >= 2:
                    dve.wait_ge(x1_out[n % 2], 32 * (n // 2))
                nc.vector.tensor_tensor(x1s_lo[:, n % 2], ps_x1[:, 0:E].rearrange("p (k n) -> p k n", k=EC),
                                        x1s_hi[:, n % 2].bitcast(F32), ALU.subtract).then_inc(s["x1_lo_done"], 1)
                nc.vector.tensor_tensor(X[:, t * NC + c], X[:, t * NC + c], xbo[:], ALU.add)

            steps = dict(A=(attend, 0), M=(tap_maxima, 1), C=(low_cat, -1), R=(residual, -1),
                         V=(statistics, -1), N=(normalise, -1), X=(low_x1, -2))
            split_out()
            tap_maxima(0)
            run(steps, "A0 X0 C0 C1 X1 A1 R0 A2 X2 C2 R1 A3 X3 C3 R2 A4 R3 V A5 M N")


RING = 3
RING_JOBS = ("K", "Q", "MX", "SH", "V", "RS", "OP")
NPB = 4


def prepare(p):
    keys = [("K", p, c) for c in range(4)]
    maxima = [("MX", p, c, h, n) for c in range(4) for h in range(2) for n in range(NC)]
    return keys, maxima


def first_round():
    keys, maxima = prepare(0)
    return ([("LDC",), ("LDA",), ("LDB",), ("X1",), ("CX", 0), ("CX", 1), ("WA",), ("WB",)] + keys[:1] + [("Q", 0)]
            + keys[1:] + [("K2", 0)] + maxima + [("SH", 0)] + [("V", t) for t in range(MT)])


def block(p, extra, maxima, tail, share):
    steps, maxima = [], list(maxima)

    def some(k):
        for _ in range(k):
            if maxima:
                steps.append(maxima.pop(0))

    for t in range(MT):
        steps.append(("S", p, t))
        some(share[t] // 2)
        if t >= 2:
            steps.append(("PV", p, t - 2))
        steps.extend(extra.get(t, []))
        some(share[t] - share[t] // 2)
    some(len(maxima))
    steps.append(("PV", p, MT - 2))
    steps += tail.get(0, [])
    steps.append(("PV", p, MT - 1))
    return steps + tail.get(1, [])


def spread(moments):
    extra = {}
    for step, t in moments:
        extra.setdefault(t, []).append(step)
    return extra


def one_round(last):
    keys, maxima = prepare(1)
    loads = [(("LDC",), 0), (("LDB",), 0)]
    first = ([] if last else loads) + [(("LDA",), 0)]
    first += [(k, t) for k, t in zip(keys[:1] + [("Q", 1)] + keys[1:] + [("K2", 1)], AT_K)]
    if not last:
        first += [(("X1",), 4), (("CX", 0), AT_CX[0]), (("CX", 1), AT_CX[1])]
    first += [(("WA",), AT_WA)]
    a = block(0, spread(first), maxima, {0: [("SH", 1)]}, SHARE[0])
    sums = [(("RS", 0), AT_RS[0]), (("R1", 0, 0), AT_RS[1]), (("R1", 0, 1), AT_RS[2]), (("R2", 0), AT_RS[3]),
            (("R3", 0), AT_RS[4]),
            (("OP", 0, 0), AT_OP[0]), (("OP", 0, 1), AT_OP[1])]
    end = [("RS", 1), ("R1", 1, 0), ("R1", 1, 1), ("R2", 1)]
    outs = [("R3", 1), ("OP", 1, 0), ("OP", 1, 1)]
    if last:
        return a + block(1, spread(sums), [], {1: end + outs}, SHARE[1])
    keys, maxima = prepare(0)
    second = [(k, t) for k, t in zip(keys[:1] + [("Q", 0)] + keys[1:] + [("K2", 0)], AT_K)]
    vs = [("V", t) for t in range(MT)]
    tail = {0: [("SH", 0)] + vs[:V_BEFORE], 1: vs[V_BEFORE:V_RS] + end + vs[V_RS:V_R3] + outs[:1] + vs[V_R3:] + outs[1:]}
    return a + block(1, spread(second + [(("WB",), AT_WB)] + sums), maxima, tail, SHARE[1])


SHARE = ((0, 0, 1, 3, 2, 2, 4, 3, 3, 3, 5, 3, 3), (0, 0, 1, 2, 2, 3, 4, 3, 3, 3, 4, 4, 3))
AT_K = (0, 0, 0, 1, 1, 3)
AT_CX = (5, 6)
AT_WA, AT_WB = 10, 5
AT_RS = (1, 2, 3, 4, 5)
AT_OP = (6, 7)
V_BEFORE, V_RS, V_R3 = (0, 1, 9)


class Count:

    def __init__(self, before, steps, prev):
        self.before, self.here, self.prev, self.jobs, self.njobs = before, {}, prev, {}, 0
        self.prologue = not prev
        self.total = {}
        for st in steps:
            for k in self.keys(st, None):
                self.total[k] = self.total.get(k, 0) + 1

    def keys(self, st, _):
        out = [st[0]]
        if st[0] == "PV" and st[2] >= 1:
            out.append("ADD")
        if st[0] == "PV" and st[2] == MT - 1:
            out.append("COPY")
        if st[0] in RING_JOBS:
            out.append("ring%d" % (self.njobs % RING))
            self.njobs += 1
        return out

    def start(self):
        self.njobs = 0

    def of(self, key):
        return self.before.get(key, 0) + self.here.get(key, 0)

    def slot(self):
        return self.njobs % RING

    def job(self, st):
        if st in self.jobs:
            slot, n = self.jobs[st]
            return slot, self.before.get("ring%d" % slot, 0) + n
        slot, n = self.prev[st]
        return slot, self.before.get("ring%d" % slot, 0) + n

    def take(self, st):
        for k in self.keys(st, None):
            self.here[k] = self.here.get(k, 0) + 1
            if k.startswith("ring"):
                self.jobs[st] = (int(k[4:]), self.here[k])

    def left(self):
        return {st: (slot, n - self.total["ring%d" % slot]) for st, (slot, n) in self.jobs.items()}


def walk(eng, handle):
    prologue, steady, final = first_round(), one_round(False), one_round(True)
    ROUNDS = B * QUADS

    def run(i, steps, before, prev):
        n = Count(before, steps, prev)
        n.start()
        for st in steps:
            handle(i, n, st)
            n.take(st)
        return n

    n0 = run(-1, prologue, {}, {})
    base = dict(n0.total)
    n1 = run(0, steady, base, n0.left())
    per = n1.total

    def before(i):
        return {k: base.get(k, 0) + i * per.get(k, 0) for k in set(base) | set(per)}

    left = n1.left()
    with eng.Fori(1, ROUNDS - 1) as i:
        run(i, steady, before(i), left)
    return run(ROUNDS - 1, final, before(ROUNDS - 1), left)


def cross_attention(nc, a, X, consts, x1_hi, x1_lo):
    ident, ones = consts["ident"], consts["ones"]
    with ExitStack() as ctx:
        def sb(name, shape, dt=F32):
            return ctx.enter_context(nc.sbuf_tensor("xa_" + name, shape, dt))

        WA_W = EC * (P + P + 2 * P) + 2 * E
        WB_W = EC * 2 * P
        ctx_raw = sb("ctx_raw", [P, EC, M])
        ctx_hi = sb("ctx_hi", [P, EC, M], F32R)
        ctx_lo = sb("ctx_lo", [P, EC, M], F32R)
        wa_raw, wa_hi, wa_lo = sb("wa_raw", [P, WA_W]), sb("wa_hi", [P, WA_W], F32R), sb("wa_lo", [P, WA_W], F32R)
        wb_raw, wb_hi, wb_lo = sb("wb_raw", [P, WB_W]), sb("wb_hi", [P, WB_W], F32R), sb("wb_lo", [P, WB_W], F32R)
        xh, xl = sb("xh", [P, EC, N], F32R), sb("xl", [P, EC, N], F32R)
        k_two = [sb(f"k_two{p}", [P, 2, M], F32R) for p in range(2)]
        k_one = [sb(f"k_one{p}", [P, 2, M], F32R) for p in range(2)]
        q_two = [sb(f"q_two{p}", [P, 2, N], F32R) for p in range(2)]
        q_low = [sb(f"q_low{p}", [P, 2, N], F32R) for p in range(2)]
        v = sb("v", [P, MT, 4 * XD])
        pexp = sb("pexp", [P, NPB, 2, N])
        total = [sb(f"total{p}", [P, 2, N]) for p in range(2)]
        parts = sb("parts", [P, 2, NC, 4])
        negmax = sb("negmax", [P, NC, P])
        pv_sb, sums, inv, att = (sb(x, [P, N]) for x in ("pv_sb", "sums", "inv", "att"))
        att_hi, att_lo = sb("att_hi", [P, N], F32R), sb("att_lo", [P, N], F32R)

        ps_s = ctx.enter_context(nc.psum_tensor("ps_s", [P, 2, 2, N], F32))
        ps_pv = ctx.enter_context(nc.psum_tensor("ps_pv", [P, N], F32))
        ps_ring = ctx.enter_context(nc.psum_tensor("ps_ring", [P, RING, 512], F32))

        s = sems(ctx, nc, "ones_set zero_set scores_ready exp_done pv_done add0_done add1_done pv_copied att_ready "
                          "k_hi_done q_hi_done k_one_in shift_ready ctx_in wa_in wb_in x1_in ctx_hi_done ctx_lo_done "
                          "wa_hi_done wa_lo_done wb_hi_done wb_lo_done att_done att_hi_done filled0 filled1 filled2 "
                          "drained0 drained1 drained2 inv_ready")
        filled = [s[f"filled{r}"] for r in range(RING)]
        drained = [s[f"drained{r}"] for r in range(RING)]
        block = ctx.enter_context(nc.Block())

        def w_a(t, part, k):
            at = (k * P, EC * P + k * P, 2 * EC * P + k * 2 * P)[part]
            return t[:, at:at + (2 * P if part == 2 else P)]

        def w_b(t, part, k):
            return t[:, part * EC * P + k * P:part * EC * P + (k + 1) * P]

        def w_kq(hi, p, part, k):
            return w_a(wa_hi if hi else wa_lo, part, k) if p == 0 else w_b(wb_hi if hi else wb_lo, part, k)

        def w_out(t, p):
            at = EC * 4 * P + p * E
            return t[:, at:at + E]

        def rows(t):
            return M_LAST if t == MT - 1 else P

        def half(p64):
            return slice(0, XD) if p64 == 0 else slice(XD, P)

        def user_before(p, t):
            n = p * MT + t
            if n >= NPB:
                return n - NPB
            return max(m for m in range(2 * MT) if m % NPB == n % NPB) - 2 * MT

        def adds_through(m):
            return m // MT * (MT - 1) + max(m % MT, 1)

        def next_batch(i):
            return (i + 1) // QUADS

        def pack_at(i):
            return i % QUADS

        @block.sync
        def _(sp):
            def handle(i, n, st):
                kind = st[0]
                if kind == "LDC":
                    need(sp, s["ctx_lo_done"], n.of("CX"))
                    sp.dma_start(ctx_raw[:], a["ctxT"][bass.ds(next_batch(i), 1)]
                                 .rearrange("b (k p) m -> p (b k) m", p=P)).then_inc(s["ctx_in"], 16)
                elif kind == "LDA":
                    need(sp, s["wa_lo_done"], n.of("WA"))
                    sp.dma_start(wa_raw[:], a["pack_a"][bass.ds(pack_at(i), 1)].rearrange("b p w -> p (b w)"))\
                        .then_inc(s["wa_in"], 16)
                elif kind == "LDB":
                    need(sp, s["wb_lo_done"], n.of("WB"))
                    sp.dma_start(wb_raw[:], a["pack_b"][bass.ds(pack_at(i), 1)].rearrange("b p w -> p (b w)"))\
                        .then_inc(s["wb_in"], 16)
                elif kind == "X1":
                    if not n.prologue:
                        slot, c = n.job(("K", 1, 3))
                        sp.wait_ge(filled[slot], c)
                    for dst, src in ((xh, x1_hi), (xl, x1_lo)):
                        sp.dma_start(dst[:].bitcast(F32), src[bass.ds(next_batch(i), 1)]
                                     .rearrange("b p k n -> p (b k) n")).then_inc(s["x1_in"], 16)
                elif kind == "K2":
                    p = st[1]
                    if n.prologue:
                        sp.wait_ge(s["ones_set"], 4)
                    sp.wait_ge(s["k_hi_done"], 2 * n.of("K"))
                    for h in range(2):
                        sp.dma_start(k_one[p][half(h), h, :].bitcast(F32), k_two[p][half(h), h, :].bitcast(F32))\
                            .then_inc(s["k_one_in"], 16)

            walk(sp, handle)

        @block.tensor
        def _(pe):
            def take_bank(n):
                r = n.slot()
                need(pe, drained[r], n.of("ring%d" % r))
                return r

            def project(out, terms):
                for q, (w, x) in enumerate(terms):
                    ins = nc.tensor.matmul(out, w, x, start=q == 0, stop=q == len(terms) - 1)
                return ins

            def handle(i, n, st):
                kind = st[0]
                if kind == "S":
                    p, t = st[1:]
                    if t == 0:
                        r, c = n.job(("SH", p))
                        pe.wait_ge(drained[r], c)
                        pe.wait_ge(s["k_one_in"], 32 * n.of("K2"))
                    need(pe, s["exp_done"], n.of("S") - 1)
                    m, ms = rows(t), slice(t * P, t * P + rows(t))
                    for h in range(2):
                        nc.tensor.matmul(ps_s[0:m, t_of(n), h, :], k_two[p][:, h, ms], q_two[p][:, h, :],
                                         start=True, stop=False)
                        ins = nc.tensor.matmul(ps_s[0:m, t_of(n), h, :], k_one[p][:, h, ms], q_low[p][:, h, :],
                                               start=False, stop=True)
                    ins.then_inc(s["scores_ready"], 1)
                elif kind == "PV":
                    p, t = st[1:]
                    if t == 0:
                        need(pe, s["pv_copied"], n.of("COPY"))
                        if p == 0:
                            r, c = n.job(("V", MT - 1))
                            pe.wait_ge(drained[r], c)
                    pe.wait_ge(s["exp_done"], n.of("PV") + 1)
                    m, buf = rows(t), (p * MT + t) % NPB
                    for h in range(2):
                        at = (2 * p + h) * XD
                        ins = nc.tensor.matmul(ps_pv[half(h), :], v[0:m, t, at:at + XD], pexp[0:m, buf, h, :],
                                               start=t == 0, stop=t == MT - 1)
                    ins.then_inc(s["pv_done"], 1)
                elif kind == "K":
                    p, c = st[1:]
                    r = take_bank(n)
                    if c == 0:
                        if p == 0:
                            pe.wait_ge(s["ctx_lo_done"], n.of("CX"))
                            pe.wait_ge(s["wa_lo_done"], n.of("WA"))
                        else:
                            pe.wait_ge(s["wb_lo_done"], n.of("WB"))
                    cols = slice(KC0[c], KC0[c] + CW)
                    terms = [(w_kq(wh, p, 0, k), (ctx_hi if ch else ctx_lo)[:, k, cols])
                             for wh, ch in ((1, 1), (0, 1), (1, 0)) for k in range(EC)]
                    project(ps_ring[:, r, 0:CW], terms).then_inc(filled[r], 1)
                elif kind == "Q":
                    p = st[1]
                    r = take_bank(n)
                    pe.wait_ge(s["x1_in"], 32 * n.of("X1"))
                    terms = [(w_kq(wh, p, 1, k), (xh if ch else xl)[:, k, :])
                             for wh, ch in ((1, 1), (0, 1), (1, 0)) for k in range(EC)]
                    project(ps_ring[:, r, :], terms).then_inc(filled[r], 1)
                elif kind == "MX":
                    p, c, h, q = st[1:]
                    r = take_bank(n)
                    kr, kc = n.job(("K", p, c))
                    pe.wait_ge(drained[kr], kc)
                    if c == 0:
                        qr, qc = n.job(("Q", p))
                        pe.wait_ge(drained[qr], qc)
                    nc.tensor.matmul(ps_ring[:, r, 0:CW], q_two[p][:, h, q * P:(q + 1) * P],
                                     k_two[p][:, h, KC0[c]:KC0[c] + CW], start=True, stop=True)\
                        .then_inc(filled[r], 1)
                elif kind == "SH":
                    r = take_bank(n)
                    pe.wait_ge(s["shift_ready"], 2 * (n.of("SH") + 1))
                    for q in range(NC):
                        ins = nc.tensor.matmul(ps_ring[:, r, q * P:(q + 1) * P], negmax[:, q, :], ident[:],
                                               start=True, stop=True)
                    ins.then_inc(filled[r], 1)
                elif kind == "V":
                    t = st[1]
                    r = take_bank(n)
                    m, ms = rows(t), slice(t * P, t * P + rows(t))
                    terms = [((ctx_hi if ch else ctx_lo)[:, k, ms], w_a(wa_hi if wh else wa_lo, 2, k))
                             for wh, ch in ((1, 1), (0, 1), (1, 0)) for k in range(EC)]
                    project(ps_ring[0:m, r, 0:4 * XD], terms).then_inc(filled[r], 1)
                elif kind == "RS":
                    p = st[1]
                    r = take_bank(n)
                    pe.wait_ge(s["add0_done"], n.of("ADD"))
                    pe.wait_ge(s["add1_done"], n.of("ADD"))
                    for h in range(2):
                        ins = nc.tensor.matmul(ps_ring[half(h), r, :], ones[:, 0:XD], total[p][:, h, :],
                                               start=True, stop=True)
                    ins.then_inc(filled[r], 1)
                elif kind == "OP":
                    p, j = st[1:]
                    r = take_bank(n)
                    pe.wait_ge(s["att_ready"], n.of("R2"))
                    for q in range(2):
                        cs = slice((2 * j + q) * P, (2 * j + q + 1) * P)
                        terms = [(att_hi[:, cs], w_out(wa_hi, p)), (att_lo[:, cs], w_out(wa_hi, p)),
                                 (att_hi[:, cs], w_out(wa_lo, p))]
                        ins = project(ps_ring[:, r, q * E:(q + 1) * E], terms)
                    ins.then_inc(filled[r], 1)

            def t_of(n):
                return n.here.get("S", 0) % 2

            walk(pe, handle)

        @block.scalar
        def _(act):
            def handle(i, n, st):
                kind = st[0]
                if kind == "S":
                    p, t = st[1:]
                    act.wait_ge(s["scores_ready"], n.of("S") + 1)
                    m, buf, prev = rows(t), (p * MT + t) % NPB, user_before(p, t)
                    first = n.before.get("S", 0)
                    need(act, s["pv_done"], first + prev + 1)
                    need(act, s["add0_done"], n.before.get("ADD", 0) + adds_through(prev))
                    need(act, s["add1_done"], n.before.get("ADD", 0) + adds_through(prev))
                    nc.scalar.activation(pexp[0:m, buf], ps_s[0:m, (p * MT + t) % 2], ACT.Exp, scale=XD ** -0.5)\
                        .then_inc(s["exp_done"], 1)
                elif kind == "PV" and st[2] == MT - 1:
                    act.wait_ge(s["pv_done"], n.of("PV") + 1)
                    need(act, s["att_ready"], n.of("R2"))
                    nc.scalar.copy(pv_sb[:], ps_pv[:]).then_inc(s["pv_copied"], 1)
                elif kind == "K":
                    p, c = st[1:]
                    r = n.slot()
                    act.wait_ge(filled[r], n.of("ring%d" % r) + 1)
                    skip = 3 * CW - KC0[3] if c == 3 else 0
                    for h in range(2):
                        nc.scalar.copy(k_two[p][half(h), h, KC0[c] + skip:KC0[c] + CW],
                                       ps_ring[half(h), r, skip:CW]).then_inc(s["k_hi_done"], 1)
                elif kind == "Q":
                    p = st[1]
                    r = n.slot()
                    act.wait_ge(filled[r], n.of("ring%d" % r) + 1)
                    for h in range(2):
                        for to in range(2):
                            nc.scalar.copy(q_two[p][half(to), h, :], ps_ring[half(h), r, :])\
                                .then_inc(s["q_hi_done"], 1)
                elif kind == "RS":
                    r = n.slot()
                    act.wait_ge(filled[r], n.of("ring%d" % r) + 1)
                    need(act, s["att_ready"], n.of("R2"))
                    nc.scalar.copy(sums[:], ps_ring[:, r, :]).then_inc(drained[r], 1)
                elif kind == "R3":
                    act.wait_ge(s["att_done"], n.of("R3") + 1)
                    nc.scalar.copy(att_hi[:], att[:]).then_inc(s["att_hi_done"], 1)
                elif kind == "SH":
                    p = st[1]
                    r = n.slot()
                    act.wait_ge(filled[r], n.of("ring%d" % r) + 1)
                    nc.scalar.copy(q_low[p][half(1), 0, :], ps_ring[half(1), r, :])
                    nc.scalar.copy(q_low[p][half(0), 1, :], ps_ring[half(0), r, :]).then_inc(drained[r], 1)
                elif kind == "V":
                    t = st[1]
                    r = n.slot()
                    act.wait_ge(filled[r], n.of("ring%d" % r) + 1)
                    nc.scalar.copy(v[0:rows(t), t, :], ps_ring[0:rows(t), r, 0:4 * XD]).then_inc(drained[r], 1)
                elif kind == "CX":
                    k = st[1]
                    act.wait_ge(s["ctx_in"], 16 * n.of("LDC"))
                    if k == 0 and not n.prologue:
                        r, c = n.job(("K", 1, 3))
                        act.wait_ge(filled[r], c)
                    nc.scalar.copy(ctx_hi[:, k], ctx_raw[:, k]).then_inc(s["ctx_hi_done"], 1)
                elif kind == "WA":
                    act.wait_ge(s["wa_in"], 16 * n.of("LDA"))
                    nc.scalar.copy(wa_hi[:], wa_raw[:]).then_inc(s["wa_hi_done"], 1)
                elif kind == "WB":
                    act.wait_ge(s["wb_in"], 16 * n.of("LDB"))
                    nc.scalar.copy(wb_hi[:], wb_raw[:]).then_inc(s["wb_hi_done"], 1)

            walk(act, handle)

        def add(eng, n, st, h, sem):
            p, t = st[1:]
            m, buf, b0 = rows(t), (p * MT + t) % NPB, (p * MT) % NPB
            eng.wait_ge(s["exp_done"], n.of("PV") + 1)
            need(eng, sem, n.of("ADD"))
            first = pexp[0:m, b0, h, :] if t == 1 else total[p][0:m, h, :]
            e = nc.vector if h == 0 else nc.gpsimd
            e.tensor_tensor(total[p][0:m, h, :], first, pexp[0:m, buf, h, :], ALU.add).then_inc(sem, 1)

        @block.gpsimd
        def _(pool):
            def handle(i, n, st):
                kind = st[0]
                if kind == "PV" and st[2] >= 1:
                    add(pool, n, st, 1, s["add1_done"])
                elif kind == "R2":
                    done = n.of("R2")
                    pool.wait_ge(s["inv_ready"], n.of("R1"))
                    pool.wait_ge(s["pv_copied"], done + 1)
                    nc.gpsimd.tensor_tensor(att[:], pv_sb[:], inv[:], ALU.mult).then_inc(s["att_done"], 1)
                    pool.wait_ge(s["att_hi_done"], done + 1)
                    nc.gpsimd.tensor_tensor(att_lo[:], att[:], att_hi[:].bitcast(F32), ALU.subtract)\
                        .then_inc(s["att_ready"], 1)
                elif kind == "CX":
                    k = st[1]
                    pool.wait_ge(s["ctx_hi_done"], n.of("CX") + 1)
                    nc.gpsimd.tensor_tensor(ctx_lo[:, k], ctx_raw[:, k], ctx_hi[:, k].bitcast(F32), ALU.subtract)\
                        .then_inc(s["ctx_lo_done"], 1)
                elif kind == "WA":
                    pool.wait_ge(s["wa_hi_done"], n.of("WA") + 1)
                    nc.gpsimd.tensor_tensor(wa_lo[:], wa_raw[:], wa_hi[:].bitcast(F32), ALU.subtract)\
                        .then_inc(s["wa_lo_done"], 1)
                elif kind == "WB":
                    pool.wait_ge(s["wb_hi_done"], n.of("WB") + 1)
                    nc.gpsimd.tensor_tensor(wb_lo[:], wb_raw[:], wb_hi[:].bitcast(F32), ALU.subtract)\
                        .then_inc(s["wb_lo_done"], 1)

            walk(pool, handle)

        @block.vector
        def _(dve):
            nc.vector.memset(negmax[:], 0.0)
            nc.vector.memset(att[:], 1.0).then_inc(s["zero_set"], 1)
            dve.wait_ge(s["zero_set"], 1)
            for p in range(2):
                for h in range(2):
                    nc.vector.tensor_copy(k_one[p][half(1 - h), h, :],
                                          att[half(1 - h), 0:1].broadcast_to([XD, M])).then_inc(s["ones_set"], 1)

            def handle(i, n, st):
                kind = st[0]
                if kind == "PV" and st[2] >= 1:
                    add(dve, n, st, 0, s["add0_done"])
                elif kind == "K":
                    p, c = st[1:]
                    r = n.slot()
                    skip = 3 * CW - KC0[3] if c == 3 else 0
                    cols = slice(KC0[c] + skip, KC0[c] + CW)
                    for h in range(2):
                        dve.wait_ge(s["k_hi_done"], 2 * n.of("K") + h + 1)
                        ins = nc.vector.tensor_tensor(k_two[p][half(1 - h), h, cols], ps_ring[half(h), r, skip:CW],
                                                      k_two[p][half(h), h, cols].bitcast(F32), ALU.subtract)
                    ins.then_inc(drained[r], 1)
                elif kind == "Q":
                    p = st[1]
                    r = n.slot()
                    dve.wait_ge(s["q_hi_done"], 4 * (n.of("Q") + 1))
                    for h in range(2):
                        ins = nc.vector.tensor_tensor(q_low[p][half(h), h, :], ps_ring[half(h), r, :],
                                                      q_two[p][half(h), h, :].bitcast(F32), ALU.subtract)
                    ins.then_inc(drained[r], 1)
                elif kind == "MX":
                    p, c, h, q = st[1:]
                    r = n.slot()
                    dve.wait_ge(filled[r], n.of("ring%d" % r) + 1)
                    nc.vector.tensor_reduce(parts[:, h, q, c:c + 1], ps_ring[:, r, 0:CW], AX.X, ALU.max)\
                        .then_inc(drained[r], 1)
                elif kind == "SH":
                    p = st[1]
                    r, c = n.job(("MX", p, 3, 1, NC - 1))
                    dve.wait_ge(drained[r], c)
                    for h, col in ((0, XD), (1, 0)):
                        nc.vector.tensor_reduce(negmax[:, :, col:col + 1], parts[:, h], AX.X, ALU.max, negate=True)\
                            .then_inc(s["shift_ready"], 1)
                elif kind == "R1":
                    if st[2] == 0:
                        r, c = n.job(("RS", st[1]))
                        dve.wait_ge(drained[r], c)
                        need(dve, s["att_ready"], n.of("R2"))
                    cs = slice(st[2] * N // 2, (st[2] + 1) * N // 2)
                    nc.vector.reciprocal(inv[:, cs], sums[:, cs]).then_inc(s["inv_ready"], 1)
                elif kind == "OP":
                    p, j = st[1:]
                    r = n.slot()
                    dve.wait_ge(filled[r], n.of("ring%d" % r) + 1)
                    xs = X[:, bass.ds(i // QUADS * NC + 2 * j, 2), :].rearrange("p t e -> p (t e)")
                    nc.vector.tensor_tensor(xs, ps_ring[:, r, :], xs, ALU.add).then_inc(drained[r], 1)

            walk(dve, handle)


def expert_round(last):
    steps = [] if last else [("L", 0)]
    after = {1: [("W", 1)] + ([] if last else [("L", 1)]), 5: [] if last else [("W", 0)]}
    for u in range(2 * B):
        steps.append(("H", u))
        if u >= 1:
            steps.append(("Y", u - 1))
            if last and u > B:
                steps.append(("F1", u - 1 - B))
            if last and u > B + 1:
                steps.append(("F2", u - 2 - B))
        steps += after.get(u, [])
    steps.append(("Y", 2 * B - 1))
    if last:
        steps += [("F2", B - 2), ("F1", B - 1), ("F2", B - 1)]
    return steps


def expert_walk(eng, handle):
    ROUNDS = NE // 2

    def run(i, steps, before):
        n = {}
        for st in steps:
            handle(i, lambda k: before.get(k, 0) + n.get(k, 0), st)
            n[st[0]] = n.get(st[0], 0) + 1
        return n

    base = {"W": 1}
    n0 = run(0, expert_round(False), base)

    def before(i):
        return {k: base.get(k, 0) + i * n0.get(k, 0) for k in set(base) | set(n0)}

    with eng.Fori(1, ROUNDS - 1) as i:
        run(i, expert_round(False), before(i))
    run(ROUNDS - 1, expert_round(True), before(ROUNDS - 1))


def experts(nc, a, X, consts, out):
    ident, neghalf = consts["ident"], consts["neghalf"]
    T = B * NC
    with ExitStack() as ctx:
        def sb(name, shape, dt=F32):
            return ctx.enter_context(nc.sbuf_tensor("ex_" + name, shape, dt))

        WW = EC * HID + HC * E
        w_raw = [sb(f"w_raw{p}", [P, WW + HC]) for p in range(2)]
        b1 = [sb(f"b1{p}", [P, HC]) for p in range(2)]
        w_hi = [sb(f"w_hi{p}", [P, WW], F32R) for p in range(2)]
        w_lo = [sb(f"w_lo{p}", [P, WW], F32R) for p in range(2)]
        wg = sb("wg", [P, EC, NE])
        b2 = sb("b2", [NE, E])
        st_ = sb("st", [P, T, 6])
        mv = sb("mv", [P, T, 2])
        rstd = sb("rstd", [P, T])
        xT_hi = sb("xT_hi", [P, EC, B * N], F32R)
        xT_lo = sb("xT_lo", [P, EC, B * N], F32R)
        xT_f = sb("xT_f", [P, 2, EC, P])
        probs = sb("probs", [P, T, NE])
        gred = sb("gred", [P, T])
        top = sb("top", [P, T, 8])
        idx = sb("idx", [P, T, 8], U32)
        idxf = sb("idxf", [P, T, 8])
        norm = sb("norm", [P, T, TOPK])
        iota = sb("iota", [P, NE])
        hot = sb("hot", [P, T, NE])
        score = sb("score", [P, T, NE])
        scoreT = sb("scoreT", [NE, T, P])
        h_f = sb("h_f", [P, 2, N])
        h_hi = sb("h_hi", [P, 2, HC, N], F32R)
        h_lo = sb("h_lo", [P, 2, HC, N], F32R)

        ps_h = ctx.enter_context(nc.psum_tensor("ps_h", [P, 4, 512], F32))
        ps_y = ctx.enter_context(nc.psum_tensor("ps_y", [P, 2, 512], F32))
        ps_t = ctx.enter_context(nc.psum_tensor("ps_t", [P, 512], F32))
        ps_g = ctx.enter_context(nc.psum_tensor("ps_g", [P, 512], F32))

        s = sems(ctx, nc, "const_in w_in0 w_in1 w_hi_done w_lo_done var_ready rstd_half rstd_ready x_done xT_tr "
                          "xT_hi_done xT_lo_done gate_mm gate_sub gate_exp score_done score_tr scoreT_done b2_mm b2_added "
                          "h_mm h_act h_lo_done y_mm y_added step fstep fvar frstd_half frstd fdone stored")
        w_in = [s["w_in0"], s["w_in1"]]
        block = ctx.enter_context(nc.Block())
        pack = a["pack_e"]

        def w1(w, k, c):
            return w[:, k * HID + c * P:k * HID + (c + 1) * P]

        def w2(w, c):
            return w[:, EC * HID + c * E:EC * HID + (c + 1) * E]

        @block.sync
        def _(sp):
            for dst, src in ((wg[:], a["Wg"].rearrange("(k p) e -> p k e", p=P)), (b2[:], a["b2"])):
                sp.dma_start(dst, src).then_inc(s["const_in"], 16)
            for p in range(2):
                sp.dma_start(w_raw[p][:], pack[p]).then_inc(w_in[p], 16)

            def handle(i, n, st):
                if st[0] == "L":
                    p = st[1]
                    sp.wait_ge(s["w_lo_done"], n("W"))
                    sp.dma_start(w_raw[p][:], pack[bass.ds(2 * i + 2 + p, 1)].rearrange("e p w -> p (e w)"))\
                        .then_inc(w_in[p], 16)
                elif st[0] == "F2":
                    b = st[1]
                    sp.wait_ge(s["fdone"], NC * (b + 1))
                    sp.dma_start(out[b].rearrange("(t p) e -> p t e", p=P), X[:, NC * b:NC * (b + 1), :])\
                        .then_inc(s["stored"], 16)

            expert_walk(sp, handle)
            sp.wait_ge(s["stored"], 16 * B)

        @block.gpsimd
        def _(pool):
            for b in range(B):
                pool.wait_ge(s["var_ready"], b + 1)
                r = slice(NC * b, NC * (b + 1))
                nc.gpsimd.tensor_scalar(rstd[:, r], mv[:, r, 1], EPS, None, ALU.add).then_inc(s["rstd_half"], 1)
                pool.wait_ge(s["rstd_half"], b + 1)
                nc.gpsimd.tensor_tensor(rstd[:, r], rstd[:, r], neghalf[:, 0:NC], ALU.pow)\
                    .then_inc(s["rstd_ready"], 1)

            def split(p, k):
                pool.wait_ge(s["w_hi_done"], k)
                nc.gpsimd.tensor_tensor(w_lo[p][:], w_raw[p][:, 0:WW], w_hi[p][:].bitcast(F32), ALU.subtract)\
                    .then_inc(s["w_lo_done"], 1)

            split(0, 1)

            def handle(i, n, st):
                if st[0] == "W":
                    split(st[1], n("W") + 1)
                elif st[0] == "F1":
                    b = st[1]
                    pool.wait_ge(s["fvar"], b + 1)
                    r = slice(NC * b, NC * (b + 1))
                    nc.gpsimd.tensor_scalar(rstd[:, r], mv[:, r, 1], EPS, None, ALU.add).then_inc(s["frstd_half"], 1)
                    pool.wait_ge(s["frstd_half"], b + 1)
                    nc.gpsimd.tensor_tensor(rstd[:, r], rstd[:, r], neghalf[:, 0:NC], ALU.pow)\
                        .then_inc(s["frstd"], 1)

            expert_walk(pool, handle)

        @block.tensor
        def _(pe):
            pe.wait_ge(s["const_in"], 32)

            def gate(t):
                pe.wait_ge(s["xT_hi_done"], t + 1)
                for k in range(EC):
                    ins = nc.tensor.matmul(ps_g[:, t * NE:(t + 1) * NE], xT_f[:, t % 2, k], wg[:, k],
                                           start=k == 0, stop=k == EC - 1)
                ins.then_inc(s["gate_mm"], 1)

            for t in range(T):
                pe.wait_ge(s["x_done"], t + 1)
                need(pe, s["xT_lo_done"], t)
                for k in range(EC):
                    ins = nc.tensor.transpose(ps_t[:, k * P:(k + 1) * P], X[:, t, k * P:(k + 1) * P], ident[:])
                ins.then_inc(s["xT_tr"], 1)
                if t >= 1:
                    gate(t - 1)
            gate(T - 1)
            pe.wait_ge(s["score_done"], 1)
            for q in range(T // 4):
                for t in range(4):
                    ins = nc.tensor.transpose(ps_h[0:NE, q, t * P:(t + 1) * P], score[:, 4 * q + t, :], ident[:])
                ins.then_inc(s["score_tr"], 1)
            for j in range(T // 2):
                pe.wait_ge(s["scoreT_done"], j // 2 + 1)
                need(pe, s["b2_added"], j - 1)
                for q in range(2):
                    ins = nc.tensor.matmul(ps_y[:, j % 2, q * E:(q + 1) * E], scoreT[:, 2 * j + q, :], b2[:],
                                           start=True, stop=True)
                ins.then_inc(s["b2_mm"], 1)

            def handle(i, n, st):
                kind = st[0]
                if kind == "H":
                    u = st[1]
                    p, rows = u // B, slice(u % B * N, (u % B + 1) * N)
                    if u % B == 0:
                        pe.wait_ge(s["w_lo_done"], n("W"))
                    for c in range(HC):
                        need(pe, s["h_act"], HC * (n("H") - 1) + c + 1)
                        terms = [(w1(w_hi[p], k, c), xT_hi[:, k, rows]) for k in range(EC)] \
                            + [(w1(w_hi[p], k, c), xT_lo[:, k, rows]) for k in range(EC)] \
                            + [(w1(w_lo[p], k, c), xT_hi[:, k, rows]) for k in range(EC)]
                        for q, (w, x) in enumerate(terms):
                            ins = nc.tensor.matmul(ps_h[:, c, :], w, x, start=q == 0, stop=q == len(terms) - 1)
                        ins.then_inc(s["h_mm"], 1)
                elif kind == "Y":
                    u = st[1]
                    p = u // B
                    pe.wait_ge(s["h_lo_done"], HC * (n("Y") + 1))
                    for j in range(2):
                        need(pe, s["y_added"], 2 * n("Y") + j - 1)
                        for q in range(2):
                            cs = slice((2 * j + q) * P, (2 * j + q + 1) * P)
                            terms = [(h_hi[:, u % 2, c, cs], w2(w_hi[p], c)) for c in range(HC)] \
                                + [(h_lo[:, u % 2, c, cs], w2(w_hi[p], c)) for c in range(HC)] \
                                + [(h_hi[:, u % 2, c, cs], w2(w_lo[p], c)) for c in range(HC)]
                            for m, (h, w) in enumerate(terms):
                                ins = nc.tensor.matmul(ps_y[:, j, q * E:(q + 1) * E], h, w,
                                                       start=m == 0, stop=m == len(terms) - 1)
                        ins.then_inc(s["y_mm"], 1)

            pe.wait_ge(s["b2_added"], T // 2)
            expert_walk(pe, handle)

        @block.scalar
        def _(act):
            act.wait_ge(w_in[0], 16)
            nc.scalar.copy(b1[0][:], w_raw[0][:, WW:WW + HC])
            nc.scalar.copy(w_hi[0][:], w_raw[0][:, 0:WW]).then_inc(s["w_hi_done"], 1)
            for t in range(T):
                act.wait_ge(s["xT_tr"], t + 1)
                need(act, s["gate_mm"], t - 1)
                src = ps_t[:, 0:E].rearrange("p (k n) -> p k n", k=EC)
                nc.scalar.copy(xT_f[:, t % 2], src)
                nc.scalar.copy(xT_hi[:, :, t * P:(t + 1) * P], src).then_inc(s["xT_hi_done"], 1)
            act.wait_ge(s["gate_sub"], 1)
            nc.scalar.activation(probs[:], probs[:], ACT.Exp).then_inc(s["gate_exp"], 1)
            for q in range(T // 4):
                act.wait_ge(s["score_tr"], q + 1)
                nc.scalar.copy(scoreT[:, 4 * q:4 * q + 4, :], ps_h[0:NE, q, :].rearrange("e (t p) -> e t p", t=4))\
                    .then_inc(s["scoreT_done"], 1)

            def handle(i, n, st):
                kind = st[0]
                if kind == "H":
                    u = st[1]
                    if u % B == 0:
                        act.wait_ge(s["w_hi_done"], n("W"))
                    for c in range(HC):
                        act.wait_ge(s["h_mm"], HC * n("H") + c + 1)
                        need(act, s["h_lo_done"], HC * n("H") + c - 1)
                        if c == 0:
                            need(act, s["y_mm"], 2 * (n("H") - 1))
                        bias = b1[u // B][:, c:c + 1]
                        nc.scalar.activation(h_f[:, c % 2], ps_h[:, c, :], ACT.Relu, bias=bias)
                        nc.scalar.activation(h_hi[:, u % 2, c], ps_h[:, c, :], ACT.Relu, bias=bias)\
                            .then_inc(s["h_act"], 1)
                elif kind == "W":
                    p = st[1]
                    act.wait_ge(w_in[p], 16 * (i + (2 if p == 0 else 1)))
                    need(act, s["y_mm"], 2 * (n("Y") - 1))
                    nc.scalar.copy(b1[p][:], w_raw[p][:, WW:WW + HC])
                    nc.scalar.copy(w_hi[p][:], w_raw[p][:, 0:WW]).then_inc(s["w_hi_done"], 1)

            expert_walk(act, handle)

        @block.vector
        def _(dve):
            done = [0]

            def link(ins):
                done[0] += 1
                ins.then_inc(s["step"], 1)
                dve.wait_ge(s["step"], done[0])

            for e in range(NE):
                nc.vector.memset(iota[:, e:e + 1], float(e))

            def statistics(t0, sem):
                for t in range(t0, t0 + NC):
                    ins = nc.vector.bn_stats(st_[:, t], X[:, t])
                link(ins)
                for t in range(t0, t0 + NC):
                    ins = nc.vector.bn_aggr(mv[:, t], st_[:, t])
                ins.then_inc(sem, 1)

            def normalise(t0, sem):
                for t in range(t0, t0 + NC):
                    nc.vector.tensor_scalar(X[:, t], X[:, t], mv[:, t, 0:1], rstd[:, t:t + 1],
                                            ALU.subtract, ALU.mult).then_inc(sem, 1)

            def take_rows(b):
                for t in range(NC * b, NC * (b + 1)):
                    dve.wait_ge(s["xT_hi_done"], t + 1)
                    nc.vector.tensor_tensor(xT_lo[:, :, t * P:(t + 1) * P],
                                            ps_t[:, 0:E].rearrange("p (k n) -> p k n", k=EC),
                                            xT_hi[:, :, t * P:(t + 1) * P].bitcast(F32), ALU.subtract)\
                        .then_inc(s["xT_lo_done"], 1)

            statistics(0, s["var_ready"])
            for b in range(B):
                if b + 1 < B:
                    statistics(NC * (b + 1), s["var_ready"])
                dve.wait_ge(s["rstd_ready"], b + 1)
                normalise(NC * b, s["x_done"])
                take_rows(b)

            def over_experts(x):
                return x.unsqueeze(2).broadcast_to([P, T, NE])

            dve.wait_ge(s["gate_mm"], T)
            logits = ps_g[:, 0:T * NE].rearrange("p (t e) -> p t e", e=NE)
            link(nc.vector.tensor_reduce(gred[:], logits, AX.X, ALU.max))
            nc.vector.tensor_tensor(probs[:], logits, over_experts(gred[:]), ALU.subtract).then_inc(s["gate_sub"], 1)
            dve.wait_ge(s["gate_exp"], 1)
            link(nc.vector.tensor_reduce(gred[:], probs[:], AX.X, ALU.add))
            link(nc.vector.reciprocal(gred[:], gred[:]))
            link(nc.vector.tensor_tensor(probs[:], probs[:], over_experts(gred[:]), ALU.mult))
            for t in range(T):
                ins = nc.vector.max(top[:, t], probs[:, t])
            link(ins)
            for t in range(T):
                ins = nc.vector.max_index(idx[:, t], top[:, t], probs[:, t])
            link(ins)
            nc.vector.tensor_copy(idxf[:], idx[:])
            link(nc.vector.tensor_tensor(gred[:], top[:, :, 0], top[:, :, 1], ALU.add))
            link(nc.vector.reciprocal(gred[:], gred[:]))
            link(nc.vector.tensor_tensor(norm[:], top[:, :, 0:TOPK], gred[:].unsqueeze(2).broadcast_to([P, T, TOPK]),
                                         ALU.mult))
            for j in range(TOPK):
                dst = score if j == 0 else hot
                link(nc.vector.tensor_tensor(dst[:], iota[:].unsqueeze(1).broadcast_to([P, T, NE]),
                                             over_experts(idxf[:, :, j]), ALU.is_equal))
                link(nc.vector.tensor_tensor(dst[:], dst[:], over_experts(norm[:, :, j]), ALU.mult))
            nc.vector.tensor_tensor(score[:], score[:], hot[:], ALU.add).then_inc(s["score_done"], 1)
            for j in range(T // 2):
                dve.wait_ge(s["b2_mm"], j + 1)
                xs = X[:, 2 * j:2 * j + 2, :].rearrange("p t e -> p (t e)")
                nc.vector.tensor_tensor(xs, ps_y[:, j % 2, :], xs, ALU.add).then_inc(s["b2_added"], 1)

            def handle(i, n, st):
                kind = st[0]
                if kind == "H":
                    u = st[1]
                    for c in range(HC):
                        dve.wait_ge(s["h_act"], HC * n("H") + c + 1)
                        nc.vector.tensor_tensor(h_lo[:, u % 2, c], h_f[:, c % 2], h_hi[:, u % 2, c].bitcast(F32),
                                                ALU.subtract).then_inc(s["h_lo_done"], 1)
                elif kind == "Y":
                    u = st[1]
                    for j in range(2):
                        dve.wait_ge(s["y_mm"], 2 * n("Y") + j + 1)
                        for q in range(2):
                            t = u % B * NC + 2 * j + q
                            ins = nc.vector.scalar_tensor_tensor(
                                out=X[:, t], in0=ps_y[:, j, q * E:(q + 1) * E],
                                scalar=score[:, t, bass.ds(2 * i + u // B, 1)], in1=X[:, t],
                                op0=ALU.mult, op1=ALU.add)
                        ins.then_inc(s["y_added"], 1)
                elif kind == "F1":
                    dve.wait_ge(s["y_added"], 2 * n("Y"))
                    statistics(NC * st[1], s["fvar"])
                elif kind == "F2":
                    dve.wait_ge(s["frstd"], st[1] + 1)
                    normalise(NC * st[1], s["fdone"])

            expert_walk(dve, handle)


def build(nc, a, out):
    with ExitStack() as ctx:
        X = ctx.enter_context(nc.sbuf_tensor("X", [P, B * NC, E], F32))
        consts = {n: ctx.enter_context(nc.sbuf_tensor(n, [P, P], F32)) for n in ("ident", "ones", "neghalf")}
        x1_hi = nc.dram_tensor("x1_hi", [B, P, EC, N], F32, kind="Internal").ap()
        x1_lo = nc.dram_tensor("x1_lo", [B, P, EC, N], F32, kind="Internal").ap()
        self_attention(nc, a, X, consts, x1_hi, x1_lo)
        cross_attention(nc, a, X, consts, x1_hi, x1_lo)
        experts(nc, a, X, consts, out)

def layout(i):
    import numpy as np

    f = {k: np.asarray(v) for k, v in i.items()}
    q, k = f["L0_xattn_w_q"], f["L0_xattn_w_kv"][:, :XH * XD]
    v, o = f["L0_xattn_w_kv"][:, XH * XD:], f["L0_xattn_w_out"]

    def cols(w, quad, pair=None):
        lo = quad * 4 * XD if pair is None else (quad * 2 + pair) * 2 * XD
        w = w[:, lo:lo + (4 if pair is None else 2) * XD]
        return w.reshape(EC, P, -1).transpose(1, 0, 2).reshape(P, -1)

    def rows(quad, pair):
        return o[(quad * 2 + pair) * P:(quad * 2 + pair + 1) * P]

    nxt = [(j + 1) % QUADS for j in range(QUADS)]
    pack_a = np.stack([np.concatenate([cols(k, n, 0), cols(q, n, 0), cols(v, n), rows(j, 0), rows(j, 1)], 1)
                       for j, n in enumerate(nxt)])
    pack_b = np.stack([np.concatenate([cols(k, n, 1), cols(q, n, 1)], 1) for n in nxt])
    w1, w2 = f["L0_ffn_W1"], f["L0_ffn_W2"]
    pack_e = np.concatenate([w1.reshape(NE, EC, P, HID).transpose(0, 2, 1, 3).reshape(NE, P, -1),
                             w2.reshape(NE, HC, P, E).transpose(0, 2, 1, 3).reshape(NE, P, -1),
                             f["L0_ffn_b1"].reshape(NE, HC, P).transpose(0, 2, 1)], 2)
    x = f["x"].reshape(B * N, E)
    return {
        "x": x, "xT": x.T, "ctxT": f["ctx_1024"].transpose(0, 2, 1),
        "w_inT": f["L0_attn_in_proj_w"].T, "w_v": f["L0_attn_in_proj_w"][2 * E:], "dynT": f["L0_attn_dyn_w"].T,
        "b_in": f["L0_attn_in_proj_b"][None], "b_v": f["L0_attn_in_proj_b"][2 * E:].reshape(EC, P).T,
        "b_dyn": f["L0_attn_dyn_b"][None], "w_oT": f["L0_attn_out_proj_w"].T, "b_o": f["L0_attn_out_proj_b"][None],
        "b_xo": f["L0_xattn_b_out"][None], "pack_a": pack_a, "pack_b": pack_b,
        "Wg": f["L0_ffn_Wg"], "pack_e": pack_e,
        "b2": f["L0_ffn_b2"],
    }


def kernel(**inputs):
    import concourse.bacc as bacc
    import numpy as np
    from concourse.bass_utils import run_bass_kernel_spmd

    nc = bacc.Bacc("TRN2", target_bir_lowering=False, num_devices=1)
    arrays, a = {}, {}
    for name, v in layout(inputs).items():
        v = np.ascontiguousarray(v)
        arrays["in_" + name] = v
        a[name] = nc.dram_tensor("in_" + name, v.shape, mybir.dt.from_np(v.dtype), kind="ExternalInput").ap()
    out = nc.dram_tensor("out", (B, N, E), F32, kind="ExternalOutput").ap()
    build(nc, a, out)
    r = run_bass_kernel_spmd(nc, [arrays], core_ids=[0])
    return r.results[0]["out"]
```

```python
from contextlib import ExitStack

import concourse.bass as bass
from concourse import mybir

P = 128
F32 = mybir.dt.float32
F32R = mybir.dt.float32r
U32 = mybir.dt.uint32
ALU = mybir.AluOpType
ACT = mybir.ActivationFunctionType
AX = mybir.AxisListType

B, N, E = 4, 512, 256
EC = E // P
NC = N // P
M = 1601
SH_, SD = 16, 16
TAPS, PAD_L = 15, 7
XH, XD = 16, 64
PAIRS = XH // 2
QUADS = XH // 4
MT = (M + P - 1) // P
M_LAST = M - (MT - 1) * P
CW = 402
KC0 = [0, CW, 2 * CW, M - CW]
NE, HID, TOPK = 8, 512, 2
HC = HID // P
QKV = 3 * E
DYN = SH_ * TAPS
ALLW = QKV + DYN
HALF = ALLW // 2
EPS = 1e-5


def sems(ctx, nc, names):
    return {n: ctx.enter_context(nc.semaphore(n)) for n in names.split()}


def need(eng, sem, value):
    if not isinstance(value, int) or value > 0:
        eng.wait_ge(sem, value)


def self_attention(nc, a, X, consts, loads, x1_hi, x1_lo):
    ident, ones, neghalf = consts["ident"], consts["ones"], consts["neghalf"]
    with ExitStack() as ctx:
        def sb(name, shape, dt=F32):
            return ctx.enter_context(nc.sbuf_tensor("sa_" + name, shape, dt))

        w_raw = sb("w_raw", [P, EC, ALLW])
        w_hi = sb("w_hi", [P, EC, ALLW], F32R)
        w_lo = sb("w_lo", [P, EC, ALLW], F32R)
        wv_nat = sb("wv_nat", [P, EC, E])
        dynT = sb("dynT", [P, EC, DYN])
        bv_col = sb("bv_col", [P, EC])
        bv_wide = sb("bv_wide", [P, EC, P])
        bias = sb("bias", [P, ALLW])
        wo_raw = sb("wo_raw", [P, 2 * EC, E])
        wo_hi = sb("wo_hi", [P, 2 * EC, E], F32R)
        wo_lo = sb("wo_lo", [P, 2 * EC, E], F32R)
        bo = sb("bo", [P, E])
        sel_raw, sel = sb("sel_raw", [P, P]), sb("sel", [P, P], F32R)
        bias2, bo2 = sb("bias2", [P, ALLW], F32R), sb("bo2", [P, E], F32R)
        xT = sb("xT", [P, 2, EC, B, P])
        xT_hi = sb("xT_hi", [P, 2, EC, B, P], F32R)
        xT_lo = sb("xT_lo", [P, 2, EC, B, P], F32R)
        qkv = sb("qkv", [P, 2, B, ALLW])
        prod = sb("prod", [P, B, B * E])
        sc = sb("sc", [P, B, B, SH_])
        mx = sb("mx", [P, B, SH_])
        den = sb("den", [P, B, SH_])
        tap = sb("tap", [P, B, SH_, TAPS])
        tmx = sb("tmx", [P, B, SH_])
        tden = sb("tden", [P, B, SH_])
        cprod = sb("cprod", [P, B, E])
        csum = sb("csum", [P, 2, E])
        cat = sb("cat", [P, B, 2 * E])
        cat_hi = sb("cat_hi", [P, 2, 2 * E], F32R)
        cat_lo = sb("cat_lo", [P, 2, 2 * E], F32R)
        y = sb("y", [P, B, E])
        st = sb("st", [P, B, 6])
        mv = sb("mv", [P, B, 2])
        rstd = sb("rstd", [P, B])
        x1s_hi = sb("x1s_hi", [P, 2, EC, P], F32R)
        x1s_lo = sb("x1s_lo", [P, 2, EC, P], F32R)
        xbo = sb("xbo", [P, E])

        ps_qkv = ctx.enter_context(nc.psum_tensor("ps_qkv", [P, 2, 2, 512], F32))
        ps_cat = ctx.enter_context(nc.psum_tensor("ps_cat", [P, 2, 512], F32))
        ps_out = ctx.enter_context(nc.psum_tensor("ps_out", [P, 512], F32))
        ps_x1 = ctx.enter_context(nc.psum_tensor("ps_x1", [P, 512], F32))

        s = sems(ctx, nc, "fold_in w_in b_in wo_in res_in x_in0 x_in1 const_ready fold_mm fold_evac w_hi_done w_lo_done x_hi_done x_lo_done "
                          "qkv_mm qkv_ready score_sub score_exp tap_max tap_sub tap_exp tap_inv tap_w conv_step "
                          "conv_done attn_done cat_tr cat_hi_done cat_lo_done out_mm var_ready rstd_half rstd_done bias_hi bias_ready bo_ready "
                          "x1_done y_ready x1_tr x1_hi_done x1_lo_done x1_out0 x1_out1 step pstep")
        x_in = [s["x_in0"], s["x_in1"]]
        x1_out = [s["x1_out0"], s["x1_out1"]]
        block = ctx.enter_context(nc.Block())

        RSTD_AT = 2

        def run(steps, order):
            for c in range(NC + 2):
                for name in order.split():
                    step, d = steps[name[0]]
                    if (0 if d < 1 else 1) <= c + d < NC:
                        if len(name) > 1:
                            step(c + d, int(name[1:]))
                        else:
                            step(c + d)

        @block.sync
        def _(sp):
            sp.dma_start(wv_nat[:], a["w_v"].rearrange("(k p) n -> p k n", p=P)).then_inc(s["fold_in"], 16)
            sp.dma_start(dynT[:], a["dynT"].rearrange("(k p) n -> p k n", p=P)).then_inc(s["fold_in"], 16)
            sp.dma_start(bv_col[:], a["b_v"]).then_inc(s["fold_in"], 16)
            sp.dma_start(w_raw[:, :, 0:QKV], a["w_inT"].rearrange("(k p) n -> p k n", p=P)).then_inc(s["w_in"], 16)
            for c in range(NC):
                for k in range(EC):
                    if c >= 2 and k == 0:
                        sp.wait_ge(s["x_lo_done"], c - 1)
                    src = a["xT"].rearrange("(k p) (t c n) -> p k t c n", p=P, t=B, c=NC)[:, k, :, c, :]
                    sp.dma_start(xT[:, c % 2, k], src).then_inc(x_in[c % 2], 16)
                if c == 0:
                    sp.dma_start(bias[:, 0:QKV], a["b_in"].broadcast_to([P, QKV])).then_inc(s["b_in"], 16)
                    sp.dma_start(bias[:, QKV:ALLW], a["b_dyn"].broadcast_to([P, DYN])).then_inc(s["b_in"], 16)
                    sp.dma_start(X[:], a["x"].rearrange("(t p) e -> p t e", p=P)).then_inc(s["res_in"], 16)
                    sp.dma_start(bo[:], a["b_o"].broadcast_to([P, E])).then_inc(s["res_in"], 16)
                    sp.dma_start(xbo[:], a["b_xo"].broadcast_to([P, E])).then_inc(s["res_in"], 16)
                    sp.dma_start(wo_raw[:], a["w_oT"].rearrange("(k p) n -> p k n", p=P)).then_inc(s["wo_in"], 16)
            loads.start(sp, a)
            for n in range(NC * B):
                c, t = n // B, n % B
                sp.wait_ge(s["x1_hi_done"], n + 1)
                sp.dma_start(x1_hi[t][:, :, c * P:(c + 1) * P], x1s_hi[:, n % 2].bitcast(F32)).then_inc(x1_out[n % 2], 16)
                sp.wait_ge(s["x1_lo_done"], n + 1)
                sp.dma_start(x1_lo[t][:, :, c * P:(c + 1) * P], x1s_lo[:, n % 2].bitcast(F32)).then_inc(x1_out[n % 2], 16)
            for q in x1_out:
                sp.wait_ge(q, 16 * NC * B)


        @block.gpsimd
        def _(pool):
            pool.memset(ones[:], 1.0)
            pool.memset(neghalf[:], -0.5)
            pool.memset(ident[:], 0.0).then_inc(s["pstep"], 1)
            pool.wait_ge(s["pstep"], 1)
            nc.gpsimd.affine_select(out=ident[:], in_=ident[:], compare_op=ALU.not_equal, fill=1.0, base=0,
                                    pattern=[[-1, P]], channel_multiplier=1).then_inc(s["const_ready"], 1)

            def split_x(c):
                pool.wait_ge(s["x_hi_done"], c + 1)
                nc.gpsimd.tensor_tensor(xT_lo[:, c % 2], xT[:, c % 2], xT_hi[:, c % 2].bitcast(F32),
                                        ALU.subtract).then_inc(s["x_lo_done"], 1)

            def conv(c, t):
                w = tap[:, t, :, PAD_L - t:PAD_L - t + B].rearrange("p h i -> p i h")
                for i in range(B):
                    ins = nc.gpsimd.tensor_tensor(
                        cprod[:, i].rearrange("p (h d) -> p h d", d=SD),
                        qkv[:, c % 2, i, 2 * E:3 * E].rearrange("p (h d) -> p h d", d=SD),
                        w[:, i].unsqueeze(2).broadcast_to([P, SH_, SD]), ALU.mult)
                ins.then_inc(s["conv_step"], 1)
                k = 3 * (B * c + t)
                pool.wait_ge(s["conv_step"], k + 1)
                nc.gpsimd.tensor_tensor(csum[:], cprod[:, 0:2], cprod[:, 2:4], ALU.add).then_inc(s["conv_step"], 1)
                pool.wait_ge(s["conv_step"], k + 2)
                need(pool, s["cat_tr"], B * (c - 1) + t + 1)
                nc.gpsimd.tensor_tensor(cat[:, t, E:2 * E], csum[:, 0], csum[:, 1],
                                        ALU.add).then_inc(s["conv_step"], 1)
                pool.wait_ge(s["conv_step"], k + 3)

            def deviation(c):
                pool.wait_ge(s["var_ready"], c + 1)
                nc.gpsimd.tensor_scalar(rstd[:], mv[:, :, 1], EPS, None, ALU.add).then_inc(s["rstd_half"], 1)
                pool.wait_ge(s["rstd_half"], c + 1)
                nc.gpsimd.tensor_tensor(rstd[:], rstd[:], neghalf[:, 0:B], ALU.pow).then_inc(s["rstd_done"], 1)

            def add_output_bias(c):
                for t in range(B):
                    pool.wait_ge(s["x1_tr"], B * c + t + 1)
                    nc.gpsimd.tensor_tensor(X[:, t * NC + c], X[:, t * NC + c], xbo[:], ALU.add)

            split_x(0)
            split_x(1)
            for c in range(NC):
                logits = qkv[:, c % 2, :, QKV:ALLW].rearrange("p t (h k) -> p t h k", k=TAPS)
                pool.wait_ge(s["tap_max"], c + 1)
                for t in range(B):
                    ins = nc.gpsimd.tensor_tensor(tap[:, t], logits[:, t],
                                                  tmx[:, t].unsqueeze(2).broadcast_to([P, SH_, TAPS]), ALU.subtract)
                ins.then_inc(s["tap_sub"], 1)
                pool.wait_ge(s["tap_inv"], c + 1)
                for t in range(B):
                    ins = nc.gpsimd.tensor_tensor(tap[:, t], tap[:, t],
                                                  tden[:, t].unsqueeze(2).broadcast_to([P, SH_, TAPS]), ALU.mult)
                ins.then_inc(s["tap_w"], 1)
                pool.wait_ge(s["tap_w"], c + 1)
                for t in range(B):
                    conv(c, t)
                    if t == 1 and c + 2 < NC:
                        split_x(c + 2)
                    if t == RSTD_AT and c >= 1:
                        deviation(c - 1)
                if c >= 2:
                    add_output_bias(c - 2)
            deviation(NC - 1)
            add_output_bias(NC - 2)
            add_output_bias(NC - 1)

        @block.tensor
        def _(pe):
            pe.wait_ge(s["fold_in"], 48)
            for kc in range(EC):
                for ec in range(EC):
                    ins = nc.tensor.matmul(ps_qkv[:, 0, kc, 0:DYN], wv_nat[:, ec, kc * P:(kc + 1) * P], dynT[:, ec],
                                           start=ec == 0, stop=ec == EC - 1)
            ins.then_inc(s["fold_mm"], 1)
            pe.wait_ge(s["step"], 3)
            for ec in range(EC):
                ins = nc.tensor.matmul(ps_qkv[:, 1, 0, 0:DYN], bv_wide[:, ec], dynT[:, ec],
                                       start=ec == 0, stop=ec == EC - 1)
            ins.then_inc(s["fold_mm"], 1)

            def project(c, t):
                if t == 0:
                    pe.wait_ge(s["x_lo_done" if c > 0 else "x_hi_done"], c + 1)
                n = B * c + t
                for h in range(2):
                    if n < 2:
                        pe.wait_ge(s["fold_evac"], 2)
                        pe.wait_ge(s["w_hi_done"], h + 1)
                    else:
                        pe.wait_ge(s["qkv_ready"], 2 * (n - 2) + h + 1)
                    for q, (xx, ww) in enumerate(((xT_hi, w_hi), (xT_lo, w_hi), (xT_hi, w_lo))):
                        if n < 2 and q == 1:
                            pe.wait_ge(s["x_lo_done"], c + 1)
                        if n < 2 and q == 2:
                            pe.wait_ge(s["w_lo_done"], h + 1)
                        for k in range(EC):
                            nc.tensor.matmul(ps_qkv[:, n % 2, h, 0:HALF], xx[:, c % 2, k, t],
                                                   ww[:, k, h * HALF:(h + 1) * HALF],
                                                   start=q == 0 and k == 0, stop=False)
                    if n < 2:
                        pe.wait_ge(s["bias_ready"], 1)
                    nc.tensor.matmul(ps_qkv[:, n % 2, h, 0:HALF], sel[:], bias2[:, h * HALF:(h + 1) * HALF],
                                     start=False, stop=True).then_inc(s["qkv_mm"], 1)

            def turn_cat(c, t):
                n = B * c + t
                if t == 0:
                    pe.wait_ge(s["attn_done"], c + 1)
                    if c == 0:
                        pe.wait_ge(s["const_ready"], 1)
                pe.wait_ge(s["conv_step"], 3 * (n + 1))
                if n >= 2:
                    pe.wait_ge(s["cat_lo_done"], n - 1)
                for j in range(2 * EC):
                    ins = nc.tensor.transpose(ps_cat[:, n % 2, j * P:(j + 1) * P], cat[:, t, j * P:(j + 1) * P],
                                              ident[:])
                ins.then_inc(s["cat_tr"], 1)

            def project_out(c, t):
                n = B * c + t
                if n == 0:
                    pe.wait_ge(s["w_lo_done"], 3)
                    pe.wait_ge(s["bo_ready"], 1)
                pe.wait_ge(s["cat_lo_done"], n + 1)
                need(pe, s["y_ready"], n)
                for q, (cc, ww) in enumerate(((cat_hi, wo_hi), (cat_lo, wo_hi), (cat_hi, wo_lo))):
                    for j in range(2 * EC):
                        ins = nc.tensor.matmul(ps_out[:, 0:E], cc[:, n % 2, j * P:(j + 1) * P], ww[:, j],
                                               start=q == 0 and j == 0, stop=False)
                nc.tensor.matmul(ps_out[:, 0:E], sel[:], bo2[:], start=False, stop=True).then_inc(s["out_mm"], 1)

            def turn_x1(c, t):
                n = B * c + t
                pe.wait_ge(s["x1_done"], n + 1)
                need(pe, s["x1_lo_done"], n)
                for k in range(EC):
                    ins = nc.tensor.transpose(ps_x1[:, k * P:(k + 1) * P], X[:, t * NC + c, k * P:(k + 1) * P],
                                              ident[:])
                ins.then_inc(s["x1_tr"], 1)

            steps = dict(P=(project, 1), C=(turn_cat, -1), O=(project_out, -1), X=(turn_x1, -2))
            for t in range(B):
                project(0, t)
            run(steps, "C0 X0 C1 P0 X1 O0 C2 P1 P2 X2 O1 C3 X3 O2 O3 P3")

        @block.scalar
        def _(act):
            def split_x(c):
                act.wait_ge(x_in[c % 2], 16 * EC * (c // 2 + 1))
                if c >= 2:
                    act.wait_ge(s["qkv_mm"], 2 * B * (c - 1))
                nc.scalar.copy(xT_hi[:, c % 2], xT[:, c % 2]).then_inc(s["x_hi_done"], 1)

            def exp_taps(c):
                act.wait_ge(s["tap_sub"], c + 1)
                nc.scalar.activation(tap[:], tap[:], ACT.Exp).then_inc(s["tap_exp"], 1)

            def exp_scores(c):
                act.wait_ge(s["score_sub"], c + 1)
                nc.scalar.activation(sc[:], sc[:], ACT.Exp, scale=SD ** -0.5).then_inc(s["score_exp"], 1)

            def high_cat(c, t):
                n = B * c + t
                act.wait_ge(s["cat_tr"], n + 1)
                need(act, s["out_mm"], n - 1)
                nc.scalar.copy(cat_hi[:, n % 2], ps_cat[:, n % 2]).then_inc(s["cat_hi_done"], 1)

            def high_x1(c, t):
                n = B * c + t
                act.wait_ge(s["x1_tr"], n + 1)
                if n >= 2:
                    act.wait_ge(x1_out[n % 2], 32 * (n // 2))
                nc.scalar.copy(x1s_hi[:, n % 2], ps_x1[:, 0:E].rearrange("p (k n) -> p k n", k=EC))\
                    .then_inc(s["x1_hi_done"], 1)

            def take(c, t):
                n = B * c + t
                if t == 0 and c >= 2:
                    act.wait_ge(s["attn_done"], c - 1)
                    act.wait_ge(s["conv_step"], 3 * B * (c - 1))
                for h in range(2):
                    act.wait_ge(s["qkv_mm"], 2 * n + h + 1)
                    nc.scalar.copy(qkv[:, c % 2, t, h * HALF:(h + 1) * HALF], ps_qkv[:, n % 2, h, 0:HALF])\
                        .then_inc(s["qkv_ready"], 1)

            act.wait_ge(s["w_in"], 16)
            nc.scalar.copy(w_hi[:, :, 0:QKV], w_raw[:, :, 0:QKV]).then_inc(s["w_hi_done"], 1)
            split_x(0)
            act.wait_ge(s["fold_evac"], 1)
            nc.scalar.copy(w_hi[:, :, QKV:ALLW], w_raw[:, :, QKV:ALLW]).then_inc(s["w_hi_done"], 1)
            act.wait_ge(s["step"], 2)
            nc.scalar.copy(sel[:], sel_raw[:])
            act.wait_ge(s["fold_evac"], 2)
            nc.scalar.copy(bias2[:], bias[:]).then_inc(s["bias_hi"], 1)
            for t in range(B):
                take(0, t)
            split_x(1)
            act.wait_ge(s["wo_in"], 16)
            nc.scalar.copy(wo_hi[:], wo_raw[:]).then_inc(s["w_hi_done"], 1)
            act.wait_ge(s["res_in"], 48)
            nc.scalar.copy(bo2[:], bo[:]).then_inc(s["bias_hi"], 1)
            steps = dict(P=(take, 1), C=(high_cat, -1), X=(high_x1, -2), T=(exp_taps, 0), E=(exp_scores, 0), S=(split_x, 2))
            run(steps, "C0 X0 C1 X1 C2 T P0 X2 E P1 C3 S X3 P2 P3")

        @block.vector
        def _(dve):
            done = [0]

            def link(ins):
                done[0] += 1
                ins.then_inc(s["step"], 1)
                dve.wait_ge(s["step"], done[0])

            link(nc.vector.memset(sel_raw[:], 0.0))
            nc.vector.memset(sel_raw[0:1], 1.0)
            link(nc.vector.memset(sel_raw[32:33], 1.0))
            dve.wait_ge(s["const_ready"], 1)
            dve.wait_ge(s["fold_in"], 48)
            for ec in range(EC):
                ins = nc.vector.tensor_scalar(bv_wide[:, ec], ones[:], bv_col[:, ec:ec + 1], None, ALU.mult)
            link(ins)
            dve.wait_ge(s["fold_mm"], 1)
            nc.vector.tensor_copy(w_raw[:, :, QKV:ALLW], ps_qkv[:, 0, :, 0:DYN]).then_inc(s["fold_evac"], 1)
            dve.wait_ge(s["fold_mm"], 2)
            dve.wait_ge(s["b_in"], 32)
            nc.vector.tensor_tensor(bias[:, QKV:ALLW], bias[:, QKV:ALLW], ps_qkv[:, 1, 0, 0:DYN],
                                    ALU.add).then_inc(s["fold_evac"], 1)
            for part, cols in enumerate((slice(0, QKV), slice(QKV, ALLW))):
                dve.wait_ge(s["w_hi_done"], part + 1)
                nc.vector.tensor_tensor(w_lo[:, :, cols], w_raw[:, :, cols], w_hi[:, :, cols].bitcast(F32),
                                        ALU.subtract).then_inc(s["w_lo_done"], 1)
            low = slice(32, 64)
            dve.wait_ge(s["bias_hi"], 1)
            nc.vector.tensor_tensor(bias2[low], bias[low], bias2[low].bitcast(F32), ALU.subtract)\
                .then_inc(s["bias_ready"], 1)

            def split_out(c):
                if c > 0:
                    return
                dve.wait_ge(s["w_hi_done"], 3)
                nc.vector.tensor_tensor(wo_lo[:], wo_raw[:], wo_hi[:].bitcast(F32), ALU.subtract)\
                    .then_inc(s["w_lo_done"], 1)
                dve.wait_ge(s["bias_hi"], 2)
                nc.vector.tensor_tensor(bo2[low], bo[low], bo2[low].bitcast(F32), ALU.subtract)\
                    .then_inc(s["bo_ready"], 1)

            def tap_maxima(c):
                dve.wait_ge(s["qkv_ready"], 2 * B * (c + 1))
                logits = qkv[:, c % 2, :, QKV:ALLW].rearrange("p t (h k) -> p t h k", k=TAPS)
                nc.vector.tensor_reduce(tmx[:], logits, AX.X, ALU.max).then_inc(s["tap_max"], 1)

            def attend(c, part):
                q, k, v = (qkv[:, c % 2, :, j * E:(j + 1) * E] for j in range(3))
                if part == 0:
                    need(dve, s["attn_done"], c)
                    for t in range(B):
                        ins = nc.vector.tensor_tensor(prod[:, t].rearrange("p (i e) -> p i e", e=E), k,
                                                      q[:, t].unsqueeze(1).broadcast_to([P, B, E]), ALU.mult)
                    link(ins)
                elif part == 1:
                    link(nc.vector.tensor_reduce(sc[:].rearrange("p t i h -> p (t i h)"),
                                                 prod[:].rearrange("p t (g d) -> p (t g) d", d=SD), AX.X, ALU.add))
                    link(nc.vector.tensor_reduce(mx[:], sc[:].rearrange("p t i h -> p t h i"), AX.X, ALU.max))
                    nc.vector.tensor_tensor(sc[:], sc[:], mx[:].unsqueeze(2).broadcast_to([P, B, B, SH_]),
                                            ALU.subtract).then_inc(s["score_sub"], 1)
                elif part == 2:
                    dve.wait_ge(s["tap_exp"], c + 1)
                    link(nc.vector.tensor_reduce(tden[:], tap[:], AX.X, ALU.add))
                    nc.vector.reciprocal(tden[:], tden[:]).then_inc(s["tap_inv"], 1)
                elif part == 3:
                    dve.wait_ge(s["score_exp"], c + 1)
                    link(nc.vector.tensor_reduce(den[:], sc[:].rearrange("p t i h -> p t h i"), AX.X, ALU.add))
                    link(nc.vector.reciprocal(den[:], den[:]))
                    link(nc.vector.tensor_tensor(sc[:], sc[:], den[:].unsqueeze(2).broadcast_to([P, B, B, SH_]),
                                                 ALU.mult))
                elif part == 4:
                    for t in range(B):
                        ins = nc.vector.tensor_tensor(
                            prod[:, t].rearrange("p (i h d) -> p i h d", h=SH_, d=SD),
                            v.rearrange("p i (h d) -> p i h d", d=SD),
                            sc[:, t].unsqueeze(3).broadcast_to([P, B, SH_, SD]), ALU.mult)
                    link(ins)
                else:
                    link(nc.vector.tensor_tensor(prod[:, :, 0:2 * E], prod[:, :, 0:2 * E], prod[:, :, 2 * E:4 * E],
                                                 ALU.add))
                    need(dve, s["cat_tr"], B * c)
                    nc.vector.tensor_tensor(cat[:, :, 0:E], prod[:, :, 0:E], prod[:, :, E:2 * E], ALU.add)\
                        .then_inc(s["attn_done"], 1)

            def low_cat(c, t):
                n = B * c + t
                dve.wait_ge(s["cat_hi_done"], n + 1)
                nc.vector.tensor_tensor(cat_lo[:, n % 2], ps_cat[:, n % 2], cat_hi[:, n % 2].bitcast(F32),
                                        ALU.subtract).then_inc(s["cat_lo_done"], 1)

            def residual(c, t):
                n = B * c + t
                if n == 0:
                    dve.wait_ge(s["res_in"], 48)
                elif t == 0:
                    dve.wait_ge(s["x1_done"], n)
                dve.wait_ge(s["out_mm"], n + 1)
                nc.vector.tensor_tensor(y[:, t], ps_out[:, 0:E], X[:, t * NC + c], ALU.add).then_inc(s["y_ready"], 1)
                dve.wait_ge(s["y_ready"], n + 1)
                ins = nc.vector.bn_stats(st[:, t], y[:, t])
                if t == B - 1:
                    link(ins)

            def statistics(c):
                for t in range(B):
                    ins = nc.vector.bn_aggr(mv[:, t], st[:, t])
                ins.then_inc(s["var_ready"], 1)

            def normalise(c):
                dve.wait_ge(s["rstd_done"], c + 1)
                for t in range(B):
                    nc.vector.tensor_scalar(X[:, t * NC + c], y[:, t], mv[:, t, 0:1], rstd[:, t:t + 1],
                                            ALU.subtract, ALU.mult).then_inc(s["x1_done"], 1)

            def low_x1(c, t):
                n = B * c + t
                dve.wait_ge(s["x1_hi_done"], n + 1)
                if n >= 2:
                    dve.wait_ge(x1_out[n % 2], 32 * (n // 2))
                nc.vector.tensor_tensor(x1s_lo[:, n % 2], ps_x1[:, 0:E].rearrange("p (k n) -> p k n", k=EC),
                                        x1s_hi[:, n % 2].bitcast(F32), ALU.subtract).then_inc(s["x1_lo_done"], 1)

            steps = dict(W=(split_out, 0), A=(attend, 0), M=(tap_maxima, 1), C=(low_cat, -1), R=(residual, -1),
                         V=(statistics, -1), N=(normalise, -1), X=(low_x1, -2))
            tap_maxima(0)
            run(steps, "A0 X0 C0 C1 A1 A2 X1 R0 C2 A3 W X2 R1 C3 X3 R2 A4 R3 V A5 M N")


RING = 3
RING_JOBS = ("K", "Q", "MX", "SH", "V", "RS", "OP")
NPB = 4


def prepare(p):
    keys = [("K", p, c) for c in range(4)]
    maxima = [("MX", p, c, h, n) for c in range(4) for h in range(2) for n in range(NC)]
    return keys, maxima


def first_round():
    keys, maxima = prepare(0)
    steps = ([("LDC",), ("LDA",), ("LDB",), ("X1",), ("WA",), ("CX", 0), ("CX", 1), ("WB",)] + keys[:1] + [("Q", 0)]
             + keys[1:] + [("K2", 0)])
    for t in range(MT):
        steps += maxima[3 * t:3 * t + 3] + [("V", t)]
    return steps + [("SH", 0)]


def block(p, extra, maxima, tail, share):
    steps, maxima = [], list(maxima)

    def some(k):
        for _ in range(k):
            if maxima:
                steps.append(maxima.pop(0))

    for t in range(MT):
        steps.append(("S", p, t))
        steps.extend(extra.get(t - 0.5, []))
        some(share[t] // 2)
        if t >= 2:
            steps.append(("PV", p, t - 2))
        steps.extend(extra.get(t, []))
        some(share[t] - share[t] // 2)
    some(len(maxima))
    steps += tail.get(-1, [])
    steps.append(("PV", p, MT - 2))
    steps += tail.get(0, [])
    steps.append(("PV", p, MT - 1))
    return steps + tail.get(1, [])


def spread(moments):
    extra = {}
    for step, t in moments:
        extra.setdefault(t, []).append(step)
    return extra


def one_round(last):
    keys, maxima = prepare(1)
    loads = [(("LDC",), 0), (("LDB",), 0)]
    first = ([] if last else loads) + [(("LDA",), 0)]
    first += [(k, t) for k, t in zip(keys[:1] + [("Q", 1)] + keys[1:] + [("K2", 1)], AT_K)]
    if not last:
        first += [(("X1",), 4), (("CX", 0), AT_CX[0]), (("CX", 1), AT_CX[1])]
    first += [(("WA",), AT_WA)]
    a = block(0, spread(first), maxima, {AT_SH[0]: [("SH", 1)]}, SHARE[0])
    sums = [(("RS", 0), AT_RS[0]), (("R1", 0, 0), AT_RS[1]), (("R1", 0, 1), AT_RS[2]), (("R2", 0), AT_RS[3]),
            (("R3", 0), AT_RS[4]),
            (("OP", 0, 0), AT_OP[0]), (("OP", 0, 1), AT_OP[1])]
    end = [("RS", 1), ("R1", 1, 0), ("R1", 1, 1), ("R2", 1)]
    outs = [("R3", 1), ("OP", 1, 0), ("OP", 1, 1)]
    if last:
        return a + block(1, spread(sums), [], {1: end + outs}, SHARE[1])
    keys, maxima = prepare(0)
    second = [(k, t) for k, t in zip(keys[:1] + [("Q", 0)] + keys[1:] + [("K2", 0)], AT_K)]
    vs = [("V", t) for t in range(MT)]
    tail = {AT_SH[1]: [("SH", 0)] + vs[:V_BEFORE], 1: vs[V_BEFORE:V_RS] + end + vs[V_RS:V_R3] + outs[:1] + vs[V_R3:] + outs[1:]}
    return a + block(1, spread(second + [(("WB",), AT_WB)] + sums), maxima, tail, SHARE[1])


SHARE = ((0, 1, 2, 3, 2, 2, 4, 4, 4, 4, 4, 2, 0), (0, 1, 1, 2, 2, 3, 4, 4, 4, 4, 4, 3, 0))
AT_K = (0, 0, 0, 1, 1, 2)
AT_CX = (5, 8)
AT_WA, AT_WB = 9, 5
AT_RS = (1, 2, 3, 4, 4)
AT_OP = (6, 8)
V_BEFORE, V_RS, V_R3 = (0, 0, 8)
AT_SH = (0, 0)


class Count:

    def __init__(self, before, steps, prev):
        self.before, self.here, self.prev, self.jobs, self.njobs = before, {}, prev, {}, 0
        self.prologue = not prev
        self.total = {}
        for st in steps:
            for k in self.keys(st, None):
                self.total[k] = self.total.get(k, 0) + 1

    def keys(self, st, _):
        out = [st[0]]
        if st[0] == "PV" and st[2] >= 1:
            out.append("ADD")
        if st[0] == "PV" and st[2] == MT - 1:
            out.append("COPY")
        if st[0] in RING_JOBS:
            out.append("ring%d" % (self.njobs % RING))
            self.njobs += 1
        return out

    def start(self):
        self.njobs = 0

    def of(self, key):
        return self.before.get(key, 0) + self.here.get(key, 0)

    def slot(self):
        return self.njobs % RING

    def job(self, st):
        if st in self.jobs:
            slot, n = self.jobs[st]
            return slot, self.before.get("ring%d" % slot, 0) + n
        slot, n = self.prev[st]
        return slot, self.before.get("ring%d" % slot, 0) + n

    def take(self, st):
        for k in self.keys(st, None):
            self.here[k] = self.here.get(k, 0) + 1
            if k.startswith("ring"):
                self.jobs[st] = (int(k[4:]), self.here[k])

    def left(self):
        return {st: (slot, n - self.total["ring%d" % slot]) for st, (slot, n) in self.jobs.items()}


def walk(eng, handle):
    prologue, steady, final = first_round(), one_round(False), one_round(True)
    ROUNDS = B * QUADS

    def run(i, steps, before, prev):
        n = Count(before, steps, prev)
        n.start()
        for st in steps:
            handle(i, n, st)
            n.take(st)
        return n

    n0 = run(-1, prologue, {}, {})
    base = dict(n0.total)
    n1 = run(0, steady, base, n0.left())
    per = n1.total

    def before(i):
        return {k: base.get(k, 0) + i * per.get(k, 0) for k in set(base) | set(per)}

    left = n1.left()
    with eng.Fori(1, ROUNDS - 1) as i:
        run(i, steady, before(i), left)
    return run(ROUNDS - 1, final, before(ROUNDS - 1), left)


WA_W = EC * (P + P + 2 * P) + 2 * E
WB_W = EC * 2 * P


class FirstLoads:

    def __init__(self, nc, ctx):
        self.ctx_raw, self.wa_raw, self.wb_raw = (
            ctx.enter_context(nc.sbuf_tensor(n, shape, F32))
            for n, shape in (("ctx_raw", [P, EC, M]), ("wa_raw", [P, WA_W]), ("wb_raw", [P, WB_W])))
        self.sems = sems(ctx, nc, "ctx_in wa_in wb_in")

    def start(self, sp, a):
        sp.dma_start(self.ctx_raw[:], a["ctxT"][0].rearrange("(k p) m -> p k m", p=P))\
            .then_inc(self.sems["ctx_in"], 16)
        sp.dma_start(self.wa_raw[:], a["pack_a"][QUADS - 1]).then_inc(self.sems["wa_in"], 16)
        sp.dma_start(self.wb_raw[:], a["pack_b"][QUADS - 1]).then_inc(self.sems["wb_in"], 16)


def cross_attention(nc, a, X, consts, loads, x1_hi, x1_lo):
    ctx_raw, wa_raw, wb_raw = loads.ctx_raw, loads.wa_raw, loads.wb_raw
    ident, ones = consts["ident"], consts["ones"]
    with ExitStack() as ctx:
        def sb(name, shape, dt=F32):
            return ctx.enter_context(nc.sbuf_tensor("xa_" + name, shape, dt))

        ctx_hi = sb("ctx_hi", [P, EC, M], F32R)
        ctx_lo = sb("ctx_lo", [P, EC, M], F32R)
        wa_hi, wa_lo = sb("wa_hi", [P, WA_W], F32R), sb("wa_lo", [P, WA_W], F32R)
        wb_hi, wb_lo = sb("wb_hi", [P, WB_W], F32R), sb("wb_lo", [P, WB_W], F32R)
        xh, xl = sb("xh", [P, EC, N], F32R), sb("xl", [P, EC, N], F32R)
        k_two = [sb(f"k_two{p}", [P, 2, M], F32R) for p in range(2)]
        k_one = [sb(f"k_one{p}", [P, 2, M], F32R) for p in range(2)]
        q_two = [sb(f"q_two{p}", [P, 2, N], F32R) for p in range(2)]
        q_low = [sb(f"q_low{p}", [P, 2, N], F32R) for p in range(2)]
        v = sb("v", [P, MT, 4 * XD])
        pexp = sb("pexp", [P, NPB, 2, N])
        total = [sb(f"total{p}", [P, 2, N]) for p in range(2)]
        parts = sb("parts", [P, 2, NC, 4])
        negmax = sb("negmax", [P, NC, P])
        pv_sb, sums, inv, att = (sb(x, [P, N]) for x in ("pv_sb", "sums", "inv", "att"))
        att_hi, att_lo = sb("att_hi", [P, N], F32R), sb("att_lo", [P, N], F32R)

        ps_s = ctx.enter_context(nc.psum_tensor("ps_s", [P, 2, 2, N], F32))
        ps_pv = ctx.enter_context(nc.psum_tensor("ps_pv", [P, N], F32))
        ps_ring = ctx.enter_context(nc.psum_tensor("ps_ring", [P, RING, 512], F32))

        s = sems(ctx, nc, "ones_set zero_set scores_ready exp_done pv_done add0_done add1_done pv_copied att_ready "
                          "k_hi_done q_hi_done k_one_in shift_ready x1_in ctx_hi_done ctx_lo_done "
                          "wa_hi_done wa_lo_done wb_hi_done wb_lo_done att_done att_hi_done filled0 filled1 filled2 "
                          "drained0 drained1 drained2 inv_ready")
        s.update(loads.sems)
        filled = [s[f"filled{r}"] for r in range(RING)]
        drained = [s[f"drained{r}"] for r in range(RING)]
        block = ctx.enter_context(nc.Block())

        def w_a(t, part, k):
            at = (k * P, EC * P + k * P, 2 * EC * P + k * 2 * P)[part]
            return t[:, at:at + (2 * P if part == 2 else P)]

        def w_b(t, part, k):
            return t[:, part * EC * P + k * P:part * EC * P + (k + 1) * P]

        def w_kq(hi, p, part, k):
            return w_a(wa_hi if hi else wa_lo, part, k) if p == 0 else w_b(wb_hi if hi else wb_lo, part, k)

        def w_out(t, p):
            at = EC * 4 * P + p * E
            return t[:, at:at + E]

        def rows(t):
            return M_LAST if t == MT - 1 else P

        def half(p64):
            return slice(0, XD) if p64 == 0 else slice(XD, P)

        def user_before(p, t):
            n = p * MT + t
            if n >= NPB:
                return n - NPB
            return max(m for m in range(2 * MT) if m % NPB == n % NPB) - 2 * MT

        def adds_through(m):
            return m // MT * (MT - 1) + max(m % MT, 1)

        def next_batch(i):
            return (i + 1) // QUADS

        def pack_at(i):
            return i % QUADS

        @block.sync
        def _(sp):
            def handle(i, n, st):
                kind = st[0]
                if n.prologue and kind in ("LDC", "LDA", "LDB"):
                    return
                if kind == "LDC":
                    need(sp, s["ctx_lo_done"], n.of("CX"))
                    sp.dma_start(ctx_raw[:], a["ctxT"][bass.ds(next_batch(i), 1)]
                                 .rearrange("b (k p) m -> p (b k) m", p=P)).then_inc(s["ctx_in"], 16)
                elif kind == "LDA":
                    need(sp, s["wa_lo_done"], n.of("WA"))
                    sp.dma_start(wa_raw[:], a["pack_a"][bass.ds(pack_at(i), 1)].rearrange("b p w -> p (b w)"))\
                        .then_inc(s["wa_in"], 16)
                elif kind == "LDB":
                    need(sp, s["wb_lo_done"], n.of("WB"))
                    sp.dma_start(wb_raw[:], a["pack_b"][bass.ds(pack_at(i), 1)].rearrange("b p w -> p (b w)"))\
                        .then_inc(s["wb_in"], 16)
                elif kind == "X1":
                    if not n.prologue:
                        slot, c = n.job(("K", 1, 3))
                        sp.wait_ge(filled[slot], c)
                    for dst, src in ((xh, x1_hi), (xl, x1_lo)):
                        sp.dma_start(dst[:].bitcast(F32), src[bass.ds(next_batch(i), 1)]
                                     .rearrange("b p k n -> p (b k) n")).then_inc(s["x1_in"], 16)
                elif kind == "K2":
                    p = st[1]
                    if n.prologue:
                        sp.wait_ge(s["ones_set"], 4)
                    sp.wait_ge(s["k_hi_done"], 2 * n.of("K"))
                    for h in range(2):
                        sp.dma_start(k_one[p][half(h), h, :].bitcast(F32), k_two[p][half(h), h, :].bitcast(F32))\
                            .then_inc(s["k_one_in"], 16)

            walk(sp, handle)

        @block.tensor
        def _(pe):
            def take_bank(n):
                r = n.slot()
                need(pe, drained[r], n.of("ring%d" % r))
                return r

            def project(out, terms):
                for q, (w, x) in enumerate(terms):
                    ins = nc.tensor.matmul(out, w, x, start=q == 0, stop=q == len(terms) - 1)
                return ins

            def handle(i, n, st):
                kind = st[0]
                if kind == "S":
                    p, t = st[1:]
                    if t == 0:
                        r, c = n.job(("SH", p))
                        pe.wait_ge(drained[r], c)
                        pe.wait_ge(s["k_one_in"], 32 * n.of("K2"))
                    need(pe, s["exp_done"], n.of("S") - 1)
                    m, ms = rows(t), slice(t * P, t * P + rows(t))
                    for h in range(2):
                        nc.tensor.matmul(ps_s[0:m, t_of(n), h, :], k_two[p][:, h, ms], q_two[p][:, h, :],
                                         start=True, stop=False)
                        ins = nc.tensor.matmul(ps_s[0:m, t_of(n), h, :], k_one[p][:, h, ms], q_low[p][:, h, :],
                                               start=False, stop=True)
                    ins.then_inc(s["scores_ready"], 1)
                elif kind == "PV":
                    p, t = st[1:]
                    if t == 0:
                        need(pe, s["pv_copied"], n.of("COPY"))
                        if p == 0:
                            r, c = n.job(("V", MT - 1))
                            pe.wait_ge(drained[r], c)
                    pe.wait_ge(s["exp_done"], n.of("PV") + 1)
                    m, buf = rows(t), (p * MT + t) % NPB
                    for h in range(2):
                        at = (2 * p + h) * XD
                        ins = nc.tensor.matmul(ps_pv[half(h), :], v[0:m, t, at:at + XD], pexp[0:m, buf, h, :],
                                               start=t == 0, stop=t == MT - 1)
                    ins.then_inc(s["pv_done"], 1)
                elif kind == "K":
                    p, c = st[1:]
                    r = take_bank(n)
                    if c == 0:
                        if p == 0:
                            pe.wait_ge(s["ctx_lo_done"], n.of("CX"))
                            pe.wait_ge(s["wa_lo_done"], n.of("WA"))
                        else:
                            pe.wait_ge(s["wb_lo_done"], n.of("WB"))
                    cols = slice(KC0[c], KC0[c] + CW)
                    terms = [(w_kq(wh, p, 0, k), (ctx_hi if ch else ctx_lo)[:, k, cols])
                             for wh, ch in ((1, 1), (0, 1), (1, 0)) for k in range(EC)]
                    project(ps_ring[:, r, 0:CW], terms).then_inc(filled[r], 1)
                elif kind == "Q":
                    p = st[1]
                    r = take_bank(n)
                    pe.wait_ge(s["x1_in"], 32 * n.of("X1"))
                    terms = [(w_kq(wh, p, 1, k), (xh if ch else xl)[:, k, :])
                             for wh, ch in ((1, 1), (0, 1), (1, 0)) for k in range(EC)]
                    project(ps_ring[:, r, :], terms).then_inc(filled[r], 1)
                elif kind == "MX":
                    p, c, h, q = st[1:]
                    r = take_bank(n)
                    kr, kc = n.job(("K", p, c))
                    pe.wait_ge(drained[kr], kc)
                    if c == 0:
                        qr, qc = n.job(("Q", p))
                        pe.wait_ge(drained[qr], qc)
                    nc.tensor.matmul(ps_ring[:, r, 0:CW], q_two[p][:, h, q * P:(q + 1) * P],
                                     k_two[p][:, h, KC0[c]:KC0[c] + CW], start=True, stop=True)\
                        .then_inc(filled[r], 1)
                elif kind == "SH":
                    r = take_bank(n)
                    pe.wait_ge(s["shift_ready"], 2 * (n.of("SH") + 1))
                    for q in range(NC):
                        ins = nc.tensor.matmul(ps_ring[:, r, q * P:(q + 1) * P], negmax[:, q, :], ident[:],
                                               start=True, stop=True)
                    ins.then_inc(filled[r], 1)
                elif kind == "V":
                    t = st[1]
                    r = take_bank(n)
                    m, ms = rows(t), slice(t * P, t * P + rows(t))
                    terms = [((ctx_hi if ch else ctx_lo)[:, k, ms], w_a(wa_hi if wh else wa_lo, 2, k))
                             for wh, ch in ((1, 1), (0, 1), (1, 0)) for k in range(EC)]
                    project(ps_ring[0:m, r, 0:4 * XD], terms).then_inc(filled[r], 1)
                elif kind == "RS":
                    p = st[1]
                    r = take_bank(n)
                    pe.wait_ge(s["add0_done"], n.of("ADD"))
                    pe.wait_ge(s["add1_done"], n.of("ADD"))
                    for h in range(2):
                        ins = nc.tensor.matmul(ps_ring[half(h), r, :], ones[:, 0:XD], total[p][:, h, :],
                                               start=True, stop=True)
                    ins.then_inc(filled[r], 1)
                elif kind == "OP":
                    p, j = st[1:]
                    r = take_bank(n)
                    pe.wait_ge(s["att_ready"], n.of("R2"))
                    for q in range(2):
                        cs = slice((2 * j + q) * P, (2 * j + q + 1) * P)
                        terms = [(att_hi[:, cs], w_out(wa_hi, p)), (att_lo[:, cs], w_out(wa_hi, p)),
                                 (att_hi[:, cs], w_out(wa_lo, p))]
                        ins = project(ps_ring[:, r, q * E:(q + 1) * E], terms)
                    ins.then_inc(filled[r], 1)

            def t_of(n):
                return n.here.get("S", 0) % 2

            walk(pe, handle)

        @block.scalar
        def _(act):
            def handle(i, n, st):
                kind = st[0]
                if kind == "S":
                    p, t = st[1:]
                    act.wait_ge(s["scores_ready"], n.of("S") + 1)
                    m, buf, prev = rows(t), (p * MT + t) % NPB, user_before(p, t)
                    first = n.before.get("S", 0)
                    need(act, s["pv_done"], first + prev + 1)
                    need(act, s["add0_done"], n.before.get("ADD", 0) + adds_through(prev))
                    need(act, s["add1_done"], n.before.get("ADD", 0) + adds_through(prev))
                    nc.scalar.activation(pexp[0:m, buf], ps_s[0:m, (p * MT + t) % 2], ACT.Exp, scale=XD ** -0.5)\
                        .then_inc(s["exp_done"], 1)
                elif kind == "PV" and st[2] == MT - 1:
                    act.wait_ge(s["pv_done"], n.of("PV") + 1)
                    need(act, s["att_ready"], n.of("R2"))
                    nc.scalar.copy(pv_sb[:], ps_pv[:]).then_inc(s["pv_copied"], 1)
                elif kind == "K":
                    p, c = st[1:]
                    r = n.slot()
                    act.wait_ge(filled[r], n.of("ring%d" % r) + 1)
                    skip = 3 * CW - KC0[3] if c == 3 else 0
                    for h in range(2):
                        nc.scalar.copy(k_two[p][half(h), h, KC0[c] + skip:KC0[c] + CW],
                                       ps_ring[half(h), r, skip:CW]).then_inc(s["k_hi_done"], 1)
                elif kind == "Q":
                    p = st[1]
                    r = n.slot()
                    act.wait_ge(filled[r], n.of("ring%d" % r) + 1)
                    for h in range(2):
                        for to in range(2):
                            nc.scalar.copy(q_two[p][half(to), h, :], ps_ring[half(h), r, :])\
                                .then_inc(s["q_hi_done"], 1)
                elif kind == "RS":
                    r = n.slot()
                    act.wait_ge(filled[r], n.of("ring%d" % r) + 1)
                    need(act, s["att_ready"], n.of("R2"))
                    nc.scalar.copy(sums[:], ps_ring[:, r, :]).then_inc(drained[r], 1)
                elif kind == "R3":
                    act.wait_ge(s["att_done"], n.of("R3") + 1)
                    nc.scalar.copy(att_hi[:], att[:]).then_inc(s["att_hi_done"], 1)
                elif kind == "SH":
                    p = st[1]
                    r = n.slot()
                    act.wait_ge(filled[r], n.of("ring%d" % r) + 1)
                    nc.scalar.copy(q_low[p][half(1), 0, :], ps_ring[half(1), r, :])
                    nc.scalar.copy(q_low[p][half(0), 1, :], ps_ring[half(0), r, :]).then_inc(drained[r], 1)
                elif kind == "V":
                    t = st[1]
                    r = n.slot()
                    act.wait_ge(filled[r], n.of("ring%d" % r) + 1)
                    nc.scalar.copy(v[0:rows(t), t, :], ps_ring[0:rows(t), r, 0:4 * XD]).then_inc(drained[r], 1)
                elif kind == "CX":
                    k = st[1]
                    act.wait_ge(s["ctx_in"], 16 * n.of("LDC"))
                    if k == 0 and not n.prologue:
                        r, c = n.job(("K", 1, 3))
                        act.wait_ge(filled[r], c)
                    nc.scalar.copy(ctx_hi[:, k], ctx_raw[:, k]).then_inc(s["ctx_hi_done"], 1)
                elif kind == "WA":
                    act.wait_ge(s["wa_in"], 16 * n.of("LDA"))
                    nc.scalar.copy(wa_hi[:], wa_raw[:]).then_inc(s["wa_hi_done"], 1)
                elif kind == "WB":
                    act.wait_ge(s["wb_in"], 16 * n.of("LDB"))
                    nc.scalar.copy(wb_hi[:], wb_raw[:]).then_inc(s["wb_hi_done"], 1)

            walk(act, handle)

        def add(eng, n, st, h, sem):
            p, t = st[1:]
            m, buf, b0 = rows(t), (p * MT + t) % NPB, (p * MT) % NPB
            eng.wait_ge(s["exp_done"], n.of("PV") + 1)
            need(eng, sem, n.of("ADD"))
            first = pexp[0:m, b0, h, :] if t == 1 else total[p][0:m, h, :]
            e = nc.vector if h == 0 else nc.gpsimd
            e.tensor_tensor(total[p][0:m, h, :], first, pexp[0:m, buf, h, :], ALU.add).then_inc(sem, 1)

        @block.gpsimd
        def _(pool):
            def handle(i, n, st):
                kind = st[0]
                if kind == "PV" and st[2] >= 1:
                    add(pool, n, st, 1, s["add1_done"])
                elif kind == "R2":
                    done = n.of("R2")
                    pool.wait_ge(s["inv_ready"], n.of("R1"))
                    pool.wait_ge(s["pv_copied"], done + 1)
                    nc.gpsimd.tensor_tensor(att[:], pv_sb[:], inv[:], ALU.mult).then_inc(s["att_done"], 1)
                    pool.wait_ge(s["att_hi_done"], done + 1)
                    nc.gpsimd.tensor_tensor(att_lo[:], att[:], att_hi[:].bitcast(F32), ALU.subtract)\
                        .then_inc(s["att_ready"], 1)
                elif kind == "CX" and not (n.prologue and st[1] == 1):
                    k = st[1]
                    pool.wait_ge(s["ctx_hi_done"], n.of("CX") + 1)
                    nc.gpsimd.tensor_tensor(ctx_lo[:, k], ctx_raw[:, k], ctx_hi[:, k].bitcast(F32), ALU.subtract)\
                        .then_inc(s["ctx_lo_done"], 1)
                elif kind == "WA":
                    pool.wait_ge(s["wa_hi_done"], n.of("WA") + 1)
                    nc.gpsimd.tensor_tensor(wa_lo[:], wa_raw[:], wa_hi[:].bitcast(F32), ALU.subtract)\
                        .then_inc(s["wa_lo_done"], 1)
                elif kind == "WB":
                    pool.wait_ge(s["wb_hi_done"], n.of("WB") + 1)
                    nc.gpsimd.tensor_tensor(wb_lo[:], wb_raw[:], wb_hi[:].bitcast(F32), ALU.subtract)\
                        .then_inc(s["wb_lo_done"], 1)

            walk(pool, handle)

        @block.vector
        def _(dve):
            nc.vector.memset(negmax[:], 0.0)
            nc.vector.memset(att[:], 1.0).then_inc(s["zero_set"], 1)
            dve.wait_ge(s["zero_set"], 1)
            for p in range(2):
                for h in range(2):
                    nc.vector.tensor_copy(k_one[p][half(1 - h), h, :],
                                          att[half(1 - h), 0:1].broadcast_to([XD, M])).then_inc(s["ones_set"], 1)

            def handle(i, n, st):
                kind = st[0]
                if kind == "PV" and st[2] >= 1:
                    add(dve, n, st, 0, s["add0_done"])
                elif kind == "CX" and n.prologue and st[1] == 1:
                    dve.wait_ge(s["ctx_hi_done"], 2)
                    nc.vector.tensor_tensor(ctx_lo[:, 1], ctx_raw[:, 1], ctx_hi[:, 1].bitcast(F32), ALU.subtract)\
                        .then_inc(s["ctx_lo_done"], 1)
                elif kind == "K":
                    p, c = st[1:]
                    r = n.slot()
                    skip = 3 * CW - KC0[3] if c == 3 else 0
                    cols = slice(KC0[c] + skip, KC0[c] + CW)
                    for h in range(2):
                        dve.wait_ge(s["k_hi_done"], 2 * n.of("K") + h + 1)
                        ins = nc.vector.tensor_tensor(k_two[p][half(1 - h), h, cols], ps_ring[half(h), r, skip:CW],
                                                      k_two[p][half(h), h, cols].bitcast(F32), ALU.subtract)
                    ins.then_inc(drained[r], 1)
                elif kind == "Q":
                    p = st[1]
                    r = n.slot()
                    dve.wait_ge(s["q_hi_done"], 4 * (n.of("Q") + 1))
                    for h in range(2):
                        ins = nc.vector.tensor_tensor(q_low[p][half(h), h, :], ps_ring[half(h), r, :],
                                                      q_two[p][half(h), h, :].bitcast(F32), ALU.subtract)
                    ins.then_inc(drained[r], 1)
                elif kind == "MX":
                    p, c, h, q = st[1:]
                    r = n.slot()
                    dve.wait_ge(filled[r], n.of("ring%d" % r) + 1)
                    nc.vector.tensor_reduce(parts[:, h, q, c:c + 1], ps_ring[:, r, 0:CW], AX.X, ALU.max)\
                        .then_inc(drained[r], 1)
                elif kind == "SH":
                    p = st[1]
                    r, c = n.job(("MX", p, 3, 1, NC - 1))
                    dve.wait_ge(drained[r], c)
                    for h, col in ((0, XD), (1, 0)):
                        nc.vector.tensor_reduce(negmax[:, :, col:col + 1], parts[:, h], AX.X, ALU.max, negate=True)\
                            .then_inc(s["shift_ready"], 1)
                elif kind == "R1":
                    if st[2] == 0:
                        r, c = n.job(("RS", st[1]))
                        dve.wait_ge(drained[r], c)
                        need(dve, s["att_ready"], n.of("R2"))
                    cs = slice(st[2] * N // 2, (st[2] + 1) * N // 2)
                    nc.vector.reciprocal(inv[:, cs], sums[:, cs]).then_inc(s["inv_ready"], 1)
                elif kind == "OP":
                    p, j = st[1:]
                    r = n.slot()
                    dve.wait_ge(filled[r], n.of("ring%d" % r) + 1)
                    xs = X[:, bass.ds(i // QUADS * NC + 2 * j, 2), :].rearrange("p t e -> p (t e)")
                    nc.vector.tensor_tensor(xs, ps_ring[:, r, :], xs, ALU.add).then_inc(drained[r], 1)

            walk(dve, handle)


def expert_round(first, last):
    steps = [] if last else [("L", 0)]
    if first:
        steps += [("T", b) for b in range(B)] + [("H", 0), ("G",), ("H", 1), ("ST", 0), ("B2", 0, 0), ("B2", 0, 1),
                                                  ("ST", 1), ("Y", 0, 0), ("B2", 1, 0)]
    else:
        steps += [("H", 0), ("Y", 2 * B - 1, -1), ("H", 1), ("Y", 0, 0)]
    steps += [("W", 1)] + ([] if last else [("L", 1)])
    for u in range(2, 2 * B):
        if first and u <= B:
            ahead = [[("ST", u)], [("B2", u, 0)]] if u < B else [[], []]
            steps += [("H", u), ("B2", u - 1, 1)] + ahead[0] + [("Y", u - 1, 0)] + ahead[1]
        else:
            steps += [("H", u), ("Y", u - 1, 0)]
        if last and u > B:
            steps.append(("F1", u - 1 - B))
        if last and u > B + 1:
            steps.append(("F2", u - 2 - B))
        if u == 5 and not last:
            steps.append(("W", 0))
    if last:
        steps += [("Y", 2 * B - 1, 0), ("F2", B - 2), ("F1", B - 1), ("F2", B - 1)]
    return steps


def expert_walk(eng, handle):
    ROUNDS = NE // 2

    def run(i, steps, before):
        n = {}
        for st in steps:
            handle(i, lambda k: before.get(k, 0) + n.get(k, 0), st)
            n[st[0]] = n.get(st[0], 0) + 1
        return n

    first = {"W": 1}
    n0 = run(0, expert_round(True, False), first)
    per = {"W": 2, "L": 2, "H": 2 * B, "Y": 2 * B}

    def before(i):
        return {k: first.get(k, 0) + n0[k] + (i - 1) * per[k] for k in per}

    with eng.Fori(1, ROUNDS - 1) as i:
        run(i, expert_round(False, False), before(i))
    run(ROUNDS - 1, expert_round(False, True), before(ROUNDS - 1))


def experts(nc, a, X, consts, out):
    ident, neghalf = consts["ident"], consts["neghalf"]
    T = B * NC
    with ExitStack() as ctx:
        def sb(name, shape, dt=F32):
            return ctx.enter_context(nc.sbuf_tensor("ex_" + name, shape, dt))

        WW = EC * HID + HC * E
        w_raw = [sb(f"w_raw{p}", [P, WW + HC]) for p in range(2)]
        b1 = [sb(f"b1{p}", [P, HC]) for p in range(2)]
        w_hi = [sb(f"w_hi{p}", [P, WW], F32R) for p in range(2)]
        w_lo = [sb(f"w_lo{p}", [P, WW], F32R) for p in range(2)]
        wg = sb("wg", [P, EC, NE])
        HI_HI, LO_HI, HI_LO = 0, 32, 64
        b2_raw, b2x = sb("b2_raw", [P, E]), sb("b2x", [P, E], F32R)
        zero = sb("zero", [P, 1])
        st_ = sb("st", [P, T, 6])
        mv = sb("mv", [P, T, 2])
        rstd = sb("rstd", [P, T])
        xT_hi = sb("xT_hi", [P, EC, B * N], F32R)
        xT_lo = sb("xT_lo", [P, EC, B * N], F32R)
        xT_f = sb("xT_f", [P, 2, EC, P])
        probs = sb("probs", [P, T, NE])
        gred = sb("gred", [P, T])
        top = sb("top", [P, T, 8])
        idx = sb("idx", [P, T, 8], U32)
        idxf = sb("idxf", [P, T, 8])
        norm = sb("norm", [P, T, TOPK])
        iota = sb("iota", [P, NE])
        hot = sb("hot", [P, T, NE])
        score = sb("score", [P, T, NE])
        scoreT = sb("scoreT", [P, T, P], F32R)
        h_f = sb("h_f", [P, 2, N])
        h_hi = sb("h_hi", [P, 2, HC, N], F32R)
        h_lo = sb("h_lo", [P, 2, HC, N], F32R)

        ps_h = ctx.enter_context(nc.psum_tensor("ps_h", [P, 4, 512], F32))
        ps_y = ctx.enter_context(nc.psum_tensor("ps_y", [P, 2, 512], F32))
        ps_t = ctx.enter_context(nc.psum_tensor("ps_t", [P, 512], F32))
        ps_g = ctx.enter_context(nc.psum_tensor("ps_g", [P, 512], F32))

        s = sems(ctx, nc, "const_in w_in0 w_in1 w_hi_done w_lo_done var_ready rstd_half rstd_ready x_done xT_tr "
                          "xT_hi_done xT_lo_done gate_mm gate_sub gate_exp score_done score_tr scoreT_hi_done scoreT_lo_done zero_set b2_hi_done b2_ready b2_mm b2_added "
                          "h_mm h_act h_lo_done y_mm y_added step fstep fvar frstd_half frstd fdone stored")
        w_in = [s["w_in0"], s["w_in1"]]
        block = ctx.enter_context(nc.Block())
        pack = a["pack_e"]

        def w1(w, k, c):
            return w[:, k * HID + c * P:k * HID + (c + 1) * P]

        def w2(w, c):
            return w[:, EC * HID + c * E:EC * HID + (c + 1) * E]

        @block.sync
        def _(sp):
            sp.dma_start(wg[:], a["Wg"].rearrange("(k p) e -> p k e", p=P)).then_inc(s["const_in"], 16)
            sp.wait_ge(s["zero_set"], 1)
            for row in (HI_HI, LO_HI, HI_LO):
                sp.dma_start(b2_raw[row:row + NE], a["b2"]).then_inc(s["const_in"], 16)
            for p in range(2):
                sp.dma_start(w_raw[p][:], pack[p]).then_inc(w_in[p], 16)

            def handle(i, n, st):
                if st[0] == "L":
                    p = st[1]
                    sp.wait_ge(s["w_lo_done"], n("W"))
                    sp.dma_start(w_raw[p][:], pack[bass.ds(2 * i + 2 + p, 1)].rearrange("e p w -> p (e w)"))\
                        .then_inc(w_in[p], 16)
                elif st[0] == "F2":
                    b = st[1]
                    sp.wait_ge(s["fdone"], NC * (b + 1))
                    sp.dma_start(out[b].rearrange("(t p) e -> p t e", p=P), X[:, NC * b:NC * (b + 1), :])\
                        .then_inc(s["stored"], 16)

            expert_walk(sp, handle)
            sp.wait_ge(s["stored"], 16 * B)

        @block.gpsimd
        def _(pool):
            for b in range(B):
                pool.wait_ge(s["var_ready"], b + 1)
                r = slice(NC * b, NC * (b + 1))
                nc.gpsimd.tensor_scalar(rstd[:, r], mv[:, r, 1], EPS, None, ALU.add).then_inc(s["rstd_half"], 1)
                pool.wait_ge(s["rstd_half"], b + 1)
                nc.gpsimd.tensor_tensor(rstd[:, r], rstd[:, r], neghalf[:, 0:NC], ALU.pow)\
                    .then_inc(s["rstd_ready"], 1)

            def split(p, k):
                pool.wait_ge(s["w_hi_done"], k)
                nc.gpsimd.tensor_tensor(w_lo[p][:], w_raw[p][:, 0:WW], w_hi[p][:].bitcast(F32), ALU.subtract)\
                    .then_inc(s["w_lo_done"], 1)

            split(0, 1)

            def handle(i, n, st):
                if st[0] == "W":
                    split(st[1], n("W") + 1)
                elif st[0] == "F1":
                    b = st[1]
                    pool.wait_ge(s["fvar"], b + 1)
                    r = slice(NC * b, NC * (b + 1))
                    nc.gpsimd.tensor_scalar(rstd[:, r], mv[:, r, 1], EPS, None, ALU.add).then_inc(s["frstd_half"], 1)
                    pool.wait_ge(s["frstd_half"], b + 1)
                    nc.gpsimd.tensor_tensor(rstd[:, r], rstd[:, r], neghalf[:, 0:NC], ALU.pow)\
                        .then_inc(s["frstd"], 1)

            expert_walk(pool, handle)

        @block.tensor
        def _(pe):
            pe.wait_ge(s["const_in"], 64)

            def gate(t):
                pe.wait_ge(s["xT_hi_done"], t + 1)
                for k in range(EC):
                    ins = nc.tensor.matmul(ps_g[:, t * NE:(t + 1) * NE], xT_f[:, t % 2, k], wg[:, k],
                                           start=k == 0, stop=k == EC - 1)
                ins.then_inc(s["gate_mm"], 1)

            def turn(t):
                pe.wait_ge(s["x_done"], t + 1)
                need(pe, s["xT_lo_done"], t - 1)
                for k in range(EC):
                    ins = nc.tensor.transpose(ps_y[:, t % 2, k * P:(k + 1) * P], X[:, t, k * P:(k + 1) * P], ident[:])
                ins.then_inc(s["xT_tr"], 1)

            def handle(i, n, st):
                kind = st[0]
                if kind == "H":
                    u = st[1]
                    p, rows = u // B, slice(u % B * N, (u % B + 1) * N)
                    if u % B == 0:
                        pe.wait_ge(s["w_lo_done"], n("W"))
                    if isinstance(i, int) and i == 0 and u < B:
                        pe.wait_ge(s["xT_lo_done"], NC * (u + 1))
                    for c in range(HC):
                        need(pe, s["h_act"], HC * (n("H") - 1) + c + 1)
                        terms = [(w1(w_hi[p], k, c), xT_hi[:, k, rows]) for k in range(EC)] \
                            + [(w1(w_hi[p], k, c), xT_lo[:, k, rows]) for k in range(EC)] \
                            + [(w1(w_lo[p], k, c), xT_hi[:, k, rows]) for k in range(EC)]
                        for q, (w, x) in enumerate(terms):
                            ins = nc.tensor.matmul(ps_h[:, c, :], w, x, start=q == 0, stop=q == len(terms) - 1)
                        ins.then_inc(s["h_mm"], 1)
                elif kind == "T":
                    for t in range(NC * st[1], NC * (st[1] + 1)):
                        turn(t)
                        if t >= 1:
                            gate(t - 1)
                    if t == T - 1:
                        gate(t)
                elif kind == "ST":
                    b = st[1]
                    pe.wait_ge(s["score_done"], 1)
                    need(pe, s["scoreT_lo_done"], b)
                    for t in range(NC):
                        ins = nc.tensor.transpose(ps_t[0:NE, t * P:(t + 1) * P], score[:, NC * b + t, :], ident[:])
                    ins.then_inc(s["score_tr"], 1)
                elif kind == "B2":
                    j = 2 * st[1] + st[2]
                    pe.wait_ge(s["scoreT_lo_done"], st[1] + 1)
                    if j == 0:
                        pe.wait_ge(s["b2_ready"], 1)
                    need(pe, s["b2_added"], j)
                    for q in range(2):
                        ins = nc.tensor.matmul(ps_g[:, q * E:(q + 1) * E], scoreT[:, 2 * j + q, :], b2x[:],
                                               start=True, stop=True)
                    ins.then_inc(s["b2_mm"], 1)
                elif kind == "Y":
                    u = st[1]
                    p = u // B
                    pe.wait_ge(s["h_lo_done"], HC * (n("Y") + 1))
                    for j in range(2):
                        need(pe, s["y_added"], 2 * n("Y") + j - 1)
                        for q in range(2):
                            cs = slice((2 * j + q) * P, (2 * j + q + 1) * P)
                            terms = [(h_hi[:, u % 2, c, cs], w2(w_hi[p], c)) for c in range(HC)] \
                                + [(h_lo[:, u % 2, c, cs], w2(w_hi[p], c)) for c in range(HC)] \
                                + [(h_hi[:, u % 2, c, cs], w2(w_lo[p], c)) for c in range(HC)]
                            for m, (h, w) in enumerate(terms):
                                ins = nc.tensor.matmul(ps_y[:, j, q * E:(q + 1) * E], h, w,
                                                       start=m == 0, stop=m == len(terms) - 1)
                        ins.then_inc(s["y_mm"], 1)

            expert_walk(pe, handle)

        @block.scalar
        def _(act):
            act.wait_ge(s["zero_set"], 1)
            nc.scalar.copy(scoreT[:], zero[:, 0:1].unsqueeze(2).broadcast_to([P, T, P]))
            act.wait_ge(s["const_in"], 64)
            nc.scalar.copy(b2x[:], b2_raw[:]).then_inc(s["b2_hi_done"], 1)
            act.wait_ge(w_in[0], 16)
            nc.scalar.copy(b1[0][:], w_raw[0][:, WW:WW + HC])
            nc.scalar.copy(w_hi[0][:], w_raw[0][:, 0:WW]).then_inc(s["w_hi_done"], 1)
            def take_row(t):
                act.wait_ge(s["xT_tr"], t + 1)
                need(act, s["gate_mm"], t - 1)
                src = ps_y[:, t % 2, 0:E].rearrange("p (k n) -> p k n", k=EC)
                nc.scalar.copy(xT_f[:, t % 2], src)
                nc.scalar.copy(xT_hi[:, :, t * P:(t + 1) * P], src).then_inc(s["xT_hi_done"], 1)

            def handle(i, n, st):
                kind = st[0]
                if kind == "H":
                    u = st[1]
                    if u % B == 0:
                        act.wait_ge(s["w_hi_done"], n("W"))
                    for c in range(HC):
                        act.wait_ge(s["h_mm"], HC * n("H") + c + 1)
                        need(act, s["h_lo_done"], HC * n("H") + c - 1)
                        if c == 0:
                            need(act, s["y_mm"], 2 * (n("H") - 1))
                        bias = b1[u // B][:, c:c + 1]
                        nc.scalar.activation(h_f[:, c % 2], ps_h[:, c, :], ACT.Relu, bias=bias)
                        nc.scalar.activation(h_hi[:, u % 2, c], ps_h[:, c, :], ACT.Relu, bias=bias)\
                            .then_inc(s["h_act"], 1)
                elif kind == "T":
                    for t in range(NC * st[1], NC * (st[1] + 1)):
                        take_row(t)
                elif kind == "G":
                    act.wait_ge(s["gate_sub"], 1)
                    nc.scalar.activation(probs[:], probs[:], ACT.Exp).then_inc(s["gate_exp"], 1)
                elif kind == "ST":
                    b = st[1]
                    act.wait_ge(s["score_tr"], b + 1)
                    for row in (HI_HI, HI_LO):
                        ins = nc.scalar.copy(scoreT[row:row + NE, NC * b:NC * (b + 1), :],
                                             ps_t[0:NE, :].rearrange("e (t p) -> e t p", t=NC))
                    ins.then_inc(s["scoreT_hi_done"], 1)
                elif kind == "W":
                    p = st[1]
                    act.wait_ge(w_in[p], 16 * (i + (2 if p == 0 else 1)))
                    need(act, s["y_mm"], 2 * (n("Y") - 1))
                    nc.scalar.copy(b1[p][:], w_raw[p][:, WW:WW + HC])
                    nc.scalar.copy(w_hi[p][:], w_raw[p][:, 0:WW]).then_inc(s["w_hi_done"], 1)

            expert_walk(act, handle)

        @block.vector
        def _(dve):
            done = [0]

            def link(ins):
                done[0] += 1
                ins.then_inc(s["step"], 1)
                dve.wait_ge(s["step"], done[0])

            nc.vector.memset(zero[:], 0.0)
            nc.vector.memset(b2_raw[:], 0.0).then_inc(s["zero_set"], 1)
            for e in range(NE):
                nc.vector.memset(iota[:, e:e + 1], float(e))

            def statistics(t0, sem):
                for t in range(t0, t0 + NC):
                    ins = nc.vector.bn_stats(st_[:, t], X[:, t])
                link(ins)
                for t in range(t0, t0 + NC):
                    ins = nc.vector.bn_aggr(mv[:, t], st_[:, t])
                ins.then_inc(sem, 1)

            def normalise(t0, sem):
                for t in range(t0, t0 + NC):
                    nc.vector.tensor_scalar(X[:, t], X[:, t], mv[:, t, 0:1], rstd[:, t:t + 1],
                                            ALU.subtract, ALU.mult).then_inc(sem, 1)

            def take_rows(b):
                for t in range(NC * b, NC * (b + 1)):
                    dve.wait_ge(s["xT_hi_done"], t + 1)
                    nc.vector.tensor_tensor(xT_lo[:, :, t * P:(t + 1) * P],
                                            ps_y[:, t % 2, 0:E].rearrange("p (k n) -> p k n", k=EC),
                                            xT_hi[:, :, t * P:(t + 1) * P].bitcast(F32), ALU.subtract)\
                        .then_inc(s["xT_lo_done"], 1)

            def over_experts(x):
                return x.unsqueeze(2).broadcast_to([P, T, NE])

            def gate():
                dve.wait_ge(s["gate_mm"], T)
                logits = ps_g[:, 0:T * NE].rearrange("p (t e) -> p t e", e=NE)
                link(nc.vector.tensor_reduce(gred[:], logits, AX.X, ALU.max))
                nc.vector.tensor_tensor(probs[:], logits, over_experts(gred[:]), ALU.subtract)\
                    .then_inc(s["gate_sub"], 1)
                dve.wait_ge(s["gate_exp"], 1)
                link(nc.vector.tensor_reduce(gred[:], probs[:], AX.X, ALU.add))
                link(nc.vector.reciprocal(gred[:], gred[:]))
                link(nc.vector.tensor_tensor(probs[:], probs[:], over_experts(gred[:]), ALU.mult))
                for t in range(T):
                    ins = nc.vector.max(top[:, t], probs[:, t])
                link(ins)
                for t in range(T):
                    ins = nc.vector.max_index(idx[:, t], top[:, t], probs[:, t])
                link(ins)
                nc.vector.tensor_copy(idxf[:], idx[:])
                link(nc.vector.tensor_tensor(gred[:], top[:, :, 0], top[:, :, 1], ALU.add))
                link(nc.vector.reciprocal(gred[:], gred[:]))
                link(nc.vector.tensor_tensor(norm[:], top[:, :, 0:TOPK],
                                             gred[:].unsqueeze(2).broadcast_to([P, T, TOPK]), ALU.mult))
                for j in range(TOPK):
                    dst = score if j == 0 else hot
                    link(nc.vector.tensor_tensor(dst[:], iota[:].unsqueeze(1).broadcast_to([P, T, NE]),
                                                 over_experts(idxf[:, :, j]), ALU.is_equal))
                    link(nc.vector.tensor_tensor(dst[:], dst[:], over_experts(norm[:, :, j]), ALU.mult))
                nc.vector.tensor_tensor(score[:], score[:], hot[:], ALU.add).then_inc(s["score_done"], 1)

            def split_scores(b):
                dve.wait_ge(s["scoreT_hi_done"], b + 1)
                r = slice(NC * b, NC * (b + 1))
                nc.vector.tensor_tensor(scoreT[LO_HI:LO_HI + NE, r, :],
                                        ps_t[0:NE, :].rearrange("e (t p) -> e t p", t=NC),
                                        scoreT[HI_HI:HI_HI + NE, r, :].bitcast(F32), ALU.subtract)\
                    .then_inc(s["scoreT_lo_done"], 1)

            def output_biases(j):
                dve.wait_ge(s["b2_mm"], j + 1)
                xs = X[:, 2 * j:2 * j + 2, :].rearrange("p t e -> p (t e)")
                nc.vector.tensor_tensor(xs, ps_g[:], xs, ALU.add).then_inc(s["b2_added"], 1)

            for b in range(B):
                statistics(NC * b, s["var_ready"])
            for b in range(2):
                dve.wait_ge(s["rstd_ready"], b + 1)
                normalise(NC * b, s["x_done"])
            lo = slice(HI_LO, HI_LO + 32)
            dve.wait_ge(s["b2_hi_done"], 1)
            nc.vector.tensor_tensor(b2x[lo], b2_raw[lo], b2x[lo].bitcast(F32), ALU.subtract)\
                .then_inc(s["b2_ready"], 1)

            def handle(i, n, st):
                kind = st[0]
                if kind == "H":
                    u = st[1]
                    for c in range(HC):
                        dve.wait_ge(s["h_act"], HC * n("H") + c + 1)
                        nc.vector.tensor_tensor(h_lo[:, u % 2, c], h_f[:, c % 2], h_hi[:, u % 2, c].bitcast(F32),
                                                ALU.subtract).then_inc(s["h_lo_done"], 1)
                elif kind == "T":
                    b = st[1]
                    take_rows(b)
                    if b + 2 < B:
                        dve.wait_ge(s["rstd_ready"], b + 3)
                        normalise(NC * (b + 2), s["x_done"])
                elif kind == "G":
                    gate()
                elif kind == "ST":
                    split_scores(st[1])
                elif kind == "B2":
                    output_biases(2 * st[1] + st[2])
                elif kind == "Y":
                    if isinstance(i, int) and i == 0 and st[1] < B:
                        dve.wait_ge(s["b2_added"], 2 * (st[1] + 1))
                    u, expert = st[1], 2 * (i + st[2]) + st[1] // B
                    for j in range(2):
                        dve.wait_ge(s["y_mm"], 2 * n("Y") + j + 1)
                        for q in range(2):
                            t = u % B * NC + 2 * j + q
                            ins = nc.vector.scalar_tensor_tensor(
                                out=X[:, t], in0=ps_y[:, j, q * E:(q + 1) * E],
                                scalar=score[:, t, bass.ds(expert, 1)], in1=X[:, t],
                                op0=ALU.mult, op1=ALU.add)
                        ins.then_inc(s["y_added"], 1)
                elif kind == "F1":
                    dve.wait_ge(s["y_added"], 2 * n("Y"))
                    statistics(NC * st[1], s["fvar"])
                elif kind == "F2":
                    dve.wait_ge(s["frstd"], st[1] + 1)
                    normalise(NC * st[1], s["fdone"])

            expert_walk(dve, handle)


def build(nc, a, out):
    with ExitStack() as ctx:
        X = ctx.enter_context(nc.sbuf_tensor("X", [P, B * NC, E], F32))
        consts = {n: ctx.enter_context(nc.sbuf_tensor(n, [P, P], F32)) for n in ("ident", "ones", "neghalf")}
        x1_hi = nc.dram_tensor("x1_hi", [B, P, EC, N], F32, kind="Internal").ap()
        x1_lo = nc.dram_tensor("x1_lo", [B, P, EC, N], F32, kind="Internal").ap()
        loads = FirstLoads(nc, ctx)
        self_attention(nc, a, X, consts, loads, x1_hi, x1_lo)
        cross_attention(nc, a, X, consts, loads, x1_hi, x1_lo)
        experts(nc, a, X, consts, out)

def layout(i):
    import numpy as np

    f = {k: np.asarray(v) for k, v in i.items()}
    q, k = f["L0_xattn_w_q"], f["L0_xattn_w_kv"][:, :XH * XD]
    v, o = f["L0_xattn_w_kv"][:, XH * XD:], f["L0_xattn_w_out"]

    def cols(w, quad, pair=None):
        lo = quad * 4 * XD if pair is None else (quad * 2 + pair) * 2 * XD
        w = w[:, lo:lo + (4 if pair is None else 2) * XD]
        return w.reshape(EC, P, -1).transpose(1, 0, 2).reshape(P, -1)

    def rows(quad, pair):
        return o[(quad * 2 + pair) * P:(quad * 2 + pair + 1) * P]

    nxt = [(j + 1) % QUADS for j in range(QUADS)]
    pack_a = np.stack([np.concatenate([cols(k, n, 0), cols(q, n, 0), cols(v, n), rows(j, 0), rows(j, 1)], 1)
                       for j, n in enumerate(nxt)])
    pack_b = np.stack([np.concatenate([cols(k, n, 1), cols(q, n, 1)], 1) for n in nxt])
    w1, w2 = f["L0_ffn_W1"], f["L0_ffn_W2"]
    pack_e = np.concatenate([w1.reshape(NE, EC, P, HID).transpose(0, 2, 1, 3).reshape(NE, P, -1),
                             w2.reshape(NE, HC, P, E).transpose(0, 2, 1, 3).reshape(NE, P, -1),
                             f["L0_ffn_b1"].reshape(NE, HC, P).transpose(0, 2, 1)], 2)
    x = f["x"].reshape(B * N, E)
    return {
        "x": x, "xT": x.T, "ctxT": f["ctx_1024"].transpose(0, 2, 1),
        "w_inT": f["L0_attn_in_proj_w"].T, "w_v": f["L0_attn_in_proj_w"][2 * E:], "dynT": f["L0_attn_dyn_w"].T,
        "b_in": f["L0_attn_in_proj_b"][None], "b_v": f["L0_attn_in_proj_b"][2 * E:].reshape(EC, P).T,
        "b_dyn": f["L0_attn_dyn_b"][None], "w_oT": f["L0_attn_out_proj_w"].T, "b_o": f["L0_attn_out_proj_b"][None],
        "b_xo": f["L0_xattn_b_out"][None], "pack_a": pack_a, "pack_b": pack_b,
        "Wg": f["L0_ffn_Wg"], "pack_e": pack_e,
        "b2": f["L0_ffn_b2"],
    }


def kernel(**inputs):
    import concourse.bacc as bacc
    import numpy as np
    from concourse.bass_utils import run_bass_kernel_spmd

    nc = bacc.Bacc("TRN2", target_bir_lowering=False, num_devices=1)
    arrays, a = {}, {}
    for name, v in layout(inputs).items():
        v = np.ascontiguousarray(v)
        arrays["in_" + name] = v
        a[name] = nc.dram_tensor("in_" + name, v.shape, mybir.dt.from_np(v.dtype), kind="ExternalInput").ap()
    out = nc.dram_tensor("out", (B, N, E), F32, kind="ExternalOutput").ap()
    build(nc, a, out)
    r = run_bass_kernel_spmd(nc, [arrays], core_ids=[0])
    return r.results[0]["out"]
```
